# Optimizing a Trainium2 kernel written in Bass

```python
import numpy as np
import jax
import jax.numpy as jnp

def _softmax(x, axis=-1):
    return jax.nn.softmax(x, axis=axis)

def _gelu(x):
    return jax.nn.gelu(x, approximate=True)

def _silu(x):
    return jax.nn.silu(x)

def _sigmoid(x):
    return jax.nn.sigmoid(x)

def _layernorm(x, axis=-1, eps=1e-05):
    m = jnp.mean(x, axis=axis, keepdims=True)
    v = jnp.var(x, axis=axis, keepdims=True)
    return (x - m) / jnp.sqrt(v + eps)

def _scatter_add(tgt, idx, src, axis=0):
    return tgt.at[idx].add(src)

def _segment_sum(src, seg, n):
    return jax.ops.segment_sum(src, seg, n)
kernel_name = 'mk_gps_d1_gnn_r8_c18a45'

def setup_inputs(seed: int=0):
    np.random.seed(seed)
    _w = jnp.asarray

    def _rec_inputs():
        import jax
        import jax.numpy as jnp
        _gk = jax.random.key(seed)
        x = -0.0003713 + 1 * jax.random.normal(jax.random.fold_in(_gk, 1), (6250, 256), jnp.float32)
        src = jax.random.randint(jax.random.fold_in(_gk, 2), (100000,), 0, 6250, jnp.int32)
        dst = jnp.minimum((6250 * jax.random.uniform(jax.random.fold_in(_gk, 3), (100000,)) ** 2.0).astype(jnp.int32), 49999)
        _o = jnp.argsort(dst, stable=True)
        src = src[_o]
        dst = dst[_o]
        return (x, src, dst)
    x, src, dst = _rec_inputs()

    def _L0_gnn_setup():
        import jax, jax.numpy as jnp
        import numpy as np
        N_NODES = 6250
        N_EDGES = 100000
        IN_FEATS = 256
        HIDDEN = 256

        def _sage_conv(x, src, dst, Wl, bl, Wr):
            msg = x[src]
            agg = jax.ops.segment_sum(msg, dst, num_segments=N_NODES)
            cnt = jax.ops.segment_sum(jnp.ones((src.shape[0],), dtype=x.dtype), dst, num_segments=N_NODES)
            mean = agg / jnp.maximum(cnt, 1.0)[:, None]
            return mean @ Wl.T + bl + x @ Wr.T
        key = jax.random.key(seed)
        ks = jax.random.split(key, 8)
        x = jax.random.normal(ks[0], (N_NODES, IN_FEATS), dtype=jnp.float32)
        edge_index = jax.random.randint(ks[1], (2, N_EDGES), 0, N_NODES, dtype=jnp.int32)
        s = 1.0 / np.sqrt(IN_FEATS)
        W1l = jax.random.uniform(ks[2], (HIDDEN, IN_FEATS), minval=-s, maxval=s, dtype=jnp.float32)
        b1 = jax.random.uniform(ks[3], (HIDDEN,), minval=-s, maxval=s, dtype=jnp.float32)
        W1r = jax.random.uniform(ks[4], (HIDDEN, IN_FEATS), minval=-s, maxval=s, dtype=jnp.float32)
        s2 = 1.0 / np.sqrt(HIDDEN)
        W2l = jax.random.uniform(ks[5], (HIDDEN, HIDDEN), minval=-s2, maxval=s2, dtype=jnp.float32)
        b2 = jax.random.uniform(ks[6], (HIDDEN,), minval=-s2, maxval=s2, dtype=jnp.float32)
        W2r = jax.random.uniform(ks[7], (HIDDEN, HIDDEN), minval=-s2, maxval=s2, dtype=jnp.float32)
        return {'x': x, 'edge_index': edge_index, 'W1l': W1l, 'b1': b1, 'W1r': W1r, 'W2l': W2l, 'b2': b2, 'W2r': W2r}
    _L0_gnn_all = _L0_gnn_setup()
    _L0_gnn_in = {k: v for k, v in _L0_gnn_all.items() if k in ('W1l', 'b1', 'W1r', 'W2l', 'b2', 'W2r')}
    del _L0_gnn_all

    def _L0_mix_setup():
        import jax, jax.numpy as jnp
        import numpy as np
        N, F, C, H = (32, 512, 256, 8)
        D = C // H
        EPS_ATTN = 1e-06
        EPS_LN = 1e-05

        def layer_norm(x, g, b):
            mu = jnp.mean(x, axis=-1, keepdims=True)
            var = jnp.var(x, axis=-1, keepdims=True)
            return (x - mu) * jax.lax.rsqrt(var + EPS_LN) * g + b
        key = jax.random.key(seed)
        ks = jax.random.split(key, 8)
        s = 1.0 / np.sqrt(C)
        return {'x': jax.random.normal(ks[0], (N, F, C), jnp.float32), 'Wqkv': jax.random.uniform(ks[1], (3 * C, C), jnp.float32, -s, s), 'ln1_g': jnp.ones((C,), jnp.float32), 'ln1_b': jnp.zeros((C,), jnp.float32), 'W1': jax.random.uniform(ks[2], (C, C), jnp.float32, -s, s), 'b1': jax.random.uniform(ks[3], (C,), jnp.float32, -s, s), 'W2': jax.random.uniform(ks[4], (C, C), jnp.float32, -s, s), 'b2': jax.random.uniform(ks[5], (C,), jnp.float32, -s, s), 'ln2_g': jnp.ones((C,), jnp.float32), 'ln2_b': jnp.zeros((C,), jnp.float32)}
    _L0_mix_all = _L0_mix_setup()
    _L0_mix_in = {k: v for k, v in _L0_mix_all.items() if k in ('Wqkv', 'ln1_g', 'ln1_b', 'W1', 'b1', 'W2', 'b2', 'ln2_g', 'ln2_b')}
    del _L0_mix_all

    def _L0_ffn_setup():
        import jax, jax.numpy as jnp
        import numpy as np
        C = 256
        HID = 1024
        E = 8
        TEMP = 1.0
        key = jax.random.key(seed)
        ks = jax.random.split(key, 7)
        x = jax.random.normal(ks[0], (8, 2048, C), dtype=jnp.float32)
        W1 = jax.random.normal(ks[1], (C, HID), dtype=jnp.float32) * 0.02
        b1 = jnp.zeros((HID,), dtype=jnp.float32)
        Wg = jax.random.normal(ks[2], (HID, E), dtype=jnp.float32) * 0.02
        bg = jnp.zeros((E,), dtype=jnp.float32)
        Wd = jax.random.normal(ks[3], (E, HID, C), dtype=jnp.float32) * 0.02
        bd = jnp.zeros((E, C), dtype=jnp.float32)
        return {'x': x, 'W1': W1, 'b1': b1, 'Wg': Wg, 'bg': bg, 'Wd': Wd, 'bd': bd}
    _L0_ffn_all = _L0_ffn_setup()
    _L0_ffn_in = {k: v for k, v in _L0_ffn_all.items() if k in ('W1', 'b1', 'Wg', 'bg', 'Wd', 'bd')}
    del _L0_ffn_all
    return {'x': x, 'src': src, 'dst': dst, 'L0_gnn_W1l': _L0_gnn_in['W1l'], 'L0_gnn_b1': _L0_gnn_in['b1'], 'L0_gnn_W1r': _L0_gnn_in['W1r'], 'L0_gnn_W2l': _L0_gnn_in['W2l'], 'L0_gnn_b2': _L0_gnn_in['b2'], 'L0_gnn_W2r': _L0_gnn_in['W2r'], 'L0_mix_Wqkv': _L0_mix_in['Wqkv'], 'L0_mix_ln1_g': _L0_mix_in['ln1_g'], 'L0_mix_ln1_b': _L0_mix_in['ln1_b'], 'L0_mix_W1': _L0_mix_in['W1'], 'L0_mix_b1': _L0_mix_in['b1'], 'L0_mix_W2': _L0_mix_in['W2'], 'L0_mix_b2': _L0_mix_in['b2'], 'L0_mix_ln2_g': _L0_mix_in['ln2_g'], 'L0_mix_ln2_b': _L0_mix_in['ln2_b'], 'L0_ffn_W1': _L0_ffn_in['W1'], 'L0_ffn_b1': _L0_ffn_in['b1'], 'L0_ffn_Wg': _L0_ffn_in['Wg'], 'L0_ffn_bg': _L0_ffn_in['bg'], 'L0_ffn_Wd': _L0_ffn_in['Wd'], 'L0_ffn_bd': _L0_ffn_in['bd']}

def reference(x, src, dst, L0_gnn_W1l, L0_gnn_b1, L0_gnn_W1r, L0_gnn_W2l, L0_gnn_b2, L0_gnn_W2r, L0_mix_Wqkv, L0_mix_ln1_g, L0_mix_ln1_b, L0_mix_W1, L0_mix_b1, L0_mix_W2, L0_mix_b2, L0_mix_ln2_g, L0_mix_ln2_b, L0_ffn_W1, L0_ffn_b1, L0_ffn_Wg, L0_ffn_bg, L0_ffn_Wd, L0_ffn_bd):
    import jax
    import jax.numpy as jnp

    def _L0_gnn_ref(x, edge_index, W1l, b1, W1r, W2l, b2, W2r):
        import jax, jax.numpy as jnp
        import numpy as np
        N_NODES = 6250
        N_EDGES = 100000
        IN_FEATS = 256
        HIDDEN = 256

        def _sage_conv(x, src, dst, Wl, bl, Wr):
            msg = x[src]
            agg = jax.ops.segment_sum(msg, dst, num_segments=N_NODES)
            cnt = jax.ops.segment_sum(jnp.ones((src.shape[0],), dtype=x.dtype), dst, num_segments=N_NODES)
            mean = agg / jnp.maximum(cnt, 1.0)[:, None]
            return mean @ Wl.T + bl + x @ Wr.T
        src, dst = (edge_index[0], edge_index[1])
        h = jax.nn.relu(_sage_conv(x, src, dst, W1l, b1, W1r))
        out = _sage_conv(h, src, dst, W2l, b2, W2r)
        return out

    def _L0_mix_ref(x, Wqkv, ln1_g, ln1_b, W1, b1, W2, b2, ln2_g, ln2_b):
        import jax, jax.numpy as jnp
        import numpy as np
        N, F, C, H = (32, 512, 256, 8)
        D = C // H
        EPS_ATTN = 1e-06
        EPS_LN = 1e-05

        def layer_norm(x, g, b):
            mu = jnp.mean(x, axis=-1, keepdims=True)
            var = jnp.var(x, axis=-1, keepdims=True)
            return (x - mu) * jax.lax.rsqrt(var + EPS_LN) * g + b
        n, f, c = x.shape
        qkv = jnp.einsum('nfc,oc->nfo', x, Wqkv)
        q, k, v = jnp.split(qkv, 3, axis=-1)
        q = q.reshape(n, f, H, D)
        k = k.reshape(n, f, H, D)
        v = v.reshape(n, f, H, D)
        q = jax.nn.elu(q) + 1.0
        k = jax.nn.elu(k) + 1.0
        kv = jnp.einsum('nshd,nshm->nhmd', k, v)
        ksum = jnp.sum(k, axis=1)
        z = 1.0 / (jnp.einsum('nlhd,nhd->nlh', q, ksum) + EPS_ATTN)
        t = jnp.einsum('nlhd,nhmd,nlh->nlhm', q, kv, z)
        t = t.reshape(n, f, c)
        x1 = layer_norm(t + x, ln1_g, ln1_b)
        h = jax.nn.gelu(jnp.einsum('nfc,oc->nfo', x1, W1) + b1, approximate=False)
        y = jnp.einsum('nfc,oc->nfo', h, W2) + b2
        return layer_norm(y + x1, ln2_g, ln2_b)

    def _L0_ffn_ref(x, W1, b1, Wg, bg, Wd, bd):
        import jax, jax.numpy as jnp
        import numpy as np
        C = 256
        HID = 1024
        E = 8
        TEMP = 1.0
        orig_shape = x.shape
        xf = x.reshape(-1, orig_shape[-1])
        H = jax.nn.gelu(xf @ W1 + b1, approximate=False)
        probs = jax.nn.softmax((H @ Wg + bg) / TEMP, axis=-1)
        assign = jnp.argmax(probs, axis=-1)
        out = jnp.zeros_like(xf)
        for e in range(Wd.shape[0]):
            y = H @ Wd[e] + bd[e]
            sel = (assign == e)[:, None]
            out = out + jnp.where(sel, probs[:, e:e + 1] * y, 0.0)
        return out.reshape(orig_shape)
    edge_index = jnp.stack([src, dst])
    xn = _layernorm(x, axis=-1)
    x = x + _L0_gnn_ref(xn, edge_index, L0_gnn_W1l, L0_gnn_b1, L0_gnn_W1r, L0_gnn_W2l, L0_gnn_b2, L0_gnn_W2r) + _L0_mix_ref(xn[None], L0_mix_Wqkv, L0_mix_ln1_g, L0_mix_ln1_b, L0_mix_W1, L0_mix_b1, L0_mix_W2, L0_mix_b2, L0_mix_ln2_g, L0_mix_ln2_b)[0]
    x = x + _L0_ffn_ref(_layernorm(x, axis=-1)[None], L0_ffn_W1, L0_ffn_b1, L0_ffn_Wg, L0_ffn_bg, L0_ffn_Wd, L0_ffn_bd)[0]
    return x

_drawn_inputs = setup_inputs


def setup_inputs(seed=0):
    import zlib

    import numpy as np

    out = dict(_drawn_inputs(seed))
    spreads = {'L0_mix_ln1_g': (1.0, 0.2),
     'L0_mix_ln1_b': (0.0, 0.1),
     'L0_mix_ln2_g': (1.0, 0.2),
     'L0_mix_ln2_b': (0.0, 0.1),
     'L0_ffn_b1': (0.0, 0.8),
     'L0_ffn_bg': (0.0, 0.784),
     'L0_ffn_bd': (0.0, 0.8)}
    factors = {'L0_gnn_b1': 6.922,
     'L0_gnn_b2': 3.1,
     'L0_mix_Wqkv': 8.0,
     'L0_mix_b1': 8.0,
     'L0_mix_b2': 3.258,
     'L0_ffn_W1': 5.435,
     'L0_ffn_Wg': 5.781,
     'L0_ffn_Wd': 6.593}
    for name, (base, spread) in spreads.items():
        noise = np.random.default_rng([zlib.crc32(name.encode()), seed]).standard_normal(out[name].shape)
        drawn = base * np.exp(spread * noise) if base else spread * noise
        out[name] = jnp.asarray(drawn.astype(out[name].dtype))
    for name, factor in factors.items():
        out[name] = (out[name] * factor).astype(out[name].dtype)
    return out
```

```python
from contextlib import ExitStack

import concourse.bass as bass
import concourse.mybir as mybir

F32, F16, I32 = mybir.dt.float32, mybir.dt.float16, mybir.dt.int32
ALU, ACT, AX = mybir.AluOpType, mybir.ActivationFunctionType, mybir.AxisListType

P = 128
N, C, EDGES = 6250, 256, 100000
CH = C // P
TILES = -(-N // P)
LAST_ROWS = N - (TILES - 1) * P
SC = 4
SUPER = EDGES // (SC * P) + 2
PAD_NODE = TILES * P - 1
ITEMS = SUPER + TILES - 1
RING = 4
HEADS, HD = 8, 32
HID, NE = 1024, 8
HJ = HID // P
SLOTS = (N + NE * (P - 1)) // P
ROW = C + 2
EPS_LN, EPS_ATTN = 1e-5, 1e-6
ITEMS_A, ITEMS_B, ITEMS_2 = 2, 3, 5
NS = ITEMS_2
NO_ROW = 1 << 20
OPENED = 16
assert ITEMS == TILES * (ITEMS_A + ITEMS_B) == TILES * ITEMS_2
GROUP = 7
assert TILES % GROUP == 0


class Line:

    def __init__(self, sem, names, credit=False):
        self.sem, self.names = sem, list(names)
        self.at = 0
        self.n = len(self.names)
        self.credit = self.n if credit is True else credit
        assert len(set(self.names)) == self.n

    def done(self, ins, name):
        assert self.names[self.at % self.n] == name, (self.names[self.at % self.n], name)
        self.at += 1
        ins.then_inc(self.sem, 1)

    def wait(self, eng, name, i, back=0):
        eng.wait_ge(self.sem, i * self.n + (self.credit + self.names.index(name) + 1 - back * self.n))


def turns(eng, n):
    yield True, 0
    with eng.Fori(1, n) as i:
        yield False, i


def ln_names(p):
    return [p + x for x in ("st", "ag", "v", "y0", "a1", "b1", "y1", "a2", "b2", "y2", "a3", "b3", "y3")]


def build(nc, x, srcL, dstL, dst_tail, w, out):
    with ExitStack() as ctx:
        def sb(name, shape, dt=F32):
            return ctx.enter_context(nc.sbuf_tensor(name, shape, dt))

        def sem(name):
            return ctx.enter_context(nc.semaphore(name))

        def dram(name, shape, dt=F32):
            return nc.dram_tensor(name, shape, dt, kind="Internal").ap()

        xh_d = dram("xh_d", [TILES * P, 2 * C], F16)
        hh_d = dram("hh_d", [TILES * P, 2 * C], F16)
        xn_d = dram("xn_d", [(TILES + 1) * P, C])
        qT_d = dram("qT_d", [(TILES + 1) * P, C])
        ck_d = dram("ck_d", [2 * P])
        srt_d = dram("srt_d", [SLOTS * P, ROW])

        res = sb("res", [P, TILES, ROW])
        big = sb("big", [P, 16640])
        G = sb("G", [P, RING, SC, 2 * C], F16)
        S = sb("S", [P, NS, SC, P], F16)
        rel = sb("rel", [P, NS, SC])
        edges = sb("edges", [P, 3, SUPER * SC])
        src, dsti, dst = edges[:, 0, :].bitcast(I32), edges[:, 1, :].bitcast(I32), edges[:, 2, :]
        ix = sb("ix", [P, RING, SC], I32)
        tab = sb("tab", [1, 4, 2 * P], I32)
        free_tab = sb("free_tab", [1, SUPER], I32)
        tv = sb("tv", [P, 2 * P])
        iota16 = sb("iota16", [P, P], F16)
        ident = sb("ident", [P, P])
        ones16 = sb("ones16", [P, P], F16)
        ones1 = sb("ones1", [1, P])
        zero16 = sb("zero16", [1, 2 * C], F16)
        vmask = sb("vmask", [P, TILES])
        epsb = sb("epsb", [P, 1])
        RC = sb("RC", [P, TILES])
        cntv = sb("cntv", [P, 1])
        lo = sb("lo", [P, C])
        mean = sb("mean", [P, C])
        mT = sb("mT", [P, CH, P])
        xTs = sb("xTs", [P, CH, P])
        hb = sb("hb", [P, C])
        hT = sb("hT", [P, CH, P])
        HL = sb("HL", [P, 2 * C], F16)
        w1l, w1r, w2l, w2r = (sb(f"w{n}", [P, CH, C]) for n in ("1l", "1r", "2l", "2r"))
        gb1, gb2 = sb("gb1", [1, C]), sb("gb2", [1, C])
        fw1 = sb("fw1", [P, CH, HID])
        fwg = sb("fwg", [P, HJ, NE])
        fb1 = sb("fb1", [P, HJ])
        fbg = sb("fbg", [1, NE])
        lnt = sb("lnt", [P, 16])

        used = [0]

        def carve(n, shape):
            a = big[:, used[0]:used[0] + n]
            used[0] += n
            names = "abc"[:len(shape)]
            kw = {names[i]: shape[i] for i in range(len(shape))}
            return a.rearrange(f"p ({' '.join(names)}) -> p {' '.join(names)}", **kw) if len(shape) > 1 else a

        xnT = carve(CH * TILES * P, [CH, TILES * P])
        wq = carve(CH * C, [CH, C])
        wkv = carve(CH * 2 * C, [CH, 2 * C])
        mw1 = carve(CH * C, [CH, C])
        mw2 = carve(CH * C, [CH, C])
        lng1, lnb1, lng2, lnb2 = (carve(C, [C]) for _ in range(4))
        mb1 = carve(CH, [CH])
        mb2 = big[0:1, used[0]:used[0] + C]
        used[0] += C
        assert used[0] <= 16640
        wd = big[:, 0:HJ * NE * C].rearrange("p (j e c) -> p j e c", j=HJ, e=NE)
        mbuf = sb("mbuf", [P, 2080])
        parts = {"xTm": C, "xnS": C, "qS": C, "hTm": C, "m_x1": C, "m_o": C, "KVs": CH * (P + 4), "v1": CH * (P + 1), "zd": HEADS}
        at = 0
        for name, n in parts.items():
            parts[name] = mbuf[:, at:at + n]
            at += n
        assert at <= 2080
        xTm, qS, hTm, KVs, v1 = (parts[n].rearrange("p (h t) -> p h t", h=CH) for n in ("xTm", "qS", "hTm", "KVs", "v1"))
        xnS, m_x1, m_o, zd = (parts[n] for n in ("xnS", "m_x1", "m_o", "zd"))
        fbd = mbuf[0:1, 0:NE * C].rearrange("p (e c) -> p e c", e=NE)
        abuf = sb("abuf", [P, 6, C])
        ek, rk, kb, eq, rq, qb = (abuf[:, n, :] for n in range(6))
        HT = abuf[:, 0:4, :].rearrange("p a b -> p (a b)").rearrange("p (j t) -> p j t", j=HJ)
        x1T = sb("x1T", [P, CH, P])
        m_s, m_t = (sb(n, [P, C]) for n in ("m_s", "m_t"))
        Gf = G.rearrange("p a b c -> p (a b c)").bitcast(F32)
        xhl = G.rearrange("p a b c -> p (a b) c")[:, 0:GROUP, :]
        xb = Gf[:, GROUP * C:2 * GROUP * C].rearrange("p (t c) -> p t c", c=C)
        st6 = sb("st6", [P, TILES, 6])
        mv = sb("mv", [P, TILES, 2])
        LG = sb("LG", [P, TILES, NE])

        ii, ik, it = sb("ii", [P, P + 3], I32), sb("ik", [P, 2 * P], I32), sb("it", [P, TILES], I32)
        iof, ikf, itf = sb("iof", [P, P + 3]), sb("ikf", [P, 2 * P]), sb("itf", [P, TILES])
        upper = sb("upper", [P, P], F16)
        scrap = sb("scrap", [1, 32], I32)
        zrow = sb("zrow", [P, ROW])
        ab = abuf.rearrange("p a c -> p (a c)")
        tl, klast, cmp = ab[:, 0:SUPER].bitcast(I32), ab[:, 256:256 + SUPER], ab[:, 512:512 + SUPER]
        ftf, tf = ab[0:1, 768:768 + SUPER], ab[:, 1024:1024 + 2 * P]
        ckc = sb("ckc", [P, 2])
        sd, rstd = sb("sd", [P, TILES]), sb("rstd", [P, TILES])
        mx, nv, posi = sb("mx", [P, TILES]), sb("nv", [P, TILES]), sb("posi", [P, TILES], I32)
        E1, E2, A1, A2 = (edges.rearrange("p a b -> p (a b)")[:, n * TILES * NE:(n + 1) * TILES * NE]
                          .rearrange("p (t e) -> p t e", e=NE) for n in range(4))
        E16 = sb("E16", [P, TILES, NE], F16)
        w8, stp, ctf = sb("w8", [P, NE]), sb("stp", [P, NE]), sb("ctf", [P, NE])
        cti, start = sb("cti", [P, NE], I32), sb("start", [P, NE + 1])
        ete = edges.rearrange("p a b -> p (a b)")[0:1, 4 * TILES * NE:4 * TILES * NE + SLOTS * (NE - 1)].rearrange("p (t e) -> p t e", e=NE - 1)
        etf, et = sb("etf", [1, SLOTS]), sb("et", [1, SLOTS], I32)
        pslot = sb("pslot", [P, GROUP], I32)
        rows = Gf[:, 0:GROUP * ROW].rearrange("p (t c) -> p t c", c=ROW)
        RB = Gf[:, 1920:1920 + 2 * ROW].rearrange("p (t c) -> p t c", c=ROW)
        o_sb = Gf[:, 2560:2560 + 2 * C].rearrange("p (t c) -> p t c", c=C)

        pb = [ctx.enter_context(nc.psum_tensor(f"bank{i}", [P, 512], F32)) for i in range(8)]
        AGG, CNT, FT, FO, B4, B5, B6, B7 = pb

        d_x = [sem(f"d_x{g}") for g in range(GROUP)]
        d_edges, d_w, d_ck = sem("d_edges"), sem("d_w"), sem("d_ck")
        d_xst = [sem(f"d_xst{g}") for g in range(GROUP)]
        d_g = [sem(f"d_g{r}") for r in range(RING)]
        d_h, d_q, d_lx, d_lq, d_wd, d_init = (sem(n) for n in ("d_h", "d_q", "d_lx", "d_lq", "d_wd", "d_init"))
        s_ready = sem("s_ready")
        p_ix = sem("p_ix")
        p_setup = sem("p_setup")
        v_setup = Line(sem("v_setup"), [f"s{i}" for i in range(200)])
        s_tab, s_const, s_ck, s_lmax, s_onehot, s_var = (sem(n) for n in ("s_tab", "s_const", "s_ck", "s_lmax", "s_onehot", "s_var"))
        passed = {n: sem("passed_" + n) for n in ("SP", "Pool", "DVE", "Activation")}

        def hold(e, name):
            e.sem_inc(passed[name], 1)
        p_const, v_st = sem("p_const"), sem("v_st")
        a_setup = sem("a_setup")
        VN = Line(sem("v_norm"), ["xn", "lo"])
        AN = Line(sem("a_norm"), ["hi", "xnT"], credit=True)
        PN = Line(sem("pe_norm"), ["tr"], credit=True)
        VI = Line(sem("v_item"), ["rel", "S0", "S1", "S2", "S3"])
        PI = Line(sem("pe_item"), ["sum"], credit=NS)
        pe_zero = sem("pe_zero")
        VF1 = Line(sem("v_fin1"), ["cnt", "rc", "lo", "mean", "mT", "hi", "hlo", "hT", "res"], credit=True)
        AF1 = Line(sem("a_fin1"), ["xT", "relu"])
        PF1 = Line(sem("pe_fin1"), ["tr1", "h", "tr2", "r2"], credit=True)
        VF2 = Line(sem("v_fin2"), ["lo", "mean", "mT", "x2"])
        PF2 = Line(sem("pe_fin2"), ["tr1", "o"])
        AMA = Line(sem("a_mixa"), ["xT", "ek", "rk", "v", "eq", "rq"], credit=True)
        VMA = Line(sem("v_mixa"), ["one", "k", "q"], credit=True)
        PMA = Line(sem("pe_mixa"), ["kv", "q", "acc"], credit=True)
        v_kv = Line(sem("v_kv"), [f"s{i}" for i in range(20)])
        PMB = Line(sem("pe_mixb"), ["t", "tr", "w1", "w2"], credit=True)
        AMB = Line(sem("a_mixb"), ["x1T", "gl0", "gl1"], credit=True)
        names = (["den", "rc", "tz", "s"] + ln_names("A") + ["n1", "g1", "x1", "s2"] + ln_names("B")
                 + ["n2", "g2", "b2", "res"])
        VMB = Line(sem("v_mixb"), names, credit=True)
        VG = Line(sem("v_gate"), ln_names("G") + ["xf", "lg"], credit=True)
        AG = Line(sem("a_gate"), ["xT"] + [f"g{j}" for j in range(HJ)], credit=True)
        PG = Line(sem("pe_gate"), ["tr"] + [f"h{j}" for j in range(HJ)] + ["lg"], credit=True)
        v_rt = Line(sem("v_rt"), [f"s{i}" for i in range(200)])
        pe_rt, a_rt, s_et = sem("pe_rt"), sem("a_rt"), sem("s_et")
        v_row = sem("v_row")
        d_srt = [sem(f"d_srt{g}") for g in range(GROUP)]
        d_rb = [sem(f"d_rb{u}") for u in range(2)]
        d_out = [sem(f"d_out{u}") for u in range(2)]
        VT = Line(sem("v_tail"), ln_names("T") + ["xf", "o"], credit=True)
        AT = Line(sem("a_tail"), ["xT"] + [f"g{j}" for j in range(HJ)], credit=True)
        PT = Line(sem("pe_tail"), ["tr"] + [f"h{j}" for j in range(HJ)] + ["y"], credit=True)

        def layer_norm(eng, line, i, p, x_in):
            def v(k):
                return lnt[:, k:k + 1]
            line.done(eng.bn_stats(lnt[:, 8:14], x_in), p + "st")
            line.wait(eng, p + "st", i)
            hold(eng, "DVE")
            line.done(eng.bn_aggr(lnt[:, 0:2], lnt[:, 8:14]), p + "ag")
            line.wait(eng, p + "ag", i)
            line.done(eng.tensor_scalar(v(2), v(1), EPS_LN, None, ALU.add), p + "v")
            line.wait(eng, p + "v", i)
            line.done(eng.tensor_scalar(v(3).bitcast(I32), v(2).bitcast(I32), -0.5, 1597463007.0,
                                        ALU.mult, ALU.add), p + "y0")
            line.wait(eng, p + "y0", i)
            for n in "123":
                line.done(eng.scalar_tensor_tensor(v(4), v(3), v(3), v(2), ALU.mult, ALU.mult), p + "a" + n)
                line.wait(eng, p + "a" + n, i)
                line.done(eng.tensor_scalar(v(5), v(4), -0.5, 1.5, ALU.mult, ALU.add), p + "b" + n)
                line.wait(eng, p + "b" + n, i)
                line.done(eng.tensor_tensor(v(3), v(3), v(5), ALU.mult), p + "y" + n)
                line.wait(eng, p + "y" + n, i)

        def item_regs(eng, k, names):
            out = []
            for n in names:
                f, hi = {"c": (0, SUPER - 1), "t": (1, TILES - 1), "last": (2, 1), "slot": (3, RING - 1)}[n]
                out.append(eng.value_load(tab[0:1, f, bass.ds(k, 1)], min_val=0, max_val=hi))
            return out

        def matmuls(eng, out_ap, pairs):
            for n, (a, b) in enumerate(pairs):
                ins = eng.matmul(out_ap, a, b, start=(n == 0), stop=(n == len(pairs) - 1))
            return ins

        block = ctx.enter_context(nc.Block())

        @block.sync
        def _(e):
            for n, s in enumerate([d_h, d_q, *d_xst]):
                e.dma_start(scrap[:, n:n + 1], dst_tail[0:1].unsqueeze(0)).then_inc(s, OPENED)
            e.wait_ge(p_setup, 1)
            for g in range(GROUP):
                lo_t, hi_t = g * GROUP, (g + 1) * GROUP
                if g < GROUP - 1:
                    e.dma_start(res[:, lo_t:hi_t, 0:C],
                                x[lo_t * P:hi_t * P, :].rearrange("(t p) c -> p t c", p=P)).then_inc(d_x[g], 32)
                else:
                    e.dma_start(res[:, lo_t:hi_t - 1, 0:C],
                                x[lo_t * P:(hi_t - 1) * P, :].rearrange("(t p) c -> p t c", p=P)).then_inc(d_x[g], 16)
                    e.dma_start(res[0:LAST_ROWS, hi_t - 1, 0:C], x[(hi_t - 1) * P:N, :]).then_inc(d_x[g], 16)
                if g == 0:
                    e.dma_start(dsti, dstL).then_inc(d_edges, 16)
                    e.dma_start(src, srcL).then_inc(d_edges, 16)
                    e.dma_start(tv.bitcast(I32)[:, 0:SUPER], dst_tail.partition_broadcast(P)).then_inc(d_edges, 16)

            def half(a):
                return a.rearrange("(h p) o -> p h o", p=P)
            loads = [(w1l, half(w["w1lT"])), (w1r, half(w["w1rT"])), (w2l, half(w["w2lT"])), (w2r, half(w["w2rT"])),
                     (gb1[:], w["gb1"].unsqueeze(0)), (gb2[:], w["gb2"].unsqueeze(0)),
                     (wq, half(w["wqkvT"])[:, :, 0:C]), (wkv, half(w["wqkvT"])[:, :, C:3 * C]),
                     (mw1, half(w["mw1T"])), (mw2, half(w["mw2T"])),
                     (lng1, w["ln1_g"].partition_broadcast(P)), (lnb1, w["ln1_b"].partition_broadcast(P)),
                     (lng2, w["ln2_g"].partition_broadcast(P)), (lnb2, w["ln2_b"].partition_broadcast(P)),
                     (mb1, w["mb1L"]), (mb2, w["mb2"].unsqueeze(0)),
                     (fw1[:], half(w["fw1"])), (fwg[:], w["fwg"].rearrange("(j p) e -> p j e", p=P)),
                     (fb1[:], w["fb1L"]), (fbg[:], w["fbg"].unsqueeze(0))]
            for a, b in loads:
                e.dma_start(a[:] if not isinstance(a, bass.AP) else a, b).then_inc(d_w, 16)
            e.wait_ge(p_setup, 2)
            e.dma_start(srt_d.rearrange("(t p) c -> p t c", p=P),
                        zrow[:, :].unsqueeze(1).to_broadcast([P, SLOTS, ROW])).then_inc(d_init, 16)
            e.wait_ge(s_ck, 1)
            e.dma_start(ck_d.rearrange("(p j) -> p j", j=2), ckc[:, 0:2]).then_inc(d_ck, 16)
            e.wait_ge(d_ck, 16)
            e.dma_start(tv[:], ck_d.partition_broadcast(P)).then_inc(d_ck, 16)
            with e.Fori(0, TILES // GROUP) as g:
                for u in range(GROUP):
                    i = g * GROUP + u
                    VN.wait(e, "lo", i)
                    hold(e, "SP")
                    e.dma_start(xh_d[bass.ds(i * P, P), :], xhl[:, u, :]).then_inc(d_xst[u], 16)
                    e.dma_start(xn_d[bass.ds(i * P, P), :], xb[:, u, :]).then_inc(d_xst[u], 16)
            for layer in range(2):
                with e.Fori(0, SUPER // RING) as b:
                    for r in range(RING):
                        uses = -(-(SUPER - r) // RING)
                        e.wait_ge(d_g[r], b * 64 + (layer * uses + 1) * 64)
                        hold(e, "SP")
                        e.sem_inc(s_ready, 1)
                for r in range(SUPER % RING):
                    uses = -(-(SUPER - r) // RING)
                    e.wait_ge(d_g[r], (layer + 1) * uses * 64)
                    e.sem_inc(s_ready, 1)
            e.wait_ge(d_init, 16)
            for g in range(GROUP):
                e.wait_ge(d_srt[g], 16 * (TILES // GROUP))
            for first, jj in turns(e, SLOTS // 2):
                for u in range(2):
                    if not first:
                        e.wait_ge(d_out[u], jj * 16)
                        hold(e, "SP")
                    e.dma_start(RB[:, u, :], srt_d[bass.ds(jj * 2 * P + u * P, P), :]).then_inc(d_rb[u], 16)
            for u in range(2):
                e.wait_ge(d_out[u], 16 * (SLOTS // 2))

        @block.gpsimd
        def _(e):
            e.memset(res[:], 0.0).then_inc(p_setup, 1)
            e.memset(zrow[:], 0.0).then_inc(p_const, 1)
            e.wait_ge(p_const, 1)
            e.memset(zrow[:, C + 1:C + 2].bitcast(I32), NO_ROW).then_inc(p_setup, 1)
            e.iota(ii[:, 0:P], pattern=[[1, P]], base=0, channel_multiplier=0).then_inc(p_const, 1)
            e.iota(ii[:, P:P + 2], pattern=[[1, 2]], base=0, channel_multiplier=2).then_inc(p_const, 1)
            e.iota(ii[:, P + 2:P + 3], pattern=[[1, 1]], base=0, channel_multiplier=1).then_inc(p_const, 1)
            e.iota(ik[:], pattern=[[1, 2 * P]], base=0, channel_multiplier=0).then_inc(p_const, 1)
            e.iota(it[:], pattern=[[P, TILES]], base=0, channel_multiplier=1).then_inc(p_const, 1)
            for layer in range(2):
                table = (xh_d, hh_d)[layer]
                if layer == 0:
                    for u in range(GROUP):
                        e.wait_ge(d_xst[u], OPENED + 32 * (TILES // GROUP))
                    PN.wait(e, "tr", TILES - 1)
                    e.wait_ge(d_edges, 48)
                    e.wait_ge(s_tab, 1)
                else:
                    e.wait_ge(d_h, OPENED + 16 * TILES)

                def gather(c, r):
                    if layer == 0:
                        need = e.value_load(free_tab[0:1, bass.ds(c, 1)], min_val=0, max_val=ITEMS)
                        e.wait_ge(PI.sem, need + NS)
                    else:
                        need = e.value_load(free_tab[0:1, bass.ds(c, 1)], min_val=0, max_val=ITEMS)
                        e.wait_ge(PI.sem, need + (NS + ITEMS))
                    hold(e, "Pool")
                    ins = e.tensor_copy(ix[:, r, :], src[:, bass.ds(c * SC, SC)])
                    ins.then_inc(p_ix, 1)
                    e.wait_ge(p_ix, c + (layer * SUPER + 1))
                    hold(e, "Pool")
                    for j in range(SC):
                        e.indirect_dma_start(G[:, r, j, :], None, table,
                                             bass.IndirectOffsetOnAxis(ap=ix[:, r, j:j + 1], axis=0)
                                             ).then_inc(d_g[r], 16)
                with e.Fori(0, SUPER // RING) as b:
                    for r in range(RING):
                        gather(b * RING + r, r)
                for r in range(SUPER % RING):
                    gather(SUPER // RING * RING + r, r)
            with e.Fori(0, TILES // GROUP) as g:
                for u in range(GROUP):
                    if u == 0:
                        e.wait_ge(v_row, g * 2 + 2)
                        hold(e, "Pool")
                    e.indirect_dma_start(srt_d, bass.IndirectOffsetOnAxis(ap=pslot[:, u:u + 1], axis=0),
                                         rows[:, u, :], None, bounds_check=SLOTS * P - 1,
                                         oob_is_err=False).then_inc(d_srt[u], 16)
            with e.Fori(0, SLOTS // 2) as jj:
                for u in range(2):
                    VT.wait(e, "o", jj * 2 + u)
                    hold(e, "Pool")
                    e.indirect_dma_start(out, bass.IndirectOffsetOnAxis(ap=RB[:, u, C + 1:C + 2].bitcast(I32), axis=0),
                                         o_sb[:, u, :], None, bounds_check=N - 1,
                                         oob_is_err=False).then_inc(d_out[u], 16)

        @block.vector
        def _(e):
            n_setup = [0]

            def step(ins):
                v_setup.done(ins, f"s{n_setup[0]}")
                v_setup.wait(e, f"s{n_setup[0]}", 0)
                n_setup[0] += 1

            e.sem_inc(PI.sem, PI.credit)
            for l in (AN, PN, VF1, PF1, AMA, VMA, PMA, PMB, AMB, VMB, VG, AG, PG, VT, AT, PT):
                e.sem_inc(l.sem, l.credit)
            e.wait_ge(p_const, 6)
            step(e.tensor_copy(iota16[:], ii[:, 0:P]))
            step(e.tensor_copy(iof[:, 0:P + 3], ii[:]))
            step(e.tensor_scalar(ident[:], iof[:, 0:P], iof[:, P + 2:P + 3], None, ALU.is_equal))
            step(e.tensor_scalar(upper[:], iof[:, 0:P], iof[:, P + 2:P + 3], None, ALU.is_gt))
            step(e.memset(ones16[:], 1.0))
            step(e.memset(ones1[:], 1.0))
            step(e.memset(zero16[:], 0.0))
            step(e.memset(epsb[:], EPS_LN))
            e.sem_inc(s_const, 1)
            step(e.tensor_copy(ikf[:], ik[:]))
            step(e.tensor_copy(itf[:], it[:]))
            step(e.tensor_scalar(vmask[:], itf[:], float(N), None, ALU.is_lt))
            e.wait_ge(d_edges, 48)
            step(e.tensor_copy(dst, dsti))
            step(e.tensor_scalar(tl, tv.bitcast(I32)[:, 0:SUPER], 7, None, ALU.logical_shift_right))
            step(e.tensor_copy(klast, tl))
            step(e.tensor_tensor(klast, klast, ikf[:, 0:SUPER], ALU.add))
            for j in range(2):
                step(e.tensor_scalar(cmp, klast, iof[:, P + j:P + j + 1], None, ALU.is_lt))
                step(e.tensor_reduce(ckc[:, j:j + 1], cmp, AX.X, ALU.add))
            e.sem_inc(s_ck, 1)
            step(e.memset(ftf, 0.0))
            step(e.tensor_scalar(ftf[:, RING:SUPER], klast[0:1, 0:SUPER - RING], 1.0, None, ALU.add))
            step(e.tensor_copy(free_tab[:], ftf))
            for g in range(GROUP):
                e.wait_ge(d_x[g], 32)
                with e.Fori(g * GROUP, (g + 1) * GROUP) as i:
                    e.bn_stats(st6[:, bass.ds(i, 1), :].rearrange("p a c -> p (a c)"),
                               res[:, bass.ds(i, 1), 0:C].rearrange("p a c -> p (a c)")).then_inc(v_st, 1)
            e.wait_ge(v_st, TILES)
            me, qe, mo, qo = (st6[:, :, n] for n in (1, 2, 4, 5))
            half = 0.5 / (C // 2)
            step(e.tensor_tensor(mv[:, :, 0], me, mo, ALU.add))
            step(e.tensor_tensor(mv[:, :, 1], me, mo, ALU.subtract))
            step(e.tensor_scalar(mv[:, :, 0], mv[:, :, 0], 0.5, None, ALU.mult))
            step(e.tensor_tensor(mv[:, :, 1], mv[:, :, 1], mv[:, :, 1], ALU.mult))
            step(e.tensor_tensor(sd[:], qe, qo, ALU.add))
            step(e.tensor_scalar(sd[:], sd[:], half, None, ALU.mult))
            step(e.scalar_tensor_tensor(mv[:, :, 1], mv[:, :, 1], 0.25, sd[:], ALU.mult, ALU.add))
            e.sem_inc(s_var, 1)
            e.wait_ge(a_setup, 1)
            step(e.reciprocal(rstd[:], sd[:]))
            with e.Fori(0, TILES // GROUP) as g:
                for u in range(GROUP):
                    i = g * GROUP + u
                    e.wait_ge(d_xst[u], g * 32 + OPENED)
                    e.wait_ge(PN.sem, g * GROUP + PN.credit)
                    VN.done(e.tensor_scalar(xb[:, u, :], res[:, bass.ds(i, 1), 0:C].rearrange("p a c -> p (a c)"),
                                            mv[:, bass.ds(i, 1), 0:1].rearrange("p a c -> p (a c)"),
                                            rstd[:, bass.ds(i, 1)], ALU.subtract, ALU.mult), "xn")
                    AN.wait(e, "hi", i)
                    VN.done(e.tensor_tensor(xhl[:, u, C:2 * C], xb[:, u, :], xhl[:, u, 0:C], ALU.subtract), "lo")
            e.wait_ge(d_ck, 32)
            step(e.tensor_tensor(tf, ikf[:], tv[:], ALU.subtract))
            step(e.tensor_copy(tab[:, 0, :], tv[0:1, :]))
            step(e.tensor_copy(tab[:, 1, :], tf[0:1, :]))
            step(e.tensor_scalar(tab[:, 3, :], tab[:, 0, :], RING - 1, None, ALU.bitwise_and))
            step(e.memset(tab[:, 2, :], 1))
            step(e.tensor_tensor(tab[:, 2, 0:ITEMS - 1], tf[0:1, 1:ITEMS], tf[0:1, 0:ITEMS - 1], ALU.subtract))
            step(e.tensor_scalar(tv[:], tf, float(P), None, ALU.mult))
            e.sem_inc(s_tab, 1)

            def item(k, u, nu, layer):
                g = k + layer * ITEMS
                c, t, last = item_regs(e, k, ["c", "t", "last"])
                e.wait_ge(PI.sem, g + (PI.credit + 1 - nu))
                VI.done(e.tensor_scalar(rel[:, u, :], dst[:, bass.ds(c * SC, SC)], tv[:, bass.ds(k, 1)], None,
                                        ALU.subtract), "rel")
                VI.wait(e, "rel", g)
                for j in range(SC):
                    VI.done(e.tensor_scalar(S[:, u, j, :], iota16[:], rel[:, u, j:j + 1], None, ALU.is_equal), f"S{j}")
                return g, t, last

            def tile_mean(line, t):
                rc = RC[:, bass.ds(t, 1)]
                line.done(e.tensor_scalar(lo[:], AGG[:, C:2 * C], rc, None, ALU.mult), "lo")
                line.wait(e, "lo", t)
                line.done(e.scalar_tensor_tensor(mean[:], AGG[:, 0:C], rc, lo[:], ALU.mult, ALU.add), "mean")

            def res_tile(t):
                return res[:, bass.ds(t, 1), 0:C].rearrange("p a c -> p (a c)")

            def finish1(g, t, mix_done):
                PI.wait(e, "sum", g)
                VF1.done(e.tensor_scalar(cntv[:], CNT[:, 0:1], 1.0, None, ALU.max), "cnt")
                VF1.wait(e, "cnt", t)
                VF1.done(e.reciprocal(RC[:, bass.ds(t, 1)], cntv[:]), "rc")
                VF1.wait(e, "rc", t)
                tile_mean(VF1, t)
                PF1.wait(e, "tr1", t)
                VF1.done(e.tensor_copy(mT[:], FT[:, 0:C].rearrange("p (h t) -> p h t", h=CH)), "mT")
                AF1.wait(e, "relu", t)
                e.wait_ge(d_h, t * 16 + OPENED)
                VF1.done(e.tensor_copy(HL[:, 0:C], hb[:]), "hi")
                VF1.wait(e, "hi", t)
                VF1.done(e.tensor_tensor(HL[:, C:2 * C], hb[:], HL[:, 0:C], ALU.subtract), "hlo")
                PF1.wait(e, "tr2", t)
                VF1.done(e.tensor_copy(hT[:], FT[:, C:2 * C].rearrange("p (h t) -> p h t", h=CH)), "hT")
                PF1.wait(e, "r2", t)
                mix_done()
                VF1.done(e.tensor_tensor(res_tile(t), res_tile(t), FO[:, C:2 * C], ALU.add), "res")

            with e.Fori(0, TILES) as i:
                for u in range(ITEMS_A):
                    g, t, last = item(i * ITEMS_A + u, u, ITEMS_A, 0)
                    with e.If(last == 1):
                        finish1(g, t, lambda: None)
                PMA.wait(e, "acc", i, 1)
                VMA.done(e.tensor_copy(v1[:, :, P:P + 1], vmask[:, bass.ds(i, 1)].unsqueeze(1).to_broadcast([P, CH, 1])), "one")
                AMA.wait(e, "rk", i)
                VMA.done(e.scalar_tensor_tensor(kb, ek, 1.0, rk, ALU.min, ALU.add), "k")
                AMA.wait(e, "rq", i)
                e.wait_ge(d_q, i * 16 + OPENED)
                VMA.done(e.scalar_tensor_tensor(qb, eq, 1.0, rq, ALU.min, ALU.add), "q")
            n_kv = [0]

            def kv(ins):
                v_kv.done(ins, f"s{n_kv[0]}")
                v_kv.wait(e, f"s{n_kv[0]}", 0)
                n_kv[0] += 1
            kv(e.memset(KVs, 0.0))
            PMA.wait(e, "acc", TILES - 1)
            for h in range(CH):
                acc = B6[:, h * (P + 1):(h + 1) * (P + 1)]
                for q in range(P // HD):
                    a = slice(q * HD, (q + 1) * HD)
                    kv(e.tensor_copy(KVs[a, h, a], acc[a, a]))
                    kv(e.tensor_copy(KVs[a, h, P + q:P + q + 1], acc[a, P:P + 1]))
            with e.Fori(0, TILES) as i:
                for u in range(ITEMS_B):
                    g, t, last = item(i * ITEMS_B + (u + TILES * ITEMS_A), u, ITEMS_B, 0)
                    with e.If(last == 1):
                        finish1(g, t, lambda: VMB.wait(e, "res", i, 1))
                PMB.wait(e, "t", i)
                den = B4[:, 0:CH * (P + 4)].rearrange("p (h m) -> p h m", h=CH)[:, :, P:P + 4]
                num = B4[:, 0:CH * (P + 4)].rearrange("p (h m) -> p h m", h=CH)[:, :, 0:P]
                VMB.done(e.tensor_scalar(zd.rearrange("p (h q) -> p h q", h=CH), den, EPS_ATTN, None, ALU.add), "den")
                VMB.wait(e, "den", i)
                VMB.done(e.reciprocal(zd, zd), "rc")
                VMB.wait(e, "rc", i)
                for_h = num.rearrange("p h (q m) -> p h q m", m=HD)
                VMB.done(e.tensor_tensor(m_t.rearrange("p (h q m) -> p h q m", h=CH, m=HD), for_h,
                                         zd.rearrange("p (h q) -> p h q", h=CH).unsqueeze(3).to_broadcast([P, CH, P // HD, HD]),
                                         ALU.mult), "tz")
                VMB.wait(e, "tz", i)
                e.wait_ge(d_lx, i * 16 + 16)
                VMB.done(e.tensor_tensor(m_s[:], m_t[:], xnS, ALU.add), "s")
                VMB.wait(e, "s", i)
                layer_norm(e, VMB, i, "A", m_s[:])
                VMB.done(e.tensor_scalar(m_t[:], m_s[:], lnt[:, 0:1], lnt[:, 3:4], ALU.subtract, ALU.mult), "n1")
                VMB.wait(e, "n1", i)
                VMB.done(e.tensor_tensor(m_t[:], m_t[:], lng1, ALU.mult), "g1")
                VMB.wait(e, "g1", i)
                VMB.done(e.tensor_tensor(m_x1, m_t[:], lnb1, ALU.add), "x1")
                PMB.wait(e, "w2", i)
                VMB.done(e.tensor_tensor(m_s[:], B6[:, 0:C], m_x1, ALU.add), "s2")
                VMB.wait(e, "s2", i)
                layer_norm(e, VMB, i, "B", m_s[:])
                VMB.done(e.tensor_scalar(m_t[:], m_s[:], lnt[:, 0:1], lnt[:, 3:4], ALU.subtract, ALU.mult), "n2")
                VMB.wait(e, "n2", i)
                VMB.done(e.tensor_tensor(m_t[:], m_t[:], lng2, ALU.mult), "g2")
                VMB.wait(e, "g2", i)
                VMB.done(e.tensor_tensor(m_o, m_t[:], lnb2, ALU.add), "b2")
                VMB.wait(e, "b2", i)
                e.wait_ge(VF1.sem, (t + last) * VF1.n + VF1.credit)
                VMB.done(e.tensor_tensor(res_tile(i), res_tile(i), m_o, ALU.add), "res")
            VMB.wait(e, "res", TILES - 1)
            VF1.wait(e, "res", TILES - 1)
            with e.Fori(0, TILES) as i:
                for u in range(ITEMS_2):
                    g, t, last = item(i * ITEMS_2 + u, u, ITEMS_2, 1)
                    with e.If(last == 1):
                        PI.wait(e, "sum", g)
                        tile_mean(VF2, t)
                        PF2.wait(e, "tr1", t)
                        VF2.done(e.tensor_copy(mT[:], FT[:, 0:C].rearrange("p (h t) -> p h t", h=CH)), "mT")
                        PF2.wait(e, "o", t)
                        VF2.done(e.tensor_tensor(res_tile(t), res_tile(t), FO[:, 0:C], ALU.add), "x2")
            VF2.wait(e, "x2", TILES - 1)
            with e.Fori(0, TILES) as i:
                layer_norm(e, VG, i, "G", res_tile(i))
                PG.wait(e, "tr", i, 1)
                VG.done(e.tensor_scalar(m_t[:], res_tile(i), lnt[:, 0:1], lnt[:, 3:4], ALU.subtract, ALU.mult), "xf")
                PG.wait(e, "lg", i)
                VG.done(e.tensor_copy(LG[:, bass.ds(i, 1), :].rearrange("p a e -> p (a e)"), B6[:, 0:NE]), "lg")
            VG.wait(e, "lg", TILES - 1)
            n_rt = [0]

            def rt(ins):
                v_rt.done(ins, f"s{n_rt[0]}")
                v_rt.wait(e, f"s{n_rt[0]}", 0)
                n_rt[0] += 1

            def over_e(a):
                return a.unsqueeze(2).to_broadcast([P, TILES, NE])

            def over_t(a):
                return a.unsqueeze(1).to_broadcast([P, TILES, NE])
            rt(e.tensor_reduce(mx[:], LG[:], AX.X, ALU.max))
            rt(e.tensor_tensor(E1, LG[:], over_e(mx[:]), ALU.is_equal))
            rt(e.tensor_tensor(LG[:], LG[:], over_e(mx[:]), ALU.subtract))
            e.sem_inc(s_lmax, 1)
            rt(e.tensor_scalar(w8[:], iof[:, 0:NE], -1.0, float(NE), ALU.mult, ALU.add))
            rt(e.tensor_tensor(E2, E1, over_t(w8[:]), ALU.mult))
            rt(e.tensor_reduce(mx[:], E2, AX.X, ALU.max))
            rt(e.tensor_tensor(E1, E2, over_e(mx[:]), ALU.is_equal))
            rt(e.tensor_tensor(E1, E1, over_e(vmask[:]), ALU.mult))
            rt(e.tensor_copy(E16[:], E1))
            e.sem_inc(s_onehot, 1)
            e.wait_ge(a_rt, 1)
            rt(e.tensor_reduce(mx[:], LG[:], AX.X, ALU.add))
            rt(e.reciprocal(res[:, :, C:C + 1], mx[:].unsqueeze(2)))
            rt(e.tensor_copy(res[:, :, C + 1:C + 2].bitcast(I32), it[:].unsqueeze(2)))
            e.wait_ge(pe_rt, 1)
            rt(e.tensor_copy(A1, B5[:, 0:TILES * NE].rearrange("p (t e) -> p t e", e=NE)))
            a, b = A1, A2
            s = 1
            while s < TILES:
                rt(e.tensor_copy(b[:, 0:s, :], a[:, 0:s, :]))
                rt(e.tensor_tensor(b[:, s:, :], a[:, s:, :], a[:, :TILES - s, :], ALU.add))
                a, b = b, a
                s *= 2
            rt(e.tensor_scalar(cti[:], a[:, TILES - 1, :], float(P - 1), None, ALU.add))
            rt(e.tensor_scalar(cti[:], cti[:], 7, None, ALU.logical_shift_right))
            rt(e.memset(start[:], 0.0))
            rt(e.tensor_copy(ctf[:], cti[:]))
            for k in range(NE):
                rt(e.tensor_tensor(start[:, k + 1:k + 2], start[:, k:k + 1], ctf[:, k:k + 1], ALU.add))
            rt(e.tensor_scalar(stp[:], start[:, 0:NE], float(P), None, ALU.mult))
            rt(e.tensor_copy(b[:, 0:1, :], B4[:, 0:NE].unsqueeze(1)))
            rt(e.tensor_tensor(b[:, 1:, :], B4[:, NE:TILES * NE].rearrange("p (t e) -> p t e", e=NE),
                               a[:, 0:TILES - 1, :], ALU.add))
            rt(e.tensor_tensor(b[:], b[:], over_t(stp[:]), ALU.add))
            rt(e.tensor_tensor(b[:], b[:], E1, ALU.mult))
            rt(e.tensor_reduce(mx[:], b[:], AX.X, ALU.add))
            rt(e.tensor_scalar(nv[:], vmask[:], -float(NO_ROW), float(NO_ROW), ALU.mult, ALU.add))
            rt(e.tensor_tensor(mx[:], mx[:], nv[:], ALU.add))
            rt(e.tensor_copy(posi[:], mx[:]))
            rt(e.tensor_tensor(ete, ikf[0:1, 0:SLOTS].unsqueeze(2).to_broadcast([1, SLOTS, NE - 1]),
                               start[0:1, 1:NE].unsqueeze(1).to_broadcast([1, SLOTS, NE - 1]), ALU.is_ge))
            rt(e.tensor_reduce(etf[:], ete, AX.X, ALU.add))
            rt(e.tensor_copy(et[:], etf[:]))
            e.sem_inc(s_et, 1)
            for first, g in turns(e, TILES // GROUP):
                for u in range(GROUP):
                    if not first:
                        e.wait_ge(d_srt[u], g * 16)
                e.tensor_copy(rows, res[:, bass.ds(g * GROUP, GROUP), :]).then_inc(v_row, 1)
                e.tensor_copy(pslot[:], posi[:, bass.ds(g * GROUP, GROUP)]).then_inc(v_row, 1)
            for first, jj in turns(e, SLOTS // 2):
                for u in range(2):
                    i = jj * 2 + u
                    e.wait_ge(d_rb[u], jj * 16 + 16)
                    layer_norm(e, VT, i, "T", RB[:, u, 0:C])
                    PT.wait(e, "tr", i, 1)
                    VT.done(e.tensor_scalar(m_t[:], RB[:, u, 0:C], lnt[:, 0:1], lnt[:, 3:4], ALU.subtract, ALU.mult), "xf")
                    PT.wait(e, "y", i)
                    if not first:
                        e.wait_ge(d_out[u], jj * 16)
                    VT.done(e.scalar_tensor_tensor(o_sb[:, u, :], B6[:, 0:C], RB[:, u, C:C + 1], RB[:, u, 0:C],
                                                   ALU.mult, ALU.add), "o")

        @block.scalar
        def _(e):
            e.wait_ge(s_const, 1)
            e.wait_ge(s_var, 1)
            e.activation(sd[:], mv[:, :, 1], ACT.Sqrt, bias=epsb[:, 0:1]).then_inc(a_setup, 1)
            with e.Fori(0, TILES // GROUP) as g:
                for u in range(GROUP):
                    i = g * GROUP + u
                    VN.wait(e, "xn", i)
                    AN.done(e.activation(xhl[:, u, 0:C], xb[:, u, :], ACT.Copy), "hi")
                    PN.wait(e, "tr", i)
                    AN.done(e.activation(xnT[:, :, bass.ds(i * P, P)],
                                         pb[4 + u % 2][:, 0:C].rearrange("p (h t) -> p h t", h=CH), ACT.Copy), "xnT")
            e.wait_ge(s_tab, 1)
            e.wait_ge(d_w, 16 * 20)

            def xT_copy(line, dst_ap, i):
                line.done(e.activation(dst_ap, xnT[:, :, bass.ds(i * P, P)], ACT.Copy), "xT")

            def finish1(t):
                xT_copy(AF1, xTs[:], t)
                PF1.wait(e, "h", t)
                AF1.done(e.activation(hb[:], FO[:, 0:C], ACT.Relu), "relu")
                VF1.wait(e, "hlo", t)
                e.dma_start(hh_d[bass.ds(t * P, P), :], HL[:]).then_inc(d_h, 16)

            def maybe_finish(k):
                t, last = item_regs(e, k, ["t", "last"])
                with e.If(last == 1):
                    e.wait_ge(PF1.sem, t * PF1.n + PF1.credit)
                    e.wait_ge(VF1.sem, t * VF1.n + VF1.credit)
                    finish1(t)

            AN.wait(e, "xnT", TILES - 1)
            with e.Fori(0, TILES) as i:
                PMA.wait(e, "q", i, 1)
                xT_copy(AMA, xTm, i)
                for u in range(ITEMS_A):
                    maybe_finish(i * ITEMS_A + u)
                PMA.wait(e, "kv", i)
                VMA.wait(e, "k", i, 1)
                AMA.done(e.activation(ek, B4[:, 0:C], ACT.Exp), "ek")
                AMA.done(e.activation(rk, B4[:, 0:C], ACT.Relu), "rk")
                PMA.wait(e, "acc", i, 1)
                AMA.done(e.activation(v1[:, :, 0:P], B4[:, C:2 * C].rearrange("p (h t) -> p h t", h=CH), ACT.Copy), "v")
                PMA.wait(e, "q", i)
                VMA.wait(e, "q", i, 1)
                AMA.done(e.activation(eq, B5[:, 0:C], ACT.Exp), "eq")
                AMA.done(e.activation(rq, B5[:, 0:C], ACT.Relu), "rq")
                VMA.wait(e, "q", i)
                e.dma_start(qT_d[bass.ds(i * P, P), :], qb).then_inc(d_q, 16)
            e.wait_ge(d_q, OPENED + 16 * TILES)
            for u in range(GROUP):
                e.wait_ge(d_xst[u], OPENED + 32 * (TILES // GROUP))

            def load_b(i):
                e.dma_start(xnS, xn_d[bass.ds(i * P, P), :]).then_inc(d_lx, 16)
                e.dma_start(qS, qT_d[bass.ds(i * P, P), :].rearrange("p (h t) -> p h t", h=CH)).then_inc(d_lq, 16)
            load_b(0)
            with e.Fori(0, TILES) as i:
                for u in range(ITEMS_B):
                    maybe_finish(i * ITEMS_B + (u + TILES * ITEMS_A))
                PMB.wait(e, "tr", i)
                AMB.done(e.activation(x1T[:], B7[:, 0:C].rearrange("p (h t) -> p h t", h=CH), ACT.Copy), "x1T")
                with e.If(i < TILES - 1):
                    VMB.wait(e, "s", i)
                    load_b(i + 1)
                PMB.wait(e, "w1", i)
                for h in range(CH):
                    AMB.done(e.activation(hTm[:, h, :], B5[:, h * P:(h + 1) * P], ACT.Gelu, bias=mb1[:, h:h + 1]), f"gl{h}")
            PMB.wait(e, "w2", TILES - 1)
            VMB.wait(e, "res", TILES - 1)
            PF1.wait(e, "r2", TILES - 1)
            for k in range(NE):
                e.dma_start(wd[:, :, k, :], w["fwd"][k].rearrange("(j p) c -> p j c", p=P)).then_inc(d_wd, 16)
            e.dma_start(fbd, w["fbd"].unsqueeze(0)).then_inc(d_wd, 16)
            with e.Fori(0, TILES) as i:
                PG.wait(e, "tr", i)
                AG.done(e.activation(x1T[:], B7[:, 0:C].rearrange("p (h t) -> p h t", h=CH), ACT.Copy), "xT")
                for j in range(HJ):
                    PG.wait(e, f"h{j // 4 * 4 + 3}", i)
                    if j == 0:
                        PG.wait(e, "lg", i, 1)
                    AG.done(e.activation(HT[:, j, :], pb[4 + j // 4][:, (j % 4) * P:(j % 4 + 1) * P], ACT.Gelu,
                                         bias=fb1[:, j:j + 1]), f"g{j}")
            e.wait_ge(s_lmax, 1)
            e.activation(LG[:], LG[:], ACT.Exp).then_inc(a_rt, 1)
            with e.Fori(0, SLOTS // 2) as jj:
                for u in range(2):
                    i = jj * 2 + u
                    PT.wait(e, "tr", i)
                    AT.done(e.activation(x1T[:], B7[:, 0:C].rearrange("p (h t) -> p h t", h=CH), ACT.Copy), "xT")
                    for j in range(HJ):
                        PT.wait(e, f"h{j // 4 * 4 + 3}", i)
                        if j == 0:
                            PT.wait(e, "y", i, 1)
                        AT.done(e.activation(HT[:, j, :], pb[4 + j // 4][:, (j % 4) * P:(j % 4 + 1) * P], ACT.Gelu,
                                             bias=fb1[:, j:j + 1]), f"g{j}")

        @block.tensor
        def _(e):
            e.wait_ge(s_const, 1)
            with e.Fori(0, TILES // GROUP) as g:
                for u in range(GROUP):
                    i = g * GROUP + u
                    VN.wait(e, "xn", i)
                    e.wait_ge(AN.sem, g * (2 * GROUP) + (2 * u - 2 if u else 0) + AN.credit)
                    for h in range(CH):
                        ins = e.transpose(pb[4 + u % 2][:, h * P:(h + 1) * P], xb[:, u, h * P:(h + 1) * P], ident[:])
                    PN.done(ins, "tr")
            e.wait_ge(s_tab, 1)
            e.wait_ge(d_w, 16 * 20)
            AN.wait(e, "xnT", TILES - 1)

            def clear(banks):
                for b in banks:
                    ins = e.matmul(b[:, 0:512], zero16[0:1, 0:P], zero16[0:1, 0:512], start=True, stop=False,
                                   skip_group_check=True)
                return ins
            clear([AGG, CNT, B6])

            def item(k, u, layer):
                g = k + layer * ITEMS
                c, t, last, slot = item_regs(e, k, ["c", "t", "last", "slot"])
                e.wait_ge(s_ready, c + (layer * SUPER + 1))
                VI.wait(e, "S3", g)
                for j in range(SC):
                    if layer == 0:
                        e.matmul(CNT[:, 0:1], S[:, u, j, :], ones16[:, 0:1], start=False, stop=False,
                                 skip_group_check=True)
                    ins = e.matmul(AGG[:], S[:, u, j, :], G[:, bass.ds(slot, 1), j, :].rearrange("p a c -> p (a c)"),
                                   start=False, stop=False, skip_group_check=True)
                PI.done(ins, "sum")
                return t, last

            def transposes(bank, off, a):
                for h in range(CH):
                    ins = e.transpose(bank[:, off + h * P:off + (h + 1) * P], a[:, h * P:(h + 1) * P], ident[:])
                return ins

            def finish1(t):
                VF1.wait(e, "mean", t)
                clear([AGG, CNT])
                PF1.done(transposes(FT, 0, mean), "tr1")
                AF1.wait(e, "xT", t)
                for h in range(CH):
                    e.matmul(FO[:, 0:C], xTs[:, h, :], w1r[:, h, :], start=(h == 0), stop=False)
                e.matmul(FO[:, 0:C], ones1[:], gb1[:], start=False, stop=False)
                VF1.wait(e, "mT", t)
                for h in range(CH):
                    ins = e.matmul(FO[:, 0:C], mT[:, h, :], w1l[:, h, :], start=False, stop=(h == CH - 1))
                PF1.done(ins, "h")
                AF1.wait(e, "relu", t)
                PF1.done(transposes(FT, C, hb), "tr2")
                VF1.wait(e, "hT", t)
                PF1.done(matmuls(e, FO[:, C:2 * C], [(hT[:, 0, :], w2r[:, 0, :]), (hT[:, 1, :], w2r[:, 1, :]),
                                                     (ones1[:], gb2[:])]), "r2")

            with e.Fori(0, TILES) as i:
                AMA.wait(e, "v", i, 1)
                AMA.wait(e, "xT", i)
                PMA.done(matmuls(e, B4[:], [(xTm[:, h, :], wkv[:, h, :]) for h in range(CH)]), "kv")
                AMA.wait(e, "rq", i, 1)
                for d in range(CH):
                    ins = matmuls(e, B5[:, d * P:(d + 1) * P], [(wq[:, h, d * P:(d + 1) * P], xTm[:, h, :]) for h in range(CH)])
                PMA.done(ins, "q")
                for u in range(ITEMS_A):
                    t, last = item(i * ITEMS_A + u, u, 0)
                    with e.If(last == 1):
                        finish1(t)
                VMA.wait(e, "k", i)
                AMA.wait(e, "v", i)
                for h in range(CH):
                    ins = e.matmul(B6[:, h * (P + 1):(h + 1) * (P + 1)], kb[:, h * P:(h + 1) * P], v1[:, h, :],
                                   start=False, stop=False, skip_group_check=True)
                PMA.done(ins, "acc")
            e.wait_ge(v_kv.sem, 1 + 2 * CH * (P // HD))
            with e.Fori(0, TILES) as i:
                for u in range(ITEMS_B):
                    t, last = item(i * ITEMS_B + (u + TILES * ITEMS_A), u, 0)
                    with e.If(last == 1):
                        finish1(t)
                e.wait_ge(d_lq, i * 16 + 16)
                for h in range(CH):
                    ins = e.matmul(B4[:, h * (P + 4):(h + 1) * (P + 4)], qS[:, h, :], KVs[:, h, :], start=True, stop=True)
                PMB.done(ins, "t")
                VMB.wait(e, "x1", i)
                PMB.done(transposes(B7, 0, m_x1), "tr")
                AMB.wait(e, "x1T", i)
                for d in range(CH):
                    ins = matmuls(e, B5[:, d * P:(d + 1) * P], [(mw1[:, h, d * P:(d + 1) * P], x1T[:, h, :]) for h in range(CH)])
                PMB.done(ins, "w1")
                AMB.wait(e, "gl1", i)
                PMB.done(matmuls(e, B6[:, 0:C], [(hTm[:, 0, :], mw2[:, 0, :]), (hTm[:, 1, :], mw2[:, 1, :]),
                                                 (ones1[:], mb2)]), "w2")
            VF1.wait(e, "res", TILES - 1)
            with e.Fori(0, TILES) as i:
                for u in range(ITEMS_2):
                    t, last = item(i * ITEMS_2 + u, u, 1)
                    with e.If(last == 1):
                        VF2.wait(e, "mean", t)
                        clear([AGG])
                        PF2.done(transposes(FT, 0, mean), "tr1")
                        VF2.wait(e, "mT", t)
                        PF2.done(matmuls(e, FO[:, 0:C], [(mT[:, h, :], w2l[:, h, :]) for h in range(CH)]), "o")

            def hidden(line, al, i):
                for j in range(HJ):
                    if j == 0:
                        al.wait(e, "xT", i)
                    if j % 4 == 0:
                        al.wait(e, f"g{j + 3}", i, 1)
                    line.done(matmuls(e, pb[4 + j // 4][:, (j % 4) * P:(j % 4 + 1) * P],
                                      [(fw1[:, h, j * P:(j + 1) * P], x1T[:, h, :]) for h in range(CH)]), f"h{j}")

            with e.Fori(0, TILES) as i:
                VG.wait(e, "xf", i)
                AG.wait(e, "xT", i, 1)
                PG.done(transposes(B7, 0, m_t), "tr")
                hidden(PG, AG, i)
                AG.wait(e, "g7", i)
                VG.wait(e, "lg", i, 1)
                PG.done(matmuls(e, B6[:, 0:NE], [(HT[:, j, :], fwg[:, j, :]) for j in range(HJ)] + [(ones1[:], fbg[:])]), "lg")
            e.wait_ge(s_onehot, 1)
            e16 = E16.rearrange("p t e -> p (t e)")
            e.matmul(B4[:, 0:TILES * NE], upper[:], e16, start=True, stop=True)
            e.matmul(B5[:, 0:TILES * NE], ones16[:], e16, start=True, stop=True).then_inc(pe_rt, 1)
            e.wait_ge(d_wd, 16 * (NE + 1))
            e.wait_ge(s_et, 1)
            with e.Fori(0, SLOTS // 2) as jj:
                for u in range(2):
                    i = jj * 2 + u
                    ex = e.value_load(et[0:1, bass.ds(i, 1)], min_val=0, max_val=NE - 1)
                    VT.wait(e, "xf", i)
                    AT.wait(e, "xT", i, 1)
                    PT.done(transposes(B7, 0, m_t), "tr")
                    hidden(PT, AT, i)
                    VT.wait(e, "o", i, 1)
                    for j in range(HJ):
                        AT.wait(e, f"g{j}", i)
                        e.matmul(B6[:, 0:C], HT[:, j, :], wd[:, j, bass.ds(ex, 1), :].rearrange("p a c -> p (a c)"),
                                 start=(j == 0), stop=False)
                    PT.done(e.matmul(B6[:, 0:C], ones1[:], fbd[:, bass.ds(ex, 1), :].rearrange("p a c -> p (a c)"),
                                     start=False, stop=True), "y")


def kernel(**inputs):
    import numpy as np
    import concourse.bacc as bacc
    from concourse.bass_utils import run_bass_kernel_spmd

    a = {k: np.asarray(v) for k, v in inputs.items()}
    pad = SUPER * SC * P - EDGES
    src = np.concatenate([a["src"], np.zeros(pad, np.int32)])
    dst = np.concatenate([a["dst"], np.full(pad, PAD_NODE, np.int32)])
    laid = {
        "x": a["x"],
        "srcL": src.reshape(SUPER * SC, P).T, "dstL": dst.reshape(SUPER * SC, P).T,
        "dst_tail": dst[SC * P - 1::SC * P],
        "w1lT": a["L0_gnn_W1l"].T, "w1rT": a["L0_gnn_W1r"].T, "w2lT": a["L0_gnn_W2l"].T, "w2rT": a["L0_gnn_W2r"].T,
        "gb1": a["L0_gnn_b1"], "gb2": a["L0_gnn_b2"],
        "wqkvT": a["L0_mix_Wqkv"].T, "mw1T": a["L0_mix_W1"].T, "mw2T": a["L0_mix_W2"].T,
        "ln1_g": a["L0_mix_ln1_g"], "ln1_b": a["L0_mix_ln1_b"], "ln2_g": a["L0_mix_ln2_g"], "ln2_b": a["L0_mix_ln2_b"],
        "mb1L": a["L0_mix_b1"].reshape(CH, P).T, "mb2": a["L0_mix_b2"],
        "fw1": a["L0_ffn_W1"], "fb1L": a["L0_ffn_b1"].reshape(HJ, P).T,
        "fwg": a["L0_ffn_Wg"], "fbg": a["L0_ffn_bg"], "fwd": a["L0_ffn_Wd"], "fbd": a["L0_ffn_bd"],
    }
    nc = bacc.Bacc("TRN2", target_bir_lowering=False, num_devices=1)
    arrays, ap = {}, {}
    for name, v in laid.items():
        v = np.ascontiguousarray(v)
        arrays[f"in_{name}_dram"] = v
        ap[name] = nc.dram_tensor(f"in_{name}_dram", v.shape, mybir.dt.from_np(v.dtype), kind="ExternalInput").ap()
    out = nc.dram_tensor("out_0_dram", (N, C), F32, kind="ExternalOutput").ap()
    build(nc, ap.pop("x"), ap.pop("srcL"), ap.pop("dstL"), ap.pop("dst_tail"), ap, out)
    r = run_bass_kernel_spmd(nc, [arrays], core_ids=[0])
    return r.results[0]["out_0_dram"]
```

```python
from contextlib import ExitStack

import concourse.bass as bass
import concourse.mybir as mybir

F32, F16, I32 = mybir.dt.float32, mybir.dt.float16, mybir.dt.int32
ALU, ACT, AX = mybir.AluOpType, mybir.ActivationFunctionType, mybir.AxisListType

P = 128
N, C, EDGES = 6250, 256, 100000
CH = C // P
TILES = -(-N // P)
LAST_ROWS = N - (TILES - 1) * P
SC = 4
SUPER = EDGES // (SC * P) + 2
PAD_NODE = TILES * P - 1
ITEMS = SUPER + TILES - 1
RING = 4
HEADS, HD = 8, 32
HID, NE = 1024, 8
HJ = HID // P
SLOTS = (N + NE * (P - 1)) // P
ROW = C + 2
EPS_LN, EPS_ATTN = 1e-5, 1e-6
ITEMS_A, ITEMS_B, ITEMS_2 = 3, 2, 5
NS = ITEMS_2
NO_ROW = 1 << 20
RB_SLOTS = 4
assert SLOTS % RB_SLOTS == 0
OPENED = 16
assert ITEMS == TILES * (ITEMS_A + ITEMS_B) == TILES * ITEMS_2
GROUP = 7
assert TILES % GROUP == 0


class Line:

    def __init__(self, sem, names, credit=False):
        self.sem, self.names = sem, list(names)
        self.at = 0
        self.n = len(self.names)
        self.credit = self.n * credit
        assert len(set(self.names)) == self.n

    def done(self, ins, name):
        assert self.names[self.at % self.n] == name, (self.names[self.at % self.n], name)
        self.at += 1
        ins.then_inc(self.sem, 1)

    def wait(self, eng, name, i, back=0):
        eng.wait_ge(self.sem, i * self.n + (self.credit + self.names.index(name) + 1 - back * self.n))


def turns(eng, n):
    yield True, 0
    with eng.Fori(1, n) as i:
        yield False, i


def ln_names(p):
    return [p + x for x in ("st", "ag", "v", "y0", "a1", "b1", "y1", "a2", "b2", "y2", "a3", "b3", "y3")]


def build(nc, x, srcL, dstL, dst_tail, w, out):
    with ExitStack() as ctx:
        def sb(name, shape, dt=F32):
            return ctx.enter_context(nc.sbuf_tensor(name, shape, dt))

        def sem(name):
            return ctx.enter_context(nc.semaphore(name))

        def dram(name, shape, dt=F32):
            return nc.dram_tensor(name, shape, dt, kind="Internal").ap()

        xh_d = dram("xh_d", [TILES * P, 2 * C], F16)
        hh_d = dram("hh_d", [TILES * P, 2 * C], F16)
        xn_d = dram("xn_d", [(TILES + 1) * P, C])
        qT_d = dram("qT_d", [(TILES + 1) * P, C])
        ck_d = dram("ck_d", [2 * P])
        srt_d = dram("srt_d", [SLOTS * P, ROW])

        res = sb("res", [P, TILES, ROW])
        big = sb("big", [P, 16640])
        G = sb("G", [P, RING, SC, 2 * C], F16)
        S = sb("S", [P, NS, SC, P], F16)
        rel = sb("rel", [P, NS, SC])
        edges = sb("edges", [P, 3, SUPER * SC])
        src, dsti, dst = edges[:, 0, :].bitcast(I32), edges[:, 1, :].bitcast(I32), edges[:, 2, :]
        ix = sb("ix", [P, RING, SC], I32)
        words = sb("words", [1, 3, TILES], I32)
        free_words = sb("free_words", [1, TILES], I32)
        tv = sb("tv", [P, 2 * P])
        iota16 = sb("iota16", [P, P], F16)
        ident = sb("ident", [P, P])
        ones16 = sb("ones16", [P, P], F16)
        ones1 = sb("ones1", [1, P])
        zero16 = sb("zero16", [1, 2 * C], F16)
        vmask = sb("vmask", [P, TILES])
        epsb = sb("epsb", [P, 1])
        RC = sb("RC", [P, TILES])
        cntv = sb("cntv", [P, 1])
        lo = sb("lo", [P, C])
        mean = sb("mean", [P, C])
        mT = sb("mT", [P, CH, P])
        xTs = sb("xTs", [P, CH, P])
        hb = sb("hb", [P, C])
        hT = sb("hT", [P, CH, P])
        HL = sb("HL", [P, 2 * C], F16)
        w1l, w1r, w2l, w2r = (sb(f"w{n}", [P, CH, C]) for n in ("1l", "1r", "2l", "2r"))
        gb1, gb2 = sb("gb1", [1, C]), sb("gb2", [1, C])
        fw1 = sb("fw1", [P, CH, HID])
        fwg = sb("fwg", [P, HJ, NE])
        fb1 = sb("fb1", [P, HJ])
        fbg = sb("fbg", [1, NE])
        lnt = sb("lnt", [P, 16])

        used = [0]

        def carve(n, shape):
            a = big[:, used[0]:used[0] + n]
            used[0] += n
            names = "abc"[:len(shape)]
            kw = {names[i]: shape[i] for i in range(len(shape))}
            return a.rearrange(f"p ({' '.join(names)}) -> p {' '.join(names)}", **kw) if len(shape) > 1 else a

        xnT = carve(CH * TILES * P, [CH, TILES * P])
        wq = carve(CH * C, [CH, C])
        wkv = carve(CH * 2 * C, [CH, 2 * C])
        mw1 = carve(CH * C, [CH, C])
        mw2 = carve(CH * C, [CH, C])
        lng1, lnb1, lng2, lnb2 = (carve(C, [C]) for _ in range(4))
        mb1 = carve(CH, [CH])
        mb2 = big[0:1, used[0]:used[0] + C]
        used[0] += C
        assert used[0] <= 16640
        wd = big[:, 0:HJ * NE * C].rearrange("p (j e c) -> p j e c", j=HJ, e=NE)
        mbuf = sb("mbuf", [P, 2080])
        parts = {"xTm": C, "xnS": C, "qS": C, "hTm": C, "m_x1": C, "m_o": C, "KVs": CH * (P + 4), "v1": CH * (P + 1), "zd": HEADS}
        at = 0
        for name, n in parts.items():
            parts[name] = mbuf[:, at:at + n]
            at += n
        assert at <= 2080
        xTm, qS, hTm, KVs, v1 = (parts[n].rearrange("p (h t) -> p h t", h=CH) for n in ("xTm", "qS", "hTm", "KVs", "v1"))
        xnS, m_x1, m_o, zd = (parts[n] for n in ("xnS", "m_x1", "m_o", "zd"))
        fbd = mbuf[0:1, 0:NE * C].rearrange("p (e c) -> p e c", e=NE)
        abuf = sb("abuf", [P, 6, C])
        ek, rk, kb, eq, rq, qb = (abuf[:, n, :] for n in range(6))
        HT = abuf[:, 0:4, :].rearrange("p a b -> p (a b)").rearrange("p (j t) -> p j t", j=HJ)
        x1T = sb("x1T", [P, CH, P])
        m_s, m_t = (sb(n, [P, C]) for n in ("m_s", "m_t"))
        Gf = G.rearrange("p a b c -> p (a b c)").bitcast(F32)
        xhl = G.rearrange("p a b c -> p (a b) c")[:, 0:GROUP, :]
        xb = Gf[:, GROUP * C:2 * GROUP * C].rearrange("p (t c) -> p t c", c=C)
        st6 = sb("st6", [P, TILES, 6])
        mv = sb("mv", [P, TILES, 2])
        LG = sb("LG", [P, TILES, NE])

        ii, ik, it = sb("ii", [P, P + 3], I32), sb("ik", [P, 2 * P], I32), sb("it", [P, TILES], I32)
        iof, ikf, itf = sb("iof", [P, P + 3]), sb("ikf", [P, 2 * P]), sb("itf", [P, TILES])
        upper = sb("upper", [P, P], F16)
        scrap = sb("scrap", [1, 32], I32)
        zrow = sb("zrow", [P, ROW])
        ab = abuf.rearrange("p a c -> p (a c)")
        tl, klast, cmp = ab[:, 0:SUPER].bitcast(I32), ab[:, 256:256 + SUPER], ab[:, 512:512 + SUPER]
        tlf, tf = ab[:, 768:768 + SUPER], ab[:, 1024:1024 + 2 * P]
        fw, lastf = ab[0:1, 512 + SUPER:512 + SUPER + TILES], ab[0:1, 1280:1280 + 2 * P]
        ckc = sb("ckc", [P, 2])
        sd, rstd = sb("sd", [P, TILES]), sb("rstd", [P, TILES])
        mx, nv, posi = sb("mx", [P, TILES]), sb("nv", [P, TILES]), sb("posi", [P, TILES], I32)
        E1, E2, A1, A2 = (edges.rearrange("p a b -> p (a b)")[:, n * TILES * NE:(n + 1) * TILES * NE]
                          .rearrange("p (t e) -> p t e", e=NE) for n in range(4))
        E16 = sb("E16", [P, TILES, NE], F16)
        w8, stp, ctf = sb("w8", [P, NE]), sb("stp", [P, NE]), sb("ctf", [P, NE])
        cti, start = sb("cti", [P, NE], I32), sb("start", [P, NE + 1])
        ete = edges.rearrange("p a b -> p (a b)")[0:1, 4 * TILES * NE:4 * TILES * NE + SLOTS * (NE - 1)].rearrange("p (t e) -> p t e", e=NE - 1)
        etf, et = sb("etf", [1, SLOTS]), sb("et", [1, SLOTS], I32)
        pslot = sb("pslot", [P, GROUP], I32)
        rows = Gf[:, 0:GROUP * ROW].rearrange("p (t c) -> p t c", c=ROW)
        RB = Gf[:, 1920:1920 + RB_SLOTS * ROW].rearrange("p (t c) -> p t c", c=ROW)
        o_sb = Gf[:, 3072:3072 + RB_SLOTS * C].rearrange("p (t c) -> p t c", c=C)

        pb = [ctx.enter_context(nc.psum_tensor(f"bank{i}", [P, 512], F32)) for i in range(8)]
        AGG, CNT, FT, FO, B4, B5, B6, B7 = pb
        FR = B7

        d_x = [sem(f"d_x{g}") for g in range(GROUP)]
        d_edges, d_w, d_ck = sem("d_edges"), sem("d_w"), sem("d_ck")
        d_xst = [sem(f"d_xst{g}") for g in range(GROUP)]
        d_g = [sem(f"d_g{r}") for r in range(RING)]
        d_h, d_q, d_lx, d_lq, d_wd, d_init = (sem(n) for n in ("d_h", "d_q", "d_lx", "d_lq", "d_wd", "d_init"))
        s_ready = sem("s_ready")
        p_ix = sem("p_ix")
        p_setup = sem("p_setup")
        v_setup = Line(sem("v_setup"), [f"s{i}" for i in range(200)])
        s_tab, s_const, s_ck, s_lmax, s_onehot, s_var = (sem(n) for n in ("s_tab", "s_const", "s_ck", "s_lmax", "s_onehot", "s_var"))
        passed = {n: sem("passed_" + n) for n in ("SP", "Pool", "DVE", "Activation")}

        def hold(e, name):
            e.sem_inc(passed[name], 1)
        p_const, v_st = sem("p_const"), sem("v_st")
        a_setup = sem("a_setup")
        VN = Line(sem("v_norm"), ["xn", "lo"])
        AN = Line(sem("a_norm"), ["hi", "xnT"], credit=1)
        PN = Line(sem("pe_norm"), ["tr"], credit=1)
        VI = Line(sem("v_item"), ["rel", "S0", "S1", "S2", "S3"])
        PI = Line(sem("pe_item"), ["sum"], credit=NS)
        pe_zero = sem("pe_zero")
        VM1 = Line(sem("v_mean1"), ["cnt", "rc", "lo", "mean"])
        VT1 = Line(sem("v_meanT1"), ["mT"])
        VB1 = Line(sem("v_hidden1"), ["hi", "hlo", "hT", "res"], credit=4)
        AX1 = Line(sem("a_xT1"), ["xT"])
        AR1 = Line(sem("a_relu1"), ["relu"], credit=2)
        PT1 = Line(sem("pe_tr1"), ["tr1"])
        PH1 = Line(sem("pe_h1"), ["h"])
        PB1 = Line(sem("pe_hidden1"), ["tr2", "r2"])
        VM2 = Line(sem("v_mean2"), ["lo", "mean"])
        VT2 = Line(sem("v_meanT2"), ["mT"])
        VX2 = Line(sem("v_x2"), ["x2"] + ln_names("G") + ["xf"])
        VL2 = Line(sem("v_lg2"), ["lg"], credit=4)
        PT2 = Line(sem("pe_tr2"), ["tr1"])
        PO2 = Line(sem("pe_o2"), ["o"])
        PX2 = Line(sem("pe_x2"), ["tr"], credit=2)
        PG2 = Line(sem("pe_hid2"), [f"h{j}" for j in range(HJ)])
        PL2 = Line(sem("pe_lg2"), ["lg"], credit=3)
        AT2 = Line(sem("a_x2T"), ["xT"])
        AG2 = Line(sem("a_hid2"), [f"g{j}" for j in range(HJ)], credit=1)
        AMA = Line(sem("a_mixa"), ["xT", "ek", "rk", "v", "eq", "rq"], credit=1)
        VMA = Line(sem("v_mixa"), ["one", "k", "q"], credit=1)
        PMA = Line(sem("pe_mixa"), ["kv", "q"], credit=1)
        PAC = Line(sem("pe_acc"), ["acc"], credit=1)
        v_kv = Line(sem("v_kv"), [f"s{i}" for i in range(20)])
        PMt = Line(sem("pe_att"), ["t"])
        PMB = Line(sem("pe_mlp"), ["tr", "w1", "w2"], credit=1)
        AMB = Line(sem("a_mlp"), ["x1T", "gl0", "gl1"])
        VD1 = Line(sem("v_ln1"), ["den", "rc", "tz", "s"] + ln_names("A") + ["n1", "g1", "x1"])
        VD2 = Line(sem("v_ln2"), ["s2"] + ln_names("B") + ["n2", "g2", "b2", "res"], credit=3)
        v_rt = Line(sem("v_rt"), [f"s{i}" for i in range(200)])
        pe_rt, a_rt, s_et = sem("pe_rt"), sem("a_rt"), sem("s_et")
        v_row = sem("v_row")
        d_srt = [sem(f"d_srt{g}") for g in range(GROUP)]
        d_rb = [sem(f"d_rb{u}") for u in range(RB_SLOTS)]
        d_out = [sem(f"d_out{u}") for u in range(RB_SLOTS)]
        VT = Line(sem("v_tail"), ln_names("T") + ["xf"])
        VO = Line(sem("v_out"), ["o"], credit=1)
        AT = Line(sem("a_tail"), ["xT"] + [f"g{j}" for j in range(HJ)], credit=1)
        PT = Line(sem("pe_tail"), ["tr"] + [f"h{j}" for j in range(HJ)], credit=1)
        PY = Line(sem("pe_y"), ["y"], credit=1)

        def layer_norm(eng, line, i, p, x_in):
            def v(k):
                return lnt[:, k:k + 1]
            line.done(eng.bn_stats(lnt[:, 8:14], x_in), p + "st")
            line.wait(eng, p + "st", i)
            hold(eng, "DVE")
            line.done(eng.bn_aggr(lnt[:, 0:2], lnt[:, 8:14]), p + "ag")
            line.wait(eng, p + "ag", i)
            line.done(eng.tensor_scalar(v(2), v(1), EPS_LN, None, ALU.add), p + "v")
            line.wait(eng, p + "v", i)
            line.done(eng.tensor_scalar(v(3).bitcast(I32), v(2).bitcast(I32), -0.5, 1597463007.0,
                                        ALU.mult, ALU.add), p + "y0")
            line.wait(eng, p + "y0", i)
            for n in "123":
                line.done(eng.scalar_tensor_tensor(v(4), v(3), v(3), v(2), ALU.mult, ALU.mult), p + "a" + n)
                line.wait(eng, p + "a" + n, i)
                line.done(eng.tensor_scalar(v(5), v(4), -0.5, 1.5, ALU.mult, ALU.add), p + "b" + n)
                line.wait(eng, p + "b" + n, i)
                line.done(eng.tensor_tensor(v(3), v(3), v(5), ALU.mult), p + "y" + n)
                line.wait(eng, p + "y" + n, i)

        def within(e, v, hi):
            return nc.s_assert_within(e.snap(v), 0, hi, skip_runtime_bounds_check_because="from the table of items, which "
                                      "counts at most SUPER superchunks and TILES tiles")

        def body_items(e, body, n, nu, first):
            w = e.value_load(words[0:1, n, bass.ds(body, 1)], min_val=0, max_val=(1 << (6 + nu)) - 1)
            t, out = w & 63, []
            for u in range(nu):
                k = body * nu + (u + first)
                t = within(e, t, TILES - 1)
                last = within(e, (w >> (6 + u)) & 1, 1)
                out.append((k, t, within(e, (k - t) & 255, SUPER - 1), last))
                t = t + last
            return out

        def part(e, t, back, do):
            if isinstance(t, int):
                if 0 <= t - back < TILES:
                    do(t - back)
            elif back == 0:
                do(t)
            else:
                with e.If(t > back - 1):
                    do(within(e, (t - back) & 63, TILES - 1 - back))

        def matmuls(eng, out_ap, pairs):
            for n, (a, b) in enumerate(pairs):
                ins = eng.matmul(out_ap, a, b, start=(n == 0), stop=(n == len(pairs) - 1))
            return ins

        block = ctx.enter_context(nc.Block())

        @block.sync
        def _(e):
            for n, s in enumerate([d_h, d_q, *d_xst]):
                e.dma_start(scrap[:, n:n + 1], dst_tail[0:1].unsqueeze(0)).then_inc(s, 3 * OPENED if s is d_h else OPENED)
            e.wait_ge(p_setup, 1)
            for g in range(GROUP):
                lo_t, hi_t = g * GROUP, (g + 1) * GROUP
                if g < GROUP - 1:
                    e.dma_start(res[:, lo_t:hi_t, 0:C],
                                x[lo_t * P:hi_t * P, :].rearrange("(t p) c -> p t c", p=P)).then_inc(d_x[g], 32)
                else:
                    e.dma_start(res[:, lo_t:hi_t - 1, 0:C],
                                x[lo_t * P:(hi_t - 1) * P, :].rearrange("(t p) c -> p t c", p=P)).then_inc(d_x[g], 16)
                    e.dma_start(res[0:LAST_ROWS, hi_t - 1, 0:C], x[(hi_t - 1) * P:N, :]).then_inc(d_x[g], 16)
                if g == 0:
                    e.dma_start(dsti, dstL).then_inc(d_edges, 16)
                    e.dma_start(src, srcL).then_inc(d_edges, 16)
                    e.dma_start(tv.bitcast(I32)[:, 0:SUPER], dst_tail.partition_broadcast(P)).then_inc(d_edges, 16)

            def half(a):
                return a.rearrange("(h p) o -> p h o", p=P)
            loads = [(w1l, half(w["w1lT"])), (w1r, half(w["w1rT"])), (w2l, half(w["w2lT"])), (w2r, half(w["w2rT"])),
                     (gb1[:], w["gb1"].unsqueeze(0)), (gb2[:], w["gb2"].unsqueeze(0)),
                     (wq, half(w["wqkvT"])[:, :, 0:C]), (wkv, half(w["wqkvT"])[:, :, C:3 * C]),
                     (mw1, half(w["mw1T"])), (mw2, half(w["mw2T"])),
                     (lng1, w["ln1_g"].partition_broadcast(P)), (lnb1, w["ln1_b"].partition_broadcast(P)),
                     (lng2, w["ln2_g"].partition_broadcast(P)), (lnb2, w["ln2_b"].partition_broadcast(P)),
                     (mb1, w["mb1L"]), (mb2, w["mb2"].unsqueeze(0)),
                     (fw1[:], half(w["fw1"])), (fwg[:], w["fwg"].rearrange("(j p) e -> p j e", p=P)),
                     (fb1[:], w["fb1L"]), (fbg[:], w["fbg"].unsqueeze(0))]
            for a, b in loads:
                e.dma_start(a[:] if not isinstance(a, bass.AP) else a, b).then_inc(d_w, 16)
            e.wait_ge(p_setup, 2)
            e.dma_start(srt_d.rearrange("(t p) c -> p t c", p=P),
                        zrow[:, :].unsqueeze(1).to_broadcast([P, SLOTS, ROW])).then_inc(d_init, 16)
            e.wait_ge(s_ck, 1)
            e.dma_start(ck_d.rearrange("(p j) -> p j", j=2), ckc[:, 0:2]).then_inc(d_ck, 16)
            e.wait_ge(d_ck, 16)
            e.dma_start(tv[:], ck_d.partition_broadcast(P)).then_inc(d_ck, 16)
            with e.Fori(0, TILES // GROUP) as g:
                for u in range(GROUP):
                    i = g * GROUP + u
                    VN.wait(e, "lo", i)
                    hold(e, "SP")
                    e.dma_start(xh_d[bass.ds(i * P, P), :], xhl[:, u, :]).then_inc(d_xst[u], 16)
                    e.dma_start(xn_d[bass.ds(i * P, P), :], xb[:, u, :]).then_inc(d_xst[u], 16)
            for layer in range(2):
                with e.Fori(0, SUPER // RING) as b:
                    for r in range(RING):
                        uses = -(-(SUPER - r) // RING)
                        e.wait_ge(d_g[r], b * 64 + (layer * uses + 1) * 64)
                        hold(e, "SP")
                        e.sem_inc(s_ready, 1)
                for r in range(SUPER % RING):
                    uses = -(-(SUPER - r) // RING)
                    e.wait_ge(d_g[r], (layer + 1) * uses * 64)
                    e.sem_inc(s_ready, 1)
            e.wait_ge(d_init, 16)
            for g in range(GROUP):
                e.wait_ge(d_srt[g], 16 * (TILES // GROUP))
            for first, jj in turns(e, SLOTS // RB_SLOTS):
                for u in range(RB_SLOTS):
                    if not first:
                        e.wait_ge(d_out[u], jj * 16)
                        hold(e, "SP")
                    e.dma_start(RB[:, u, :], srt_d[bass.ds(jj * RB_SLOTS * P + u * P, P), :]).then_inc(d_rb[u], 16)
            for u in range(RB_SLOTS):
                e.wait_ge(d_out[u], 16 * (SLOTS // RB_SLOTS))

        @block.gpsimd
        def _(e):
            e.memset(res[:], 0.0).then_inc(p_setup, 1)
            e.memset(zrow[:], 0.0).then_inc(p_const, 1)
            e.wait_ge(p_const, 1)
            e.memset(zrow[:, C + 1:C + 2].bitcast(I32), NO_ROW).then_inc(p_setup, 1)
            e.iota(ii[:, 0:P], pattern=[[1, P]], base=0, channel_multiplier=0).then_inc(p_const, 1)
            e.iota(ii[:, P:P + 2], pattern=[[1, 2]], base=0, channel_multiplier=2).then_inc(p_const, 1)
            e.iota(ii[:, P + 2:P + 3], pattern=[[1, 1]], base=0, channel_multiplier=1).then_inc(p_const, 1)
            e.iota(ik[:], pattern=[[1, 2 * P]], base=0, channel_multiplier=0).then_inc(p_const, 1)
            e.iota(it[:], pattern=[[P, TILES]], base=0, channel_multiplier=1).then_inc(p_const, 1)
            for layer in range(2):
                table = (xh_d, hh_d)[layer]
                if layer == 0:
                    for u in range(GROUP):
                        e.wait_ge(d_xst[u], OPENED + 32 * (TILES // GROUP))
                    PN.wait(e, "tr", TILES - 1)
                    e.wait_ge(d_edges, 48)
                    e.wait_ge(s_tab, 1)
                else:
                    e.wait_ge(d_h, 3 * OPENED + 16 * TILES)

                def gather(c, r, tile=None):
                    if tile is not None:
                        e.wait_ge(PI.sem, c + tile + (PI.credit + 1 - RING + layer * ITEMS))
                        hold(e, "Pool")
                    e.tensor_copy(ix[:, r, :], src[:, bass.ds(c * SC, SC)]).then_inc(p_ix, 1)
                    e.wait_ge(p_ix, c + (layer * SUPER + 1))
                    hold(e, "Pool")
                    for j in range(SC):
                        e.indirect_dma_start(G[:, r, j, :], None, table,
                                             bass.IndirectOffsetOnAxis(ap=ix[:, r, j:j + 1], axis=0)
                                             ).then_inc(d_g[r], 16)
                for r in range(RING):
                    gather(r, r)
                with e.Fori(1, SUPER // RING) as b:
                    w = e.value_load(free_words[0:1, bass.ds(b - 1, 1)], min_val=0, max_val=(1 << 24) - 1)
                    for r in range(RING):
                        gather(b * RING + r, r, within(e, (w >> (6 * r)) & 63, TILES - 1))
                w = e.value_load(free_words[0:1, SUPER // RING - 1:SUPER // RING], min_val=0, max_val=(1 << 24) - 1)
                for r in range(SUPER % RING):
                    gather(SUPER // RING * RING + r, r, within(e, (w >> (6 * r)) & 63, TILES - 1))
            with e.Fori(0, TILES // GROUP) as g:
                for u in range(GROUP):
                    if u == 0:
                        e.wait_ge(v_row, g * 2 + 2)
                        hold(e, "Pool")
                    e.indirect_dma_start(srt_d, bass.IndirectOffsetOnAxis(ap=pslot[:, u:u + 1], axis=0),
                                         rows[:, u, :], None, bounds_check=SLOTS * P - 1,
                                         oob_is_err=False).then_inc(d_srt[u], 16)
            with e.Fori(0, SLOTS // RB_SLOTS) as jj:
                for u in range(RB_SLOTS):
                    VO.wait(e, "o", jj * RB_SLOTS + u)
                    hold(e, "Pool")
                    e.indirect_dma_start(out, bass.IndirectOffsetOnAxis(ap=RB[:, u, C + 1:C + 2].bitcast(I32), axis=0),
                                         o_sb[:, u, :], None, bounds_check=N - 1,
                                         oob_is_err=False).then_inc(d_out[u], 16)

        @block.vector
        def _(e):
            n_setup = [0]

            def step(ins):
                v_setup.done(ins, f"s{n_setup[0]}")
                v_setup.wait(e, f"s{n_setup[0]}", 0)
                n_setup[0] += 1

            e.sem_inc(PI.sem, PI.credit)
            for l in (AN, PN, VB1, AR1, VL2, PX2, PL2, AG2, AMA, VMA, PMA, PAC, PMB, VD2, VO, AT, PT, PY):
                e.sem_inc(l.sem, l.credit)
            e.wait_ge(p_const, 6)
            step(e.tensor_copy(iota16[:], ii[:, 0:P]))
            step(e.tensor_copy(iof[:, 0:P + 3], ii[:]))
            step(e.tensor_scalar(ident[:], iof[:, 0:P], iof[:, P + 2:P + 3], None, ALU.is_equal))
            step(e.tensor_scalar(upper[:], iof[:, 0:P], iof[:, P + 2:P + 3], None, ALU.is_gt))
            step(e.memset(ones16[:], 1.0))
            step(e.memset(ones1[:], 1.0))
            step(e.memset(zero16[:], 0.0))
            step(e.memset(epsb[:], EPS_LN))
            e.sem_inc(s_const, 1)
            step(e.tensor_copy(ikf[:], ik[:]))
            step(e.tensor_copy(itf[:], it[:]))
            step(e.tensor_scalar(vmask[:], itf[:], float(N), None, ALU.is_lt))
            e.wait_ge(d_edges, 48)
            step(e.tensor_copy(dst, dsti))
            step(e.tensor_scalar(tl, tv.bitcast(I32)[:, 0:SUPER], 7, None, ALU.logical_shift_right))
            step(e.tensor_copy(tlf, tl))
            step(e.tensor_tensor(klast, tlf, ikf[:, 0:SUPER], ALU.add))
            for j in range(2):
                step(e.tensor_scalar(cmp, klast, iof[:, P + j:P + j + 1], None, ALU.is_lt))
                step(e.tensor_reduce(ckc[:, j:j + 1], cmp, AX.X, ALU.add))
            e.sem_inc(s_ck, 1)
            last_t = tlf[0:1, 0:RING * TILES].rearrange("p (g r) -> p g r", r=RING)
            step(e.tensor_copy(fw, last_t[:, :, 0]))
            for n in range(1, RING):
                step(e.scalar_tensor_tensor(fw, last_t[:, :, n], float(64 ** n), fw, ALU.mult, ALU.add))
            step(e.tensor_copy(free_words[:], fw))
            for g in range(GROUP):
                e.wait_ge(d_x[g], 32)
                with e.Fori(g * GROUP, (g + 1) * GROUP) as i:
                    e.bn_stats(st6[:, bass.ds(i, 1), :].rearrange("p a c -> p (a c)"),
                               res[:, bass.ds(i, 1), 0:C].rearrange("p a c -> p (a c)")).then_inc(v_st, 1)
            e.wait_ge(v_st, TILES)
            me, qe, mo, qo = (st6[:, :, n] for n in (1, 2, 4, 5))
            half = 0.5 / (C // 2)
            step(e.tensor_tensor(mv[:, :, 0], me, mo, ALU.add))
            step(e.tensor_tensor(mv[:, :, 1], me, mo, ALU.subtract))
            step(e.tensor_scalar(mv[:, :, 0], mv[:, :, 0], 0.5, None, ALU.mult))
            step(e.tensor_tensor(mv[:, :, 1], mv[:, :, 1], mv[:, :, 1], ALU.mult))
            step(e.tensor_tensor(sd[:], qe, qo, ALU.add))
            step(e.tensor_scalar(sd[:], sd[:], half, None, ALU.mult))
            step(e.scalar_tensor_tensor(mv[:, :, 1], mv[:, :, 1], 0.25, sd[:], ALU.mult, ALU.add))
            e.sem_inc(s_var, 1)
            e.wait_ge(a_setup, 1)
            step(e.reciprocal(rstd[:], sd[:]))
            with e.Fori(0, TILES // GROUP) as g:
                for u in range(GROUP):
                    i = g * GROUP + u
                    e.wait_ge(d_xst[u], g * 32 + OPENED)
                    e.wait_ge(PN.sem, g * GROUP + PN.credit)
                    VN.done(e.tensor_scalar(xb[:, u, :], res[:, bass.ds(i, 1), 0:C].rearrange("p a c -> p (a c)"),
                                            mv[:, bass.ds(i, 1), 0:1].rearrange("p a c -> p (a c)"),
                                            rstd[:, bass.ds(i, 1)], ALU.subtract, ALU.mult), "xn")
                    AN.wait(e, "hi", i)
                    VN.done(e.tensor_tensor(xhl[:, u, C:2 * C], xb[:, u, :], xhl[:, u, 0:C], ALU.subtract), "lo")
            e.wait_ge(d_ck, 32)
            step(e.tensor_tensor(tf, ikf[:], tv[:], ALU.subtract))
            step(e.memset(lastf, 1.0))
            step(e.tensor_tensor(lastf[:, 0:ITEMS - 1], tf[0:1, 1:ITEMS], tf[0:1, 0:ITEMS - 1], ALU.subtract))
            for n, (first, nu) in enumerate(((0, ITEMS_A), (ITEMS_A * TILES, ITEMS_B), (0, ITEMS_2))):
                ts, ls = (a[:, first:first + nu * TILES].rearrange("p (b u) -> p b u", u=nu) for a in (tf[0:1], lastf))
                step(e.tensor_copy(fw, ts[:, :, 0]))
                for u in range(nu):
                    step(e.scalar_tensor_tensor(fw, ls[:, :, u], float(64 << u), fw, ALU.mult, ALU.add))
                step(e.tensor_copy(words[:, n, :], fw))
            step(e.tensor_scalar(tv[:], tf, float(P), None, ALU.mult))
            e.sem_inc(s_tab, 1)

            def one_hots(items, layer):
                nu = len(items)
                for u, (k, t, c, last) in enumerate(items):
                    g = k + layer * ITEMS
                    e.wait_ge(PI.sem, g + (PI.credit + 1 - nu))
                    VI.done(e.tensor_scalar(rel[:, u, :], dst[:, bass.ds(c * SC, SC)], tv[:, bass.ds(k, 1)], None,
                                            ALU.subtract), "rel")
                    VI.wait(e, "rel", g)
                    for j in range(SC):
                        VI.done(e.tensor_scalar(S[:, u, j, :], iota16[:], rel[:, u, j:j + 1], None, ALU.is_equal),
                                f"S{j}")

            def tile_mean(line, t):
                rc = RC[:, bass.ds(t, 1)]
                line.done(e.tensor_scalar(lo[:], AGG[:, C:2 * C], rc, None, ALU.mult), "lo")
                line.wait(e, "lo", t)
                line.done(e.scalar_tensor_tensor(mean[:], AGG[:, 0:C], rc, lo[:], ALU.mult, ALU.add), "mean")

            def res_tile(t):
                return res[:, bass.ds(t, 1), 0:C].rearrange("p a c -> p (a c)")

            def finish1(t, g, mix_done):
                def mean_of(t):
                    PI.wait(e, "sum", g)
                    VM1.done(e.tensor_scalar(cntv[:], CNT[:, 0:1], 1.0, None, ALU.max), "cnt")
                    VM1.wait(e, "cnt", t)
                    VM1.done(e.reciprocal(RC[:, bass.ds(t, 1)], cntv[:]), "rc")
                    VM1.wait(e, "rc", t)
                    tile_mean(VM1, t)

                def hidden(t):
                    AR1.wait(e, "relu", t)
                    e.wait_ge(d_h, t * 16 + 3 * OPENED)
                    VB1.done(e.tensor_copy(HL[:, 0:C], hb[:]), "hi")
                    VB1.wait(e, "hi", t)
                    VB1.done(e.tensor_tensor(HL[:, C:2 * C], hb[:], HL[:, 0:C], ALU.subtract), "hlo")
                    PB1.wait(e, "tr2", t)
                    VB1.done(e.tensor_copy(hT[:], FT[:, C:2 * C].rearrange("p (h t) -> p h t", h=CH)), "hT")
                    PB1.wait(e, "r2", t)
                    mix_done()
                    VB1.done(e.tensor_tensor(res_tile(t), res_tile(t), FR[:, 0:C], ALU.add), "res")

                def meanT(t):
                    PT1.wait(e, "tr1", t)
                    VT1.done(e.tensor_copy(mT[:], FT[:, 0:C].rearrange("p (h t) -> p h t", h=CH)), "mT")
                part(e, t, 0, mean_of)
                part(e, t, 2, hidden)
                part(e, t, 0, meanT)

            for first, i in turns(e, TILES):
                items = body_items(e, i, 0, ITEMS_A, 0)
                one_hots(items, 0)
                if not first:
                    PAC.wait(e, "acc", i, 1)
                VMA.done(e.tensor_copy(v1[:, :, P:P + 1], vmask[:, bass.ds(i, 1)].unsqueeze(1).to_broadcast([P, CH, 1])), "one")
                AMA.wait(e, "rk", i)
                VMA.done(e.scalar_tensor_tensor(kb, ek, 1.0, rk, ALU.min, ALU.add), "k")
                AMA.wait(e, "rq", i)
                e.wait_ge(d_q, i * 16 + OPENED)
                VMA.done(e.scalar_tensor_tensor(qb, eq, 1.0, rq, ALU.min, ALU.add), "q")
                for k, t, c, last in items:
                    with e.If(last == 1):
                        finish1(t, k, lambda: None)
            n_kv = [0]

            def kv(ins):
                v_kv.done(ins, f"s{n_kv[0]}")
                v_kv.wait(e, f"s{n_kv[0]}", 0)
                n_kv[0] += 1
            kv(e.memset(KVs, 0.0))
            PAC.wait(e, "acc", TILES - 1)
            for h in range(CH):
                acc = B6[:, h * (P + 1):(h + 1) * (P + 1)]
                for q in range(P // HD):
                    a = slice(q * HD, (q + 1) * HD)
                    kv(e.tensor_copy(KVs[a, h, a], acc[a, a]))
                    kv(e.tensor_copy(KVs[a, h, P + q:P + q + 1], acc[a, P:P + 1]))
            def attention(i):
                PMt.wait(e, "t", i)
                blocks = B4[:, 0:CH * (P + 4)].rearrange("p (h m) -> p h m", h=CH)
                VD1.done(e.tensor_scalar(zd.rearrange("p (h q) -> p h q", h=CH), blocks[:, :, P:P + 4], EPS_ATTN, None,
                                         ALU.add), "den")
                VD1.wait(e, "den", i)
                VD1.done(e.reciprocal(zd, zd), "rc")
                VD1.wait(e, "rc", i)
                VD1.done(e.tensor_tensor(m_t.rearrange("p (h q m) -> p h q m", h=CH, m=HD),
                                         blocks[:, :, 0:P].rearrange("p h (q m) -> p h q m", m=HD),
                                         zd.rearrange("p (h q) -> p h q", h=CH).unsqueeze(3)
                                         .to_broadcast([P, CH, P // HD, HD]), ALU.mult), "tz")
                VD1.wait(e, "tz", i)
                e.wait_ge(d_lx, i * 16 + 16)
                VD1.done(e.tensor_tensor(m_s[:], m_t[:], xnS, ALU.add), "s")
                VD1.wait(e, "s", i)
                layer_norm(e, VD1, i, "A", m_s[:])
                VD1.done(e.tensor_scalar(m_t[:], m_s[:], lnt[:, 0:1], lnt[:, 3:4], ALU.subtract, ALU.mult), "n1")
                VD1.wait(e, "n1", i)
                VD1.done(e.tensor_tensor(m_t[:], m_t[:], lng1, ALU.mult), "g1")
                VD1.wait(e, "g1", i)
                PMB.wait(e, "tr", i, 1)
                VD1.done(e.tensor_tensor(m_x1, m_t[:], lnb1, ALU.add), "x1")

            def mix_out(i, done1):
                PMB.wait(e, "w2", i)
                VD2.done(e.tensor_copy(m_s[:], B6[:, 0:C]), "s2")
                VD2.wait(e, "s2", i)
                layer_norm(e, VD2, i, "B", m_s[:])
                VD2.done(e.tensor_scalar(m_t[:], m_s[:], lnt[:, 0:1], lnt[:, 3:4], ALU.subtract, ALU.mult), "n2")
                VD2.wait(e, "n2", i)
                VD2.done(e.tensor_tensor(m_t[:], m_t[:], lng2, ALU.mult), "g2")
                VD2.wait(e, "g2", i)
                VD2.done(e.tensor_tensor(m_o, m_t[:], lnb2, ALU.add), "b2")
                VD2.wait(e, "b2", i)
                e.wait_ge(VB1.sem, done1 * VB1.n + (VB1.credit - 2 * VB1.n))
                VD2.done(e.tensor_tensor(res_tile(i), res_tile(i), m_o, ALU.add), "res")

            def turn_b(i, stage):
                if stage <= 2:
                    items = body_items(e, i, 1, ITEMS_B, TILES * ITEMS_A)
                    one_hots(items, 0)
                    for k, t, c, last in items:
                        with e.If(last == 1):
                            finish1(t, k, lambda: VD2.wait(e, "res", i, 3))
                    done1 = items[-1][1] + items[-1][3]
                else:
                    done1 = TILES
                if stage >= 2:
                    mix_out(i - 2, done1)
                if stage <= 2:
                    attention(i)
            turn_b(0, 0)
            turn_b(1, 1)
            with e.Fori(2, TILES) as i:
                turn_b(i, 2)
            turn_b(TILES, 3)
            turn_b(TILES + 1, 4)
            for t in (TILES, TILES + 1):
                finish1(t, None, lambda: VD2.wait(e, "res", TILES - 1))

            def finish2(t, g):
                def mean_of(t):
                    PI.wait(e, "sum", g)
                    tile_mean(VM2, t)

                def x2(t):
                    PO2.wait(e, "o", t)
                    VX2.done(e.tensor_tensor(res_tile(t), res_tile(t), FO[:, 0:C], ALU.add), "x2")
                    VX2.wait(e, "x2", t)
                    hold(e, "DVE")
                    layer_norm(e, VX2, t, "G", res_tile(t))
                    PX2.wait(e, "tr", t, 1)
                    VX2.done(e.tensor_scalar(m_t[:], res_tile(t), lnt[:, 0:1], lnt[:, 3:4], ALU.subtract, ALU.mult), "xf")

                def logits(t):
                    PL2.wait(e, "lg", t)
                    VL2.done(e.tensor_copy(LG[:, bass.ds(t, 1), :].rearrange("p a e -> p (a e)"), B6[:, 0:NE]), "lg")

                def meanT(t):
                    PT2.wait(e, "tr1", t)
                    VT2.done(e.tensor_copy(mT[:], FT[:, 0:C].rearrange("p (h t) -> p h t", h=CH)), "mT")
                part(e, t, 0, mean_of)
                part(e, t, 1, x2)
                part(e, t, 3, logits)
                part(e, t, 0, meanT)
            with e.Fori(0, TILES) as i:
                items = body_items(e, i, 2, ITEMS_2, 0)
                one_hots(items, 1)
                for k, t, c, last in items:
                    with e.If(last == 1):
                        finish2(t, k + ITEMS)
            for t in range(TILES, TILES + 3):
                finish2(t, None)
            VL2.wait(e, "lg", TILES - 1)
            VX2.wait(e, "x2", TILES - 1)
            n_rt = [0]

            def rt(ins):
                v_rt.done(ins, f"s{n_rt[0]}")
                v_rt.wait(e, f"s{n_rt[0]}", 0)
                n_rt[0] += 1

            def over_e(a):
                return a.unsqueeze(2).to_broadcast([P, TILES, NE])

            def over_t(a):
                return a.unsqueeze(1).to_broadcast([P, TILES, NE])
            rt(e.tensor_reduce(mx[:], LG[:], AX.X, ALU.max))
            rt(e.tensor_tensor(E1, LG[:], over_e(mx[:]), ALU.is_equal))
            rt(e.tensor_tensor(LG[:], LG[:], over_e(mx[:]), ALU.subtract))
            e.sem_inc(s_lmax, 1)
            rt(e.tensor_scalar(w8[:], iof[:, 0:NE], -1.0, float(NE), ALU.mult, ALU.add))
            rt(e.tensor_tensor(E2, E1, over_t(w8[:]), ALU.mult))
            rt(e.tensor_reduce(mx[:], E2, AX.X, ALU.max))
            rt(e.tensor_tensor(E1, E2, over_e(mx[:]), ALU.is_equal))
            rt(e.tensor_tensor(E1, E1, over_e(vmask[:]), ALU.mult))
            rt(e.tensor_copy(E16[:], E1))
            e.sem_inc(s_onehot, 1)
            e.wait_ge(a_rt, 1)
            rt(e.tensor_reduce(mx[:], LG[:], AX.X, ALU.add))
            rt(e.reciprocal(res[:, :, C:C + 1], mx[:].unsqueeze(2)))
            rt(e.tensor_copy(res[:, :, C + 1:C + 2].bitcast(I32), it[:].unsqueeze(2)))
            e.wait_ge(pe_rt, 1)
            rt(e.tensor_copy(A1, B5[:, 0:TILES * NE].rearrange("p (t e) -> p t e", e=NE)))
            a, b = A1, A2
            s = 1
            while s < TILES:
                rt(e.tensor_copy(b[:, 0:s, :], a[:, 0:s, :]))
                rt(e.tensor_tensor(b[:, s:, :], a[:, s:, :], a[:, :TILES - s, :], ALU.add))
                a, b = b, a
                s *= 2
            rt(e.tensor_scalar(cti[:], a[:, TILES - 1, :], float(P - 1), None, ALU.add))
            rt(e.tensor_scalar(cti[:], cti[:], 7, None, ALU.logical_shift_right))
            rt(e.memset(start[:], 0.0))
            rt(e.tensor_copy(ctf[:], cti[:]))
            for k in range(NE):
                rt(e.tensor_tensor(start[:, k + 1:k + 2], start[:, k:k + 1], ctf[:, k:k + 1], ALU.add))
            rt(e.tensor_scalar(stp[:], start[:, 0:NE], float(P), None, ALU.mult))
            rt(e.tensor_copy(b[:, 0:1, :], B4[:, 0:NE].unsqueeze(1)))
            rt(e.tensor_tensor(b[:, 1:, :], B4[:, NE:TILES * NE].rearrange("p (t e) -> p t e", e=NE),
                               a[:, 0:TILES - 1, :], ALU.add))
            rt(e.tensor_tensor(b[:], b[:], over_t(stp[:]), ALU.add))
            rt(e.tensor_tensor(b[:], b[:], E1, ALU.mult))
            rt(e.tensor_reduce(mx[:], b[:], AX.X, ALU.add))
            rt(e.tensor_scalar(nv[:], vmask[:], -float(NO_ROW), float(NO_ROW), ALU.mult, ALU.add))
            rt(e.tensor_tensor(mx[:], mx[:], nv[:], ALU.add))
            rt(e.tensor_copy(posi[:], mx[:]))
            rt(e.tensor_tensor(ete, ikf[0:1, 0:SLOTS].unsqueeze(2).to_broadcast([1, SLOTS, NE - 1]),
                               start[0:1, 1:NE].unsqueeze(1).to_broadcast([1, SLOTS, NE - 1]), ALU.is_ge))
            rt(e.tensor_reduce(etf[:], ete, AX.X, ALU.add))
            rt(e.tensor_copy(et[:], etf[:]))
            e.sem_inc(s_et, 1)
            for first, g in turns(e, TILES // GROUP):
                for u in range(GROUP):
                    if not first:
                        e.wait_ge(d_srt[u], g * 16)
                e.tensor_copy(rows, res[:, bass.ds(g * GROUP, GROUP), :]).then_inc(v_row, 1)
                e.tensor_copy(pslot[:], posi[:, bass.ds(g * GROUP, GROUP)]).then_inc(v_row, 1)
            def normed(i, u, turn):
                e.wait_ge(d_rb[u], turn * 16 + 16)
                layer_norm(e, VT, i, "T", RB[:, u, 0:C])
                PT.wait(e, "tr", i, 1)
                VT.done(e.tensor_scalar(m_t[:], RB[:, u, 0:C], lnt[:, 0:1], lnt[:, 3:4], ALU.subtract, ALU.mult), "xf")

            def result(i, u, turn):
                PY.wait(e, "y", i)
                if turn is not None:
                    e.wait_ge(d_out[u], turn * 16)
                VO.done(e.scalar_tensor_tensor(o_sb[:, u, :], B6[:, 0:C], RB[:, u, C:C + 1], RB[:, u, 0:C],
                                               ALU.mult, ALU.add), "o")
            for first, jj in turns(e, SLOTS // RB_SLOTS):
                for u in range(RB_SLOTS):
                    i = jj * RB_SLOTS + u
                    normed(i, u, jj)
                    if u > 0:
                        result(i - 1, u - 1, None if first else jj)
                    elif not first:
                        with e.If(jj > 1):
                            e.wait_ge(d_out[RB_SLOTS - 1], (jj - 1) * 16)
                            hold(e, "DVE")
                        result(i - 1, RB_SLOTS - 1, None)
            result(SLOTS - 1, RB_SLOTS - 1, SLOTS // RB_SLOTS - 1)

        @block.scalar
        def _(e):
            e.wait_ge(s_const, 1)
            e.wait_ge(s_var, 1)
            e.activation(sd[:], mv[:, :, 1], ACT.Sqrt, bias=epsb[:, 0:1]).then_inc(a_setup, 1)
            with e.Fori(0, TILES // GROUP) as g:
                for u in range(GROUP):
                    i = g * GROUP + u
                    VN.wait(e, "xn", i)
                    AN.done(e.activation(xhl[:, u, 0:C], xb[:, u, :], ACT.Copy), "hi")
                    PN.wait(e, "tr", i)
                    AN.done(e.activation(xnT[:, :, bass.ds(i * P, P)],
                                         pb[4 + u % 2][:, 0:C].rearrange("p (h t) -> p h t", h=CH), ACT.Copy), "xnT")
            e.wait_ge(s_tab, 1)
            e.wait_ge(d_w, 16 * 20)

            def xT_copy(line, dst_ap, i):
                line.done(e.activation(dst_ap, xnT[:, :, bass.ds(i * P, P)], ACT.Copy), "xT")

            def finish1(t):
                def relu(t):
                    PH1.wait(e, "h", t)
                    VB1.wait(e, "hlo", t, 1)
                    AR1.done(e.activation(hb[:], FO[:, 0:C], ACT.Relu), "relu")

                def store(t):
                    VB1.wait(e, "hlo", t)
                    e.dma_start(hh_d[bass.ds(t * P, P), :], HL[:]).then_inc(d_h, 16)
                part(e, t, 1, relu)
                part(e, t, 0, lambda t: xT_copy(AX1, xTs[:], t))
                part(e, t, 2, store)

            def finishes(items):
                for k, t, c, last in items:
                    with e.If(last == 1):
                        finish1(t)

            AN.wait(e, "xnT", TILES - 1)
            with e.Fori(0, TILES) as i:
                PMA.wait(e, "q", i, 1)
                xT_copy(AMA, xTm, i)
                PMA.wait(e, "kv", i)
                VMA.wait(e, "k", i, 1)
                AMA.done(e.activation(ek, B4[:, 0:C], ACT.Exp), "ek")
                AMA.done(e.activation(rk, B4[:, 0:C], ACT.Relu), "rk")
                PAC.wait(e, "acc", i, 1)
                AMA.done(e.activation(v1[:, :, 0:P], B4[:, C:2 * C].rearrange("p (h t) -> p h t", h=CH), ACT.Copy), "v")
                PMA.wait(e, "q", i)
                VMA.wait(e, "q", i, 1)
                AMA.done(e.activation(eq, B5[:, 0:C], ACT.Exp), "eq")
                AMA.done(e.activation(rq, B5[:, 0:C], ACT.Relu), "rq")
                finishes(body_items(e, i, 0, ITEMS_A, 0))
                VMA.wait(e, "q", i)
                e.dma_start(qT_d[bass.ds(i * P, P), :], qb).then_inc(d_q, 16)
            e.wait_ge(d_q, OPENED + 16 * TILES)
            for u in range(GROUP):
                e.wait_ge(d_xst[u], OPENED + 32 * (TILES // GROUP))

            def load_b(i):
                e.dma_start(xnS, xn_d[bass.ds(i * P, P), :]).then_inc(d_lx, 16)
                e.dma_start(qS, qT_d[bass.ds(i * P, P), :].rearrange("p (h t) -> p h t", h=CH)).then_inc(d_lq, 16)
            load_b(0)

            def next_loads(i):
                VD1.wait(e, "s", i)
                PMt.wait(e, "t", i)
                load_b(i + 1)

            def turn_b(i, stage):
                if stage >= 1 and stage <= 3:
                    PMB.wait(e, "tr", i - 1)
                    AMB.done(e.activation(x1T[:], B5[:, 0:C].rearrange("p (h t) -> p h t", h=CH), ACT.Copy), "x1T")
                items = body_items(e, i, 1, ITEMS_B, TILES * ITEMS_A) if stage <= 2 else []
                finishes(items[0:1])
                if stage >= 1 and stage <= 3:
                    PMB.wait(e, "w1", i - 1)
                    for h in range(CH):
                        AMB.done(e.activation(hTm[:, h, :], B5[:, h * P:(h + 1) * P], ACT.Gelu, bias=mb1[:, h:h + 1]), f"gl{h}")
                finishes(items[1:])
                if stage < 2:
                    next_loads(i)
                elif stage == 2:
                    with e.If(i < TILES - 1):
                        next_loads(i)
            turn_b(0, 0)
            turn_b(1, 1)
            with e.Fori(2, TILES) as i:
                turn_b(i, 2)
            turn_b(TILES, 3)
            for t in (TILES, TILES + 1):
                finish1(t)
            PMB.wait(e, "w2", TILES - 1)
            VD2.wait(e, "res", TILES - 1)
            PB1.wait(e, "r2", TILES - 1)
            for k in range(NE):
                e.dma_start(wd[:, :, k, :], w["fwd"][k].rearrange("(j p) c -> p j c", p=P)).then_inc(d_wd, 16)
            e.dma_start(fbd, w["fbd"].unsqueeze(0)).then_inc(d_wd, 16)

            def gelus(line, pe, i):
                for j in range(HJ):
                    pe.wait(e, f"h{j // 4 * 4 + 3}", i)
                    line.done(e.activation(HT[:, j, :], pb[4 + j // 4][:, (j % 4) * P:(j % 4 + 1) * P], ACT.Gelu,
                                           bias=fb1[:, j:j + 1]), f"g{j}")

            def finish2(t):
                def hid(t):
                    PX2.wait(e, "tr", t)
                    AT2.done(e.activation(x1T[:], B7[:, 0:C].rearrange("p (h t) -> p h t", h=CH), ACT.Copy), "xT")
                    PL2.wait(e, "lg", t, 1)
                    gelus(AG2, PG2, t)
                part(e, t, 2, hid)
            with e.Fori(0, TILES) as i:
                for k, t, c, last in body_items(e, i, 2, ITEMS_2, 0):
                    with e.If(last == 1):
                        finish2(t)
            for t in range(TILES, TILES + 2):
                finish2(t)
            e.wait_ge(s_lmax, 1)
            e.activation(LG[:], LG[:], ACT.Exp).then_inc(a_rt, 1)
            with e.Fori(0, SLOTS) as i:
                PT.wait(e, "tr", i)
                AT.done(e.activation(x1T[:], B7[:, 0:C].rearrange("p (h t) -> p h t", h=CH), ACT.Copy), "xT")
                PY.wait(e, "y", i, 1)
                gelus(AT, PT, i)

        @block.tensor
        def _(e):
            e.wait_ge(s_const, 1)
            with e.Fori(0, TILES // GROUP) as g:
                for u in range(GROUP):
                    i = g * GROUP + u
                    VN.wait(e, "xn", i)
                    e.wait_ge(AN.sem, g * (2 * GROUP) + (2 * u - 2 if u else 0) + AN.credit)
                    for h in range(CH):
                        ins = e.transpose(pb[4 + u % 2][:, h * P:(h + 1) * P], xb[:, u, h * P:(h + 1) * P], ident[:])
                    PN.done(ins, "tr")
            e.wait_ge(s_tab, 1)
            e.wait_ge(d_w, 16 * 20)
            AN.wait(e, "xnT", TILES - 1)

            def clear(banks):
                for b in banks:
                    ins = e.matmul(b[:, 0:512], zero16[0:1, 0:P], zero16[0:1, 0:512], start=True, stop=False,
                                   skip_group_check=True)
                return ins
            clear([AGG, CNT, B6])

            def add_item(item, u, layer):
                k, t, c, last = item
                slot = within(e, c & (RING - 1), RING - 1)
                e.wait_ge(s_ready, c + (layer * SUPER + 1))
                VI.wait(e, f"S{SC - 1}", k + layer * ITEMS)
                for j in range(SC):
                    if layer == 0:
                        e.matmul(CNT[:, 0:1], S[:, u, j, :], ones16[:, 0:1], start=False, stop=False,
                                 skip_group_check=True)
                    ins = e.matmul(AGG[:], S[:, u, j, :], G[:, bass.ds(slot, 1), j, :].rearrange("p a c -> p (a c)"),
                                   start=False, stop=False, skip_group_check=True)
                PI.done(ins, "sum")

            def transposes(bank, off, a):
                for h in range(CH):
                    ins = e.transpose(bank[:, off + h * P:off + (h + 1) * P], a[:, h * P:(h + 1) * P], ident[:])
                return ins

            def finish1(t):
                def tr2(t):
                    AR1.wait(e, "relu", t)
                    VT1.wait(e, "mT", t + 1)
                    PB1.done(transposes(FT, C, hb), "tr2")

                def tr2_last(t):
                    AR1.wait(e, "relu", t)
                    PB1.done(transposes(FT, C, hb), "tr2")

                def out1(t):
                    AX1.wait(e, "xT", t)
                    AR1.wait(e, "relu", t, 1)
                    for h in range(CH):
                        e.matmul(FO[:, 0:C], xTs[:, h, :], w1r[:, h, :], start=(h == 0), stop=False)
                    e.matmul(FO[:, 0:C], ones1[:], gb1[:], start=False, stop=False)
                    VT1.wait(e, "mT", t)
                    for h in range(CH):
                        ins = e.matmul(FO[:, 0:C], mT[:, h, :], w1l[:, h, :], start=False, stop=(h == CH - 1))
                    PH1.done(ins, "h")

                def r2(t):
                    VB1.wait(e, "hT", t)
                    VB1.wait(e, "res", t, 1)
                    PB1.done(matmuls(e, FR[:, 0:C], [(hT[:, 0, :], w2r[:, 0, :]), (hT[:, 1, :], w2r[:, 1, :]),
                                                     (ones1[:], gb2[:])]), "r2")

                def tr1(t):
                    VM1.wait(e, "mean", t)
                    clear([AGG, CNT])
                    PT1.done(transposes(FT, 0, mean), "tr1")
                part(e, t, 2, tr2 if not isinstance(t, int) or t == TILES else tr2_last)
                part(e, t, 1, out1)
                part(e, t, 2, r2)
                part(e, t, 0, tr1)

            def items_of(items, us, layer, finish):
                for u in us:
                    add_item(items[u], u, layer)
                    with e.If(items[u][3] == 1):
                        finish(items[u][1])

            def accumulate(i):
                VMA.wait(e, "k", i)
                AMA.wait(e, "v", i)
                for h in range(CH):
                    ins = e.matmul(B6[:, h * (P + 1):(h + 1) * (P + 1)], kb[:, h * P:(h + 1) * P], v1[:, h, :],
                                   start=False, stop=False, skip_group_check=True)
                PAC.done(ins, "acc")

            for first, i in turns(e, TILES):
                if not first:
                    accumulate(i - 1)
                AMA.wait(e, "v", i, 1)
                AMA.wait(e, "xT", i)
                PMA.done(matmuls(e, B4[:], [(xTm[:, h, :], wkv[:, h, :]) for h in range(CH)]), "kv")
                AMA.wait(e, "rq", i, 1)
                for d in range(CH):
                    ins = matmuls(e, B5[:, d * P:(d + 1) * P], [(wq[:, h, d * P:(d + 1) * P], xTm[:, h, :]) for h in range(CH)])
                PMA.done(ins, "q")
                items_of(body_items(e, i, 0, ITEMS_A, 0), range(ITEMS_A), 0, finish1)
            accumulate(TILES - 1)
            e.wait_ge(v_kv.sem, 1 + 2 * CH * (P // HD))

            def turn_b(i, stage):
                mlp, items = stage in (1, 2, 3), None
                if mlp:
                    VD1.wait(e, "x1", i - 1)
                    PMB.done(transposes(B5, 0, m_x1), "tr")
                if stage <= 2:
                    e.wait_ge(d_lq, i * 16 + 16)
                    for h in range(CH):
                        ins = e.matmul(B4[:, h * (P + 4):(h + 1) * (P + 4)], qS[:, h, :], KVs[:, h, :], start=True, stop=True)
                    PMt.done(ins, "t")
                    items = body_items(e, i, 1, ITEMS_B, TILES * ITEMS_A)
                    items_of(items, [0], 0, finish1)
                if mlp:
                    AMB.wait(e, "x1T", i - 1)
                    for d in range(CH):
                        ins = matmuls(e, B5[:, d * P:(d + 1) * P], [(mw1[:, h, d * P:(d + 1) * P], x1T[:, h, :]) for h in range(CH)])
                    PMB.done(ins, "w1")
                if stage <= 2:
                    items_of(items, range(1, ITEMS_B), 0, finish1)
                if mlp:
                    AMB.wait(e, "gl1", i - 1)
                    VD2.wait(e, "s2", i, 2)
                    out2 = [(hTm[:, h, :], mw2[:, h, :], B6[:, 0:C]) for h in range(CH)] + [(ones1[:], mb2, B6[:, 0:C])]
                    out2 += [(x1T[:, h, :], ident[:], B6[:, h * P:(h + 1) * P]) for h in range(CH)]
                    for n, (a, b, o) in enumerate(out2):
                        ins = e.matmul(o, a, b, start=(n == 0), stop=(n == len(out2) - 1), skip_group_check=True)
                    PMB.done(ins, "w2")
            turn_b(0, 0)
            turn_b(1, 1)
            with e.Fori(2, TILES) as i:
                turn_b(i, 2)
            turn_b(TILES, 3)
            for t in (TILES, TILES + 1):
                finish1(t)
            VB1.wait(e, "res", TILES - 1)

            def hidden(pe, xt, act, i):
                xt.wait(e, "xT", i)
                for j in range(HJ):
                    if j % 4 == 0:
                        act.wait(e, f"g{j + 3}", i, 1)
                    pe.done(matmuls(e, pb[4 + j // 4][:, (j % 4) * P:(j % 4 + 1) * P],
                                    [(fw1[:, h, j * P:(j + 1) * P], x1T[:, h, :]) for h in range(CH)]), f"h{j}")

            def finish2(t):
                def out2(t):
                    VT2.wait(e, "mT", t)
                    PO2.done(matmuls(e, FO[:, 0:C], [(mT[:, h, :], w2l[:, h, :]) for h in range(CH)]), "o")

                def trx(t):
                    VX2.wait(e, "xf", t)
                    PX2.done(transposes(B7, 0, m_t), "tr")

                def logits(t):
                    AG2.wait(e, f"g{HJ - 1}", t)
                    VL2.wait(e, "lg", t, 1)
                    PL2.done(matmuls(e, B6[:, 0:NE], [(HT[:, j, :], fwg[:, j, :]) for j in range(HJ)] + [(ones1[:], fbg[:])]), "lg")

                def tr1(t):
                    VM2.wait(e, "mean", t)
                    clear([AGG])
                    PT2.done(transposes(FT, 0, mean), "tr1")
                part(e, t, 2, trx)
                part(e, t, 1, out2)
                part(e, t, 3, logits)
                part(e, t, 2, lambda t: hidden(PG2, AT2, AG2, t))
                part(e, t, 0, tr1)
            with e.Fori(0, TILES) as i:
                items_of(body_items(e, i, 2, ITEMS_2, 0), range(ITEMS_2), 1, finish2)
            for t in range(TILES, TILES + 3):
                finish2(t)
            e.wait_ge(s_onehot, 1)
            e16 = E16.rearrange("p t e -> p (t e)")
            e.matmul(B4[:, 0:TILES * NE], upper[:], e16, start=True, stop=True)
            e.matmul(B5[:, 0:TILES * NE], ones16[:], e16, start=True, stop=True).then_inc(pe_rt, 1)
            e.wait_ge(d_wd, 16 * (NE + 1))
            e.wait_ge(s_et, 1)
            def y(i, ex):
                VO.wait(e, "o", i, 1)
                for j in range(HJ):
                    AT.wait(e, f"g{j}", i)
                    e.matmul(B6[:, 0:C], HT[:, j, :], wd[:, j, bass.ds(ex, 1), :].rearrange("p a c -> p (a c)"),
                             start=(j == 0), stop=False)
                PY.done(e.matmul(B6[:, 0:C], ones1[:], fbd[:, bass.ds(ex, 1), :].rearrange("p a c -> p (a c)"),
                                 start=False, stop=True), "y")

            def expert(i):
                return e.value_load(et[0:1, bass.ds(i, 1)], min_val=0, max_val=NE - 1)
            for first, i in turns(e, SLOTS):
                ex = None if first else expert(i - 1)
                VT.wait(e, "xf", i)
                PT.done(transposes(B7, 0, m_t), "tr")
                if not first:
                    y(i - 1, ex)
                hidden(PT, AT, AT, i)
            y(SLOTS - 1, expert(SLOTS - 1))


def kernel(**inputs):
    import numpy as np
    import concourse.bacc as bacc
    from concourse.bass_utils import run_bass_kernel_spmd

    a = {k: np.asarray(v) for k, v in inputs.items()}
    pad = SUPER * SC * P - EDGES
    src = np.concatenate([a["src"], np.zeros(pad, np.int32)])
    dst = np.concatenate([a["dst"], np.full(pad, PAD_NODE, np.int32)])
    laid = {
        "x": a["x"],
        "srcL": src.reshape(SUPER * SC, P).T, "dstL": dst.reshape(SUPER * SC, P).T,
        "dst_tail": dst[SC * P - 1::SC * P],
        "w1lT": a["L0_gnn_W1l"].T, "w1rT": a["L0_gnn_W1r"].T, "w2lT": a["L0_gnn_W2l"].T, "w2rT": a["L0_gnn_W2r"].T,
        "gb1": a["L0_gnn_b1"], "gb2": a["L0_gnn_b2"],
        "wqkvT": a["L0_mix_Wqkv"].T, "mw1T": a["L0_mix_W1"].T, "mw2T": a["L0_mix_W2"].T,
        "ln1_g": a["L0_mix_ln1_g"], "ln1_b": a["L0_mix_ln1_b"], "ln2_g": a["L0_mix_ln2_g"], "ln2_b": a["L0_mix_ln2_b"],
        "mb1L": a["L0_mix_b1"].reshape(CH, P).T, "mb2": a["L0_mix_b2"],
        "fw1": a["L0_ffn_W1"], "fb1L": a["L0_ffn_b1"].reshape(HJ, P).T,
        "fwg": a["L0_ffn_Wg"], "fbg": a["L0_ffn_bg"], "fwd": a["L0_ffn_Wd"], "fbd": a["L0_ffn_bd"],
    }
    nc = bacc.Bacc("TRN2", target_bir_lowering=False, num_devices=1)
    arrays, ap = {}, {}
    for name, v in laid.items():
        v = np.ascontiguousarray(v)
        arrays[f"in_{name}_dram"] = v
        ap[name] = nc.dram_tensor(f"in_{name}_dram", v.shape, mybir.dt.from_np(v.dtype), kind="ExternalInput").ap()
    out = nc.dram_tensor("out_0_dram", (N, C), F32, kind="ExternalOutput").ap()
    build(nc, ap.pop("x"), ap.pop("srcL"), ap.pop("dstL"), ap.pop("dst_tail"), ap, out)
    r = run_bass_kernel_spmd(nc, [arrays], core_ids=[0])
    return r.results[0]["out_0_dram"]
```

```python
from contextlib import ExitStack

import concourse.bass as bass
import concourse.mybir as mybir

F32, F16, BF16, I32 = mybir.dt.float32, mybir.dt.float16, mybir.dt.bfloat16, mybir.dt.int32
ALU, ACT, AX = mybir.AluOpType, mybir.ActivationFunctionType, mybir.AxisListType

P = 128
N, C, EDGES = 6250, 256, 100000
CH = C // P
TILES = -(-N // P)
LAST_ROWS = N - (TILES - 1) * P
SC = 4
SUPER = EDGES // (SC * P) + 2
PAD_NODE = TILES * P - 1
ITEMS = SUPER + TILES - 1
RING = 4
HEADS, HD = 8, 32
HID, NE = 1024, 8
HJ = HID // P
SLOTS = (N + NE * (P - 1)) // P
EPS_LN, EPS_ATTN = 1e-5, 1e-6
ITEMS_A, ITEMS_B, ITEMS_2 = 2, 3, 5
NS = ITEMS_2
NO_ROW = 1 << 20
SPLIT_AT = 8
RB_SLOTS = 4
assert SLOTS % RB_SLOTS == 0
OPENED = 16
assert ITEMS == TILES * (ITEMS_A + ITEMS_B) == TILES * ITEMS_2
GROUP = 7
assert TILES % GROUP == 0
HALVES = [(0, 4), (4, GROUP)]
STORED = [(0, 2), (2, 4), (4, GROUP)]


class Line:

    def __init__(self, sem, names, credit=False):
        self.sem, self.names = sem, list(names)
        self.at = 0
        self.n = len(self.names)
        self.credit = self.n * credit
        assert len(set(self.names)) == self.n

    def done(self, ins, name):
        assert self.names[self.at % self.n] == name, (self.names[self.at % self.n], name)
        self.at += 1
        ins.then_inc(self.sem, 1)

    def skip(self, eng, name):
        assert self.names[self.at % self.n] == name
        self.at += 1
        eng.sem_inc(self.sem, 1)

    def wait(self, eng, name, i, back=0):
        eng.wait_ge(self.sem, i * self.n + (self.credit + self.names.index(name) + 1 - back * self.n))


def turns(eng, n):
    yield True, 0
    with eng.Fori(1, n) as i:
        yield False, i


def chain_names(p):
    return [p + x for x in ("v", "y0", "a1", "b1", "y1", "a2", "b2", "c2", "y2")]


def ln_names(p):
    return [p + "st", p + "ag"] + chain_names(p)


def build(nc, x, srcL, dstL, dst_tail, w, out):
    with ExitStack() as ctx:
        def sb(name, shape, dt=F32):
            return ctx.enter_context(nc.sbuf_tensor(name, shape, dt))

        def sem(name):
            return ctx.enter_context(nc.semaphore(name))

        def dram(name, shape, dt=F32):
            return nc.dram_tensor(name, shape, dt, kind="Internal").ap()

        xh_d = dram("xh_d", [TILES * P, 2 * C], F16)
        hh_d = dram("hh_d", [TILES * P, 2 * C], F16)
        xn_d = dram("xn_d", [(TILES + 1) * P, C])
        qT_d = dram("qT_d", [(TILES + 1) * P, C])
        ck_d = dram("ck_d", [2 * P])
        x2_d = dram("x2_d", [TILES * P, C])

        res = sb("res", [P, TILES, C])
        big = sb("big", [P, 16640])
        G = sb("G", [P, RING, SC, 2 * C], F16)
        S = sb("S", [P, NS, SC, P], F16)
        edges = sb("edges", [P, 2, SUPER * SC])
        dsti, dst = edges[:, 0, :].bitcast(I32), edges[:, 1, :]
        ix = sb("ix", [P, RING, SC], I32)
        words = sb("words", [1, 3, TILES], I32)
        free_words = sb("free_words", [1, TILES], I32)
        tv = sb("tv", [P, 2 * P])
        iota16 = sb("iota16", [P, P], F16)
        ident = sb("ident", [P, P])
        ones16 = sb("ones16", [P, P], F16)
        zero16 = sb("zero16", [1, 2 * C], F16)
        vmask = sb("vmask", [P, TILES])
        epsb = sb("epsb", [P, 1])
        RC = sb("RC", [P, TILES])
        cntv = sb("cntv", [P, 1])
        lo = sb("lo", [P, C])
        mean = sb("mean", [P, C])
        mT = sb("mT", [P, CH, P])
        xTs = sb("xTs", [P, CH, P])
        hb = sb("hb", [P, C])
        hT = sb("hT", [P, CH, P])
        HL = sb("HL", [P, 2 * C], F16)
        w1 = sb("w1", [P, 2, CH, C])
        w1l, w1r = w1[:, 0], w1[:, 1]
        w2l, w2r = (sb(f"w{n}", [P, CH, C]) for n in ("2l", "2r"))
        fbd = w1[0:3].rearrange("p a h c -> p (a h c)").bitcast(BF16).rearrange("p (e c) -> p e c", e=NE)
        BIAS = 3 * C + NE
        bias_f, bias_t, bias = sb("bias_f", [3, BIAS]), sb("bias_t", [3, BIAS], BF16), sb("bias", [3, BIAS], BF16)
        gb1, gb2, mb2, fbg = (bias[:, n * C:min(n * C + C, BIAS)] for n in range(4))
        b2_f = sb("b2_f", [3, C])
        minus = sb("minus", [3, 2])
        ones3 = sb("ones3", [3, P], BF16)
        fw1 = sb("fw1", [P, CH, HID])
        fwg = sb("fwg", [P, HJ, NE])
        fb1 = sb("fb1", [P, HJ])
        lnt = sb("lnt", [P, 28])

        used = [0]

        def carve(n, shape):
            a = big[:, used[0]:used[0] + n]
            used[0] += n
            names = "abc"[:len(shape)]
            kw = {names[i]: shape[i] for i in range(len(shape))}
            return a.rearrange(f"p ({' '.join(names)}) -> p {' '.join(names)}", **kw) if len(shape) > 1 else a

        xnT = carve(CH * TILES * P, [CH, TILES * P])
        wq = carve(CH * C, [CH, C])
        wkv = carve(CH * 2 * C, [CH, 2 * C])
        mw1 = carve(CH * C, [CH, C])
        mw2 = carve(CH * C, [CH, C])
        lng2 = carve(C, [C])
        lnT = carve(2 * CH, [2 * CH])
        mb1 = carve(CH, [CH])
        assert used[0] <= 16640
        wd = big[:, 0:HJ * NE * C].rearrange("p (j e c) -> p j e c", j=HJ, e=NE)
        abuf = sb("abuf", [P, 6, C])
        mbuf = sb("mbuf", [P, 2080])
        parts = {"xTm": C, "xnS": C, "qS": C, "hTm": C, "m_x1": C, "m_o": C, "KVs": CH * (P + 4), "v1": CH * (P + 1), "zd": HEADS}
        at = 0
        for name, n in parts.items():
            parts[name] = mbuf[:, at:at + n]
            at += n
        assert at <= 2080
        xTm, qS, hTm, KVs, v1 = (parts[n].rearrange("p (h t) -> p h t", h=CH) for n in ("xTm", "qS", "hTm", "KVs", "v1"))
        xnS, m_x1, m_o, zd = (parts[n] for n in ("xnS", "m_x1", "m_o", "zd"))
        fbd_f, fbd_t = mbuf[0:3, 0:NE * C], w2r[0:3].rearrange("p h c -> p (h c)").bitcast(BF16)
        ek, rk, kb, eq, rq, qb = (abuf[:, n, :] for n in range(6))
        HT = abuf[:, 0:4, :].rearrange("p a b -> p (a b)").rearrange("p (j t) -> p j t", j=HJ)
        x1T = sb("x1T", [P, CH, P])
        m_s, m_t = (sb(n, [P, C]) for n in ("m_s", "m_t"))
        Gf = G.rearrange("p a b c -> p (a b c)").bitcast(F32)
        xhl = G.rearrange("p a b c -> p (a b) c")[:, 0:GROUP, :]
        xb = Gf[:, GROUP * C:2 * GROUP * C].rearrange("p (t c) -> p t c", c=C)
        st6 = sb("st6", [P, TILES, 6])
        mv = sb("mv", [P, TILES, 2])
        LG = sb("LG", [P, TILES, NE])

        ii, ik, it = sb("ii", [P, P + 3], I32), sb("ik", [P, 2 * P], I32), sb("it", [P, TILES], I32)
        iof, ikf, itf = sb("iof", [P, P + 3]), sb("ikf", [P, 2 * P]), sb("itf", [P, TILES])
        upper = sb("upper", [P, P], F16)
        scrap = sb("scrap", [1, 32], I32)
        ab = abuf.rearrange("p a c -> p (a c)")
        tl, klast, cmp = ab[:, 0:SUPER].bitcast(I32), ab[:, 256:256 + SUPER], ab[:, 512:512 + SUPER]
        tlf, tf = ab[:, 768:768 + SUPER], ab[:, 1024:1024 + 2 * P]
        fw, lastf = ab[0:1, 512 + SUPER:512 + SUPER + TILES], ab[0:1, 1280:1280 + 2 * P]
        ckc = sb("ckc", [P, 2])
        sd, rstd = sb("sd", [P, TILES]), sb("rstd", [P, TILES])
        mx, nv, posi = sb("mx", [P, TILES]), sb("nv", [P, TILES]), sb("posi", [P, TILES], I32)
        E1, E2, A1, A2 = (edges.rearrange("p a b -> p (a b)")[:, n * TILES * NE:(n + 1) * TILES * NE]
                          .rearrange("p (t e) -> p t e", e=NE) for n in range(4))
        E16 = sb("E16", [P, TILES, NE], F16)
        w8, stp, ctf = sb("w8", [P, NE]), sb("stp", [P, NE]), sb("ctf", [P, NE])
        cti, start = sb("cti", [P, NE], I32), sb("start", [P, NE + 1])
        ete = sb("ete", [1, SLOTS, NE - 1])[:]
        etf, et = sb("etf", [1, SLOTS]), sb("et", [1, SLOTS], I32)
        prob = sb("prob", [P, TILES])
        OL = Gf[:, 0:GROUP * P].rearrange("p (t r) -> p t r", r=P)
        RH = Gf[:, GROUP * P:GROUP * (P + 3 * SLOTS)].rearrange("p (t k s) -> p t k s", k=3, s=SLOTS)
        node_g, node_s = sb("node_g", [P, SLOTS], I32), sb("node_s", [P, SLOTS], I32)
        prob_s, place = sb("prob_s", [P, SLOTS]), sb("place", [P, SLOTS])
        ixt = sb("ixt", [P, 2, RB_SLOTS], I32)
        RB = Gf[:, 0:RB_SLOTS * C].rearrange("p (t c) -> p t c", c=C)
        o_sb = Gf[:, RB_SLOTS * C:2 * RB_SLOTS * C].rearrange("p (t c) -> p t c", c=C)

        pb = [ctx.enter_context(nc.psum_tensor(f"bank{i}", [P, 512], F32)) for i in range(8)]
        AGG, CNT, FT, FO, B4, B5, B6, B7 = pb
        FH = FT[:, C:2 * C]
        FR = B7

        d_x = [sem(f"d_x{g}") for g in range(GROUP)]
        d_edges, d_w, d_ck, s_x, s_gb2, d_fbd = (sem(n) for n in ("d_edges", "d_w", "d_ck", "s_x", "s_gb2", "d_fbd"))
        d_xst = [sem(f"d_xst{n}") for n in range(len(STORED))]
        d_g = [sem(f"d_g{r}") for r in range(RING)]
        d_h, d_q, d_lx, d_lq, d_wd, d_store2 = (sem(n) for n in ("d_h", "d_q", "d_lx", "d_lq", "d_wd", "d_store2"))
        s_ready = sem("s_ready")
        d_ix = [sem(f"d_ix{r}") for r in range(RING)]
        p_setup = sem("p_setup")
        v_setup = Line(sem("v_setup"), [f"s{i}" for i in range(200)])
        s_tab, s_const, s_ck, s_lmax, s_onehot, s_var = (sem(n) for n in ("s_tab", "s_const", "s_ck", "s_lmax", "s_onehot", "s_var"))
        passed = {n: sem("passed_" + n) for n in ("SP", "Pool", "DVE", "Activation")}

        def hold(e, name):
            e.sem_inc(passed[name], 1)
        p_const, v_st = sem("p_const"), sem("v_st")
        a_setup = sem("a_setup")
        VN = Line(sem("v_norm"), ["xn"])
        VL = Line(sem("v_low"), ["lo"])
        AN = Line(sem("a_norm"), ["hi"])
        AXN = Line(sem("a_xnT"), ["xnT"], credit=1)
        PN = Line(sem("pe_norm"), ["tr"], credit=1)
        VI = Line(sem("v_item"), ["S"])
        PI = Line(sem("pe_item"), ["sum"], credit=NS)
        v_zero = sem("v_zero")
        VM1 = Line(sem("v_mean1"), ["cnt", "rc", "lo", "mean"])
        AM1 = Line(sem("a_meanT1"), ["mT"])
        VB1 = Line(sem("v_hidden1"), ["hi", "hlo"], credit=2)
        AH1 = Line(sem("a_hiddenT1"), ["hT"], credit=2)
        VR1 = Line(sem("v_res1"), ["res"], credit=4)
        AX1 = Line(sem("a_xT1"), ["xT"])
        AR1 = Line(sem("a_relu1"), ["relu"], credit=2)
        PT1 = Line(sem("pe_tr1"), ["tr1"])
        PH1 = Line(sem("pe_h1"), ["h"])
        PB1 = Line(sem("pe_hidden1"), ["tr2", "r2"])
        VM2 = Line(sem("v_mean2"), ["lo", "mean"])
        AM2 = Line(sem("a_meanT2"), ["mT"])
        VX2 = Line(sem("v_x2"), ["x2"] + ln_names("G") + ["xf"])
        VL2 = Line(sem("v_lg2"), ["lg"], credit=4)
        PT2 = Line(sem("pe_tr2"), ["tr1"])
        PO2 = Line(sem("pe_o2"), ["o"])
        PX2 = Line(sem("pe_x2"), ["tr"], credit=2)
        PG2 = Line(sem("pe_hid2"), [f"h{j}" for j in range(HJ)])
        PL2 = Line(sem("pe_lg2"), ["lg"], credit=3)
        AT2 = Line(sem("a_x2T"), ["xT"])
        AG2 = Line(sem("a_hid2"), [f"g{j}" for j in range(HJ)], credit=1)
        AXA = Line(sem("a_xTA"), ["xT"])
        AMA = Line(sem("a_mixa"), ["ek", "rk", "v", "eq", "rq"], credit=1)
        VMA = Line(sem("v_mixa"), ["one", "k", "q"], credit=1)
        PMA = Line(sem("pe_mixa"), ["kv", "q"], credit=1)
        PAC = Line(sem("pe_acc"), ["acc"], credit=1)
        v_kv = Line(sem("v_kv"), [f"s{i}" for i in range(20)])
        PMt = Line(sem("pe_att"), ["t"])
        PMB = Line(sem("pe_mlp"), ["tr", "w1", "w2"], credit=1)
        AS2 = Line(sem("a_s2"), ["s2"], credit=2)
        AMB = Line(sem("a_mlp"), ["x1T0", "x1T1", "gl0", "gl1"])
        VD = Line(sem("v_ln"), ["st2", "ag2", "den", "rc", "tz", "s", "st1", "ag1"] + chain_names("")
                  + ["n1", "n2", "res"], credit=2)
        v_rt = Line(sem("v_rt"), [f"s{i}" for i in range(200)])
        pe_rt, a_rt, s_et = sem("pe_rt"), sem("a_rt"), sem("s_et")
        VP = Line(sem("v_perm"), [x + h for h in "01" for x in ("row", "tile", "node", "prob")])
        PP = Line(sem("pe_perm"), ["sum0", "sum1"])
        s_perm, s_fbd, p_ixt = sem("s_perm"), sem("s_fbd"), sem("p_ixt")
        d_rb = [sem(f"d_rb{u}") for u in range(RB_SLOTS)]
        d_out = [sem(f"d_out{u}") for u in range(RB_SLOTS)]
        VT = Line(sem("v_tail"), ln_names("T") + ["xf"])
        VO = Line(sem("v_out"), ["o"], credit=1)
        AT = Line(sem("a_tail"), ["xT"] + [f"g{j}" for j in range(HJ)], credit=1)
        PT = Line(sem("pe_tail"), ["tr"] + [f"h{j}" for j in range(HJ)], credit=1)
        PY = Line(sem("pe_y"), ["y"], credit=1)

        def rstds(eng, line, i, p, n=1):
            var, v, y, c, d = (lnt[:, 1:2 * n:2], *(lnt[:, 2 * k:2 * k + n] for k in (2, 3, 4, 5)))
            k2 = 0.375 ** 0.5

            def step(ins, name):
                line.done(ins, p + name)
                line.wait(eng, p + name, i)
            step(eng.tensor_scalar(v, var, EPS_LN, None, ALU.add), "v")
            step(eng.tensor_scalar(y.bitcast(I32), v.bitcast(I32), -0.5, float(0x5F1FFFF9), ALU.mult, ALU.add), "y0")
            step(eng.scalar_tensor_tensor(c, y, -0.703952009, v, ALU.mult, ALU.mult), "a1")
            step(eng.tensor_tensor(d, c, y, ALU.mult), "b1")
            step(eng.scalar_tensor_tensor(y, d, 1.68191391, y, ALU.add, ALU.mult), "y1")
            step(eng.scalar_tensor_tensor(c, y, k2, v, ALU.mult, ALU.mult), "a2")
            step(eng.tensor_tensor(d, c, y, ALU.mult), "b2")
            step(eng.scalar_tensor_tensor(c, d, -1.25 / k2, d, ALU.add, ALU.mult), "c2")
            step(eng.scalar_tensor_tensor(y, c, 1.875, y, ALU.add, ALU.mult), "y2")

        def layer_norm(eng, line, i, p, x_in):
            line.done(eng.bn_stats(lnt[:, 16:22], x_in), p + "st")
            line.wait(eng, p + "st", i)
            hold(eng, "DVE")
            line.done(eng.bn_aggr(lnt[:, 0:2], lnt[:, 16:22]), p + "ag")
            line.wait(eng, p + "ag", i)
            rstds(eng, line, i, p)

        def within(e, v, hi):
            return nc.s_assert_within(e.snap(v), 0, hi, skip_runtime_bounds_check_because="from the table of items, which "
                                      "counts at most SUPER superchunks and TILES tiles")

        def body_items(e, body, n, nu, first):
            w = e.value_load(words[0:1, n, bass.ds(body, 1)], min_val=0, max_val=(1 << (6 + nu)) - 1)
            t, out = w & 63, []
            for u in range(nu):
                k = body * nu + (u + first)
                t = within(e, t, TILES - 1)
                last = within(e, (w >> (6 + u)) & 1, 1)
                out.append((k, t, within(e, (k - t) & 255, SUPER - 1), last))
                t = t + last
            return out

        def part(e, t, back, do):
            if isinstance(t, int):
                if 0 <= t - back < TILES:
                    do(t - back)
            elif back == 0:
                do(t)
            else:
                with e.If(t > back - 1):
                    do(within(e, (t - back) & 63, TILES - 1 - back))

        def matmuls(eng, out_ap, pairs):
            for n, (a, b) in enumerate(pairs):
                ins = eng.matmul(out_ap, a, b, start=(n == 0), stop=(n == len(pairs) - 1))
            return ins

        block = ctx.enter_context(nc.Block())

        @block.sync
        def _(e):
            for n, s in enumerate([d_h, d_q, *d_xst]):
                e.dma_start(scrap[:, n:n + 1], dst_tail[0:1].unsqueeze(0)).then_inc(s, 3 * OPENED if s is d_h else OPENED)
            e.dma_start(tv.bitcast(I32)[:, 0:SUPER], dst_tail.partition_broadcast(P)).then_inc(d_edges, 16)
            for g in range(GROUP):
                if g == 1:
                    e.dma_start(dsti, dstL).then_inc(d_edges, 16)
                if g == GROUP - 1:
                    e.wait_ge(p_setup, 1)
                lo_t, hi_t = g * GROUP, (g + 1) * GROUP
                if g < GROUP - 1:
                    e.dma_start(res[:, lo_t:hi_t, 0:C],
                                x[lo_t * P:hi_t * P, :].rearrange("(t p) c -> p t c", p=P)).then_inc(d_x[g], 32)
                else:
                    e.dma_start(res[:, lo_t:hi_t - 1, 0:C],
                                x[lo_t * P:(hi_t - 1) * P, :].rearrange("(t p) c -> p t c", p=P)).then_inc(d_x[g], 16)
                    e.dma_start(res[0:LAST_ROWS, hi_t - 1, 0:C], x[(hi_t - 1) * P:N, :]).then_inc(d_x[g], 16)
            for g in range(GROUP):
                e.wait_ge(d_x[g], 32)
                e.sem_inc(s_x, 1)
            e.wait_ge(s_ck, 1)
            e.dma_start(ck_d.rearrange("(p j) -> p j", j=2), ckc[:, 0:2]).then_inc(d_ck, 16)
            e.wait_ge(d_ck, 16)
            e.dma_start(tv[:], ck_d.partition_broadcast(P)).then_inc(d_ck, 16)

            def half(a):
                return a.rearrange("(h p) o -> p h o", p=P)
            loads = [(w1l, half(w["w1lT"])), (w1r, half(w["w1rT"])), (w2l, half(w["w2lT"])), (w2r, half(w["w2rT"])),
                     *((bias_f[:, n * C:n * C + C], w[b].partition_broadcast(3)) for n, b in enumerate(("gb1", "gb2", "mb2"))),
                     (wq, half(w["wqkvT"])[:, :, 0:C]), (wkv, half(w["wqkvT"])[:, :, C:3 * C]),
                     (mw1, half(w["mw1T"])), (mw2, half(w["mw2T"])),
                     (lnT[:, 0:CH], w["ln1_gL"]), (lnT[:, CH:2 * CH], w["ln1_bL"]),
                     (lng2, w["ln2_g"].partition_broadcast(P)), (b2_f[:], w["ln2_b"].partition_broadcast(3)),
                     (mb1, w["mb1L"]),
                     (fw1[:], half(w["fw1"])), (fwg[:], w["fwg"].rearrange("(j p) e -> p j e", p=P)),
                     (fb1[:], w["fb1L"]), (bias_f[:, 3 * C:], w["fbg"].partition_broadcast(3))]
            for a, b in loads:
                e.dma_start(a[:] if not isinstance(a, bass.AP) else a, b).then_inc(d_w, 16)
            with e.Fori(0, TILES // GROUP) as g:
                for n, (a, b) in enumerate(STORED):
                    VL.wait(e, "lo", g * GROUP + (b - 1))
                    hold(e, "SP")
                    at = bass.ds(g * (GROUP * P) + a * P, (b - a) * P)
                    e.dma_start(xh_d[at, :].rearrange("(t p) c -> p t c", p=P), xhl[:, a:b, :]).then_inc(d_xst[n], 16)
                    e.dma_start(xn_d[at, :].rearrange("(t p) c -> p t c", p=P), xb[:, a:b, :]).then_inc(d_xst[n], 16)
            def indices(c, r):
                e.dma_start(ix[:, r, :], srcL[:, bass.ds(c * SC, SC)]).then_inc(d_ix[r], 16)

            def relay(layer, b, last=False):
                for r in range(RING):
                    uses = -(-(SUPER - r) // RING)
                    e.wait_ge(d_g[r], b * 64 + (layer * uses + 1) * 64)
                    hold(e, "SP")
                    e.sem_inc(s_ready, 1)
                    if not last or r < SUPER % RING:
                        indices(b * RING + (RING + r), r)

            def relay_rest(layer):
                for r in range(SUPER % RING):
                    uses = -(-(SUPER - r) // RING)
                    e.wait_ge(d_g[r], (layer + 1) * uses * 64)
                    e.sem_inc(s_ready, 1)
            for r in range(RING):
                indices(r, r)
            with e.Fori(0, SUPER // RING - 1) as b:
                relay(0, b)
            relay(0, SUPER // RING - 1, True)
            relay_rest(0)
            for r in range(RING):
                indices(r, r)
            EVERY = SUPER // RING // NE
            with e.Fori(0, NE) as k:
                with e.Fori(0, EVERY) as b:
                    relay(1, k * EVERY + b)
                PMB.wait(e, "w2", TILES - 1)
                VD.wait(e, "res", TILES + 1)
                e.dma_start(wd[:, :, bass.ds(k, 1), :].rearrange("p j a c -> p j (a c)"),
                            w["fwd"][bass.ds(k, 1)].rearrange("a (j p) c -> p (a j) c", p=P)).then_inc(d_wd, 16)
            for b in range(NE * EVERY, SUPER // RING):
                relay(1, b, b == SUPER // RING - 1)
            relay_rest(1)
            for u in range(RB_SLOTS):
                e.wait_ge(d_out[u], 16 * (SLOTS // RB_SLOTS))

        @block.gpsimd
        def _(e):
            e.memset(res[:, TILES - 1, :], 0.0).then_inc(p_setup, 1)
            e.iota(ii[:, 0:P], pattern=[[1, P]], base=0, channel_multiplier=0).then_inc(p_const, 1)
            e.iota(ii[:, P:P + 2], pattern=[[1, 2]], base=0, channel_multiplier=2).then_inc(p_const, 1)
            e.iota(ii[:, P + 2:P + 3], pattern=[[1, 1]], base=0, channel_multiplier=1).then_inc(p_const, 1)
            e.iota(ik[:], pattern=[[1, 2 * P]], base=0, channel_multiplier=0).then_inc(p_const, 1)
            e.iota(it[:], pattern=[[P, TILES]], base=0, channel_multiplier=1).then_inc(p_const, 1)
            for layer in range(2):
                table = (xh_d, hh_d)[layer]
                if layer == 0:
                    for u in range(len(STORED)):
                        e.wait_ge(d_xst[u], OPENED + 32 * (TILES // GROUP))
                    PN.wait(e, "tr", TILES - 1)
                    e.wait_ge(d_edges, 32)
                    e.wait_ge(s_tab, 1)
                else:
                    e.wait_ge(d_h, 3 * OPENED + 16 * TILES)

                def gather(c, r, turn, tile=None):
                    if tile is not None:
                        e.wait_ge(PI.sem, c + tile + (PI.credit + 1 - RING + layer * ITEMS))
                        hold(e, "Pool")
                    e.wait_ge(d_ix[r], turn * 16 + (-(-(SUPER - r) // RING) * layer + 1) * 16)
                    if not isinstance(turn, int):
                        hold(e, "Pool")
                    for j in range(SC):
                        e.indirect_dma_start(G[:, r, j, :], None, table,
                                             bass.IndirectOffsetOnAxis(ap=ix[:, r, j:j + 1], axis=0)
                                             ).then_inc(d_g[r], 16)
                for r in range(RING):
                    gather(r, r, 0)
                with e.Fori(1, SUPER // RING) as b:
                    w = e.value_load(free_words[0:1, bass.ds(b - 1, 1)], min_val=0, max_val=(1 << 24) - 1)
                    for r in range(RING):
                        gather(b * RING + r, r, b, within(e, (w >> (6 * r)) & 63, TILES - 1))
                w = e.value_load(free_words[0:1, SUPER // RING - 1:SUPER // RING], min_val=0, max_val=(1 << 24) - 1)
                for r in range(SUPER % RING):
                    gather(SUPER // RING * RING + r, r, SUPER // RING, within(e, (w >> (6 * r)) & 63, TILES - 1))
            e.wait_ge(d_store2, 16 * TILES)
            e.wait_ge(s_perm, 1)

            def index_x(kind, i, u):
                table = (node_g, node_s)[kind]
                e.tensor_copy(ixt[:, kind, u:u + 1], table[:, bass.ds(i, 1)]).then_inc(p_ixt, 1)

            def gather_x(i, u):
                e.indirect_dma_start(RB[:, u, :], None, x2_d, bass.IndirectOffsetOnAxis(ap=ixt[:, 0, u:u + 1], axis=0)
                                     ).then_inc(d_rb[u], 16)

            def scatter(i, u):
                e.indirect_dma_start(out, bass.IndirectOffsetOnAxis(ap=ixt[:, 1, u:u + 1], axis=0),
                                     o_sb[:, u, :], None, bounds_check=N - 1, oob_is_err=False).then_inc(d_out[u], 16)
            for u in range(RB_SLOTS):
                index_x(0, u, u)
                e.wait_ge(p_ixt, u + 1)
                gather_x(u, u)
            with e.Fori(1, SLOTS // RB_SLOTS) as jj:
                for u in range(RB_SLOTS):
                    i = jj * RB_SLOTS + u
                    VO.wait(e, "o", i, RB_SLOTS)
                    hold(e, "Pool")
                    index_x(0, i, u)
                    with e.If(jj > 1):
                        e.wait_ge(d_out[u], (jj - 1) * 16)
                        hold(e, "Pool")
                    index_x(1, (jj - 1) * RB_SLOTS + u, u)
                    e.wait_ge(p_ixt, jj * (2 * RB_SLOTS) + (2 * u + 2 - RB_SLOTS))
                    hold(e, "Pool")
                    scatter(i - RB_SLOTS, u)
                    gather_x(i, u)
            for u in range(RB_SLOTS):
                i = SLOTS - RB_SLOTS + u
                VO.wait(e, "o", i)
                e.wait_ge(d_out[u], (SLOTS // RB_SLOTS - 1) * 16)
                index_x(1, i, u)
                e.wait_ge(p_ixt, 2 * SLOTS - RB_SLOTS + u + 1)
                scatter(i, u)

        @block.vector
        def _(e):
            n_setup = [0]

            def step(ins):
                v_setup.done(ins, f"s{n_setup[0]}")
                v_setup.wait(e, f"s{n_setup[0]}", 0)
                n_setup[0] += 1

            e.sem_inc(PI.sem, PI.credit)
            for l in (AXN, PN, VB1, AH1, VR1, AR1, VL2, PX2, PL2, AG2, AMA, VMA, PMA, PAC, PMB, AS2, VD, VO, AT, PT, PY):
                e.sem_inc(l.sem, l.credit)
            e.wait_ge(p_const, 5)
            step(e.tensor_copy(iota16[:], ii[:, 0:P]))
            step(e.tensor_copy(iof[:, 0:P + 3], ii[:]))
            step(e.tensor_scalar(ident[:], iof[:, 0:P], iof[:, P + 2:P + 3], None, ALU.is_equal))
            step(e.tensor_scalar(upper[:], iof[:, 0:P], iof[:, P + 2:P + 3], None, ALU.is_gt))
            step(e.memset(ones16[:], 1.0))
            step(e.memset(ones3[:], 1.0))
            for n in range(2):
                step(e.tensor_scalar(minus[:, n:n + 1], iof[0:3, P + 2:P + 3], float(n + 1), -1.0, ALU.is_ge, ALU.mult))
            step(e.memset(zero16[:], 0.0))
            step(e.memset(epsb[:], EPS_LN))
            e.sem_inc(s_const, 1)
            step(e.tensor_copy(ikf[:], ik[:]))
            step(e.tensor_copy(itf[:], it[:]))
            step(e.tensor_scalar(vmask[:], itf[:], float(N), None, ALU.is_lt))
            e.wait_ge(d_edges, 32)
            step(e.tensor_copy(dst, dsti))
            step(e.tensor_scalar(tl, tv.bitcast(I32)[:, 0:SUPER], 7, None, ALU.logical_shift_right))
            step(e.tensor_copy(tlf, tl))
            step(e.tensor_tensor(klast, tlf, ikf[:, 0:SUPER], ALU.add))
            for j in range(2):
                step(e.tensor_scalar(cmp, klast, iof[:, P + j:P + j + 1], None, ALU.is_lt))
                step(e.tensor_reduce(ckc[:, j:j + 1], cmp, AX.X, ALU.add))
            e.sem_inc(s_ck, 1)
            last_t = tlf[0:1, 0:RING * TILES].rearrange("p (g r) -> p g r", r=RING)
            step(e.tensor_copy(fw, last_t[:, :, 0]))
            for n in range(1, RING):
                step(e.scalar_tensor_tensor(fw, last_t[:, :, n], float(64 ** n), fw, ALU.mult, ALU.add))
            step(e.tensor_copy(free_words[:], fw))
            with e.Fori(0, TILES // GROUP) as g:
                e.wait_ge(s_x, g + 1)
                hold(e, "DVE")
                for u in range(GROUP):
                    e.bn_stats(st6[:, bass.ds(g * GROUP + u, 1), :].rearrange("p a c -> p (a c)"),
                               res[:, bass.ds(g * GROUP + u, 1), 0:C].rearrange("p a c -> p (a c)")).then_inc(v_st, 1)
            e.wait_ge(v_st, TILES)
            me, qe, mo, qo = (st6[:, :, n] for n in (1, 2, 4, 5))
            half = 0.5 / (C // 2)
            step(e.tensor_tensor(mv[:, :, 0], me, mo, ALU.add))
            step(e.tensor_tensor(mv[:, :, 1], me, mo, ALU.subtract))
            step(e.tensor_scalar(mv[:, :, 0], mv[:, :, 0], 0.5, None, ALU.mult))
            step(e.tensor_tensor(mv[:, :, 1], mv[:, :, 1], mv[:, :, 1], ALU.mult))
            step(e.tensor_tensor(sd[:], qe, qo, ALU.add))
            step(e.tensor_scalar(sd[:], sd[:], half, None, ALU.mult))
            step(e.scalar_tensor_tensor(mv[:, :, 1], mv[:, :, 1], 0.25, sd[:], ALU.mult, ALU.add))
            e.sem_inc(s_var, 1)
            e.wait_ge(d_ck, 32)
            step(e.tensor_tensor(tf, ikf[:], tv[:], ALU.subtract))
            step(e.memset(lastf, 1.0))
            step(e.tensor_tensor(lastf[:, 0:ITEMS - 1], tf[0:1, 1:ITEMS], tf[0:1, 0:ITEMS - 1], ALU.subtract))
            for n, (first, nu) in enumerate(((0, ITEMS_A), (ITEMS_A * TILES, ITEMS_B), (0, ITEMS_2))):
                ts, ls = (a[:, first:first + nu * TILES].rearrange("p (b u) -> p b u", u=nu) for a in (tf[0:1], lastf))
                step(e.tensor_copy(fw, ts[:, :, 0]))
                for u in range(nu):
                    step(e.scalar_tensor_tensor(fw, ls[:, :, u], float(64 << u), fw, ALU.mult, ALU.add))
                step(e.tensor_copy(words[:, n, :], fw))
            step(e.tensor_scalar(tv[:], tf, float(P), None, ALU.mult))
            e.sem_inc(s_tab, 1)
            e.wait_ge(a_setup, 1)
            step(e.reciprocal(rstd[:], sd[:]))
            def low(i, u):
                AN.wait(e, "hi", i)
                VL.done(e.tensor_tensor(xhl[:, u, C:2 * C], xb[:, u, :], xhl[:, u, 0:C], ALU.subtract), "lo")
            with e.Fori(0, TILES // GROUP) as g:
                for u in range(GROUP):
                    i = g * GROUP + u
                    stored = [n for n, (a, b) in enumerate(STORED) if a <= u < b][0]
                    e.wait_ge(d_xst[stored], g * 32 + OPENED)
                    e.wait_ge(PN.sem, g * GROUP + PN.credit)
                    VN.done(e.tensor_scalar(xb[:, u, :], res[:, bass.ds(i, 1), :].rearrange("p a c -> p (a c)"),
                                            mv[:, bass.ds(i, 1), 0:1].rearrange("p a c -> p (a c)"),
                                            rstd[:, bass.ds(i, 1)], ALU.subtract, ALU.mult), "xn")
                    if u > 0:
                        low(i - 1, u - 1)
                low(g * GROUP + GROUP - 1, GROUP - 1)
            def split(line_step, parts, left, t):
                for n in range(2):
                    line_step(e.tensor_copy(t, left))
                    line_step(e.scalar_tensor_tensor(left, t, minus[:, n:n + 1], left, ALU.mult, ALU.add))
                line_step(e.tensor_copy(parts, left))
            e.wait_ge(d_w, 16 * 20)
            step(e.tensor_tensor(bias_f[:, C:2 * C], bias_f[:, C:2 * C], b2_f[:], ALU.add))
            split(step, bias[:], bias_f[:], bias_t[:])
            e.sem_inc(s_gb2, 1)

            def one_hots(items, layer):
                nu = len(items)
                for u, (k, t, c, last) in enumerate(items):
                    g = k + layer * ITEMS
                    e.wait_ge(PI.sem, g + (PI.credit + 1 - nu))
                    VI.done(e.scalar_tensor_tensor(
                        S[:, u, :, :], dst[:, bass.ds(c * SC, SC)].unsqueeze(2).to_broadcast([P, SC, P]),
                        tv[:, bass.ds(k, 1)], iota16[:].unsqueeze(1).to_broadcast([P, SC, P]),
                        ALU.subtract, ALU.is_equal), "S")

            def tile_mean(line, t):
                rc = RC[:, bass.ds(t, 1)]
                line.done(e.tensor_scalar(lo[:], AGG[:, C:2 * C], rc, None, ALU.mult), "lo")
                line.wait(e, "lo", t)
                line.done(e.scalar_tensor_tensor(mean[:], AGG[:, 0:C], rc, lo[:], ALU.mult, ALU.add), "mean")

            def res_tile(t):
                return res[:, bass.ds(t, 1), 0:C].rearrange("p a c -> p (a c)")

            def finish1(t, g, mix_done):
                def mean_of(t):
                    PI.wait(e, "sum", g)
                    VM1.done(e.tensor_scalar(cntv[:], CNT[:, 0:1], 1.0, None, ALU.max), "cnt")
                    VM1.wait(e, "cnt", t)
                    VM1.done(e.reciprocal(RC[:, bass.ds(t, 1)], cntv[:]), "rc")
                    VM1.wait(e, "rc", t)
                    tile_mean(VM1, t)

                def hidden(t):
                    AR1.wait(e, "relu", t)
                    e.wait_ge(d_h, t * 16 + 3 * OPENED)
                    VB1.done(e.tensor_copy(HL[:, 0:C], hb[:]), "hi")
                    VB1.wait(e, "hi", t)
                    VB1.done(e.tensor_tensor(HL[:, C:2 * C], hb[:], HL[:, 0:C], ALU.subtract), "hlo")

                def residual(t):
                    PB1.wait(e, "r2", t)
                    mix_done()
                    VR1.done(e.tensor_tensor(res_tile(t), res_tile(t), FR[:, 0:C], ALU.add), "res")
                part(e, t, 0, mean_of)
                part(e, t, 3, residual)
                part(e, t, 2, hidden)

            for first, i in turns(e, TILES):
                items = body_items(e, i, 0, ITEMS_A, 0)
                one_hots(items, 0)
                if not first:
                    PAC.wait(e, "acc", i, 1)
                VMA.done(e.tensor_copy(v1[:, :, P:P + 1], vmask[:, bass.ds(i, 1)].unsqueeze(1).to_broadcast([P, CH, 1])), "one")
                AMA.wait(e, "rk", i)
                VMA.done(e.scalar_tensor_tensor(kb, ek, 1.0, rk, ALU.min, ALU.add), "k")
                AMA.wait(e, "rq", i)
                e.wait_ge(d_q, i * 16 + OPENED)
                VMA.done(e.scalar_tensor_tensor(qb, eq, 1.0, rq, ALU.min, ALU.add), "q")
                for k, t, c, last in items:
                    with e.If(last == 1):
                        finish1(t, k, lambda: None)
            n_kv = [0]

            def kv(ins):
                v_kv.done(ins, f"s{n_kv[0]}")
                v_kv.wait(e, f"s{n_kv[0]}", 0)
                n_kv[0] += 1
            kv(e.memset(KVs, 0.0))
            PAC.wait(e, "acc", TILES - 1)
            for h in range(CH):
                acc = B6[:, h * (P + 1):(h + 1) * (P + 1)]
                for q in range(P // HD):
                    a = slice(q * HD, (q + 1) * HD)
                    kv(e.tensor_copy(KVs[a, h, a], acc[a, a]))
                    kv(e.tensor_copy(KVs[a, h, P + q:P + q + 1], acc[a, P:P + 1]))
            e.memset(lnt[:], 0.0).then_inc(v_zero, 1)
            e.wait_ge(v_zero, 1)

            def steps(i, first, second):
                def step(name, do=None):
                    if do:
                        VD.done(do(), name)
                    else:
                        VD.skip(e, name)

                def after(name):
                    VD.wait(e, name, i)
                mo = (lambda f: f) if second else (lambda f: None)
                at = (lambda f: f) if first else (lambda f: None)
                return step, after, mo, at

            def to_stats(i, first, second, items):
                step, after, mo, at = steps(i, first, second)
                if second:
                    AS2.wait(e, "s2", i - 2)
                step("st2", mo(lambda: e.bn_stats(lnt[:, 22:28], m_o)))
                after("st2")
                if second:
                    hold(e, "DVE")
                step("ag2", mo(lambda: e.bn_aggr(lnt[:, 2:4], lnt[:, 22:28])))
                blocks = B4[:, 0:CH * (P + 4)].rearrange("p (h m) -> p h m", h=CH)
                if first:
                    PMt.wait(e, "t", i)
                step("den", at(lambda: e.tensor_scalar(zd.rearrange("p (h q) -> p h q", h=CH), blocks[:, :, P:P + 4],
                                                       EPS_ATTN, None, ALU.add)))
                after("den")
                step("rc", at(lambda: e.reciprocal(zd, zd)))
                after("rc")
                step("tz", at(lambda: e.tensor_tensor(
                    m_t.rearrange("p (h q m) -> p h q m", h=CH, m=HD), blocks[:, :, 0:P].rearrange("p h (q m) -> p h q m", m=HD),
                    zd.rearrange("p (h q) -> p h q", h=CH).unsqueeze(3).to_broadcast([P, CH, P // HD, HD]), ALU.mult)))
                after("tz")
                if first:
                    e.wait_ge(d_lx, i * 16 + 16)
                step("s", at(lambda: e.tensor_tensor(m_s[:], m_t[:], xnS, ALU.add)))
                after("s")
                step("st1", at(lambda: e.bn_stats(lnt[:, 16:22], m_s[:])))
                for k, t, c, last in items:
                    with e.If(last == 1):
                        finish1(t, k, lambda: VD.wait(e, "res", i, 1))
                after("st1")
                if first:
                    hold(e, "DVE")
                step("ag1", at(lambda: e.bn_aggr(lnt[:, 0:2], lnt[:, 16:22])))
                e.wait_ge(VR1.sem, items[-1][1] + items[-1][3] + (VR1.credit - 3) if items else TILES + VR1.credit)
                if items:
                    hold(e, "DVE")

            def from_stats(i, first, second, meanwhile=lambda: None):
                step, after, mo, at = steps(i, first, second)
                after("ag1")
                rstds(e, VD, i, "", 2)
                if first and not isinstance(i, int) or i == 1:
                    PMB.wait(e, "tr", i, 1)
                step("n1", at(lambda: e.tensor_scalar(m_x1, m_s[:], lnt[:, 0:1], lnt[:, 6:7], ALU.subtract, ALU.mult)))
                if not (first and second):
                    after("n1")
                step("n2", mo(lambda: e.scalar_tensor_tensor(m_t[:], m_o, lnt[:, 2:3], lng2, ALU.subtract, ALU.mult)))
                got = meanwhile()
                after("n2")
                step("res", mo(lambda: e.scalar_tensor_tensor(res_tile(i - 2), m_t[:], lnt[:, 7:8], res_tile(i - 2),
                                                              ALU.mult, ALU.add)))

                return got

            def read_items(i):
                items = body_items(e, i, 1, ITEMS_B, TILES * ITEMS_A)
                one_hots(items, 0)
                return items

            def front(i, second, items):
                to_stats(i, True, second, items)
            front(0, False, read_items(0))
            for i in (0, 1):
                front(i + 1, i == 1, from_stats(i, True, False, lambda: read_items(i + 1)))
            with e.Fori(2, TILES - 1) as i:
                front(i + 1, True, from_stats(i, True, True, lambda: read_items(i + 1)))
            from_stats(TILES - 1, True, True)
            for t in range(TILES, TILES + 3):
                finish1(t, None, lambda: VD.wait(e, "res", TILES - 1))
            for i in (TILES, TILES + 1):
                to_stats(i, False, True, [])
                from_stats(i, False, True)

            def finish2(t, g):
                def mean_of(t):
                    PI.wait(e, "sum", g)
                    tile_mean(VM2, t)

                def x2(t):
                    PO2.wait(e, "o", t)
                    VX2.done(e.tensor_tensor(res_tile(t), res_tile(t), FO[:, 0:C], ALU.add), "x2")
                    VX2.wait(e, "x2", t)
                    hold(e, "DVE")
                    layer_norm(e, VX2, t, "G", res_tile(t))
                    PX2.wait(e, "tr", t, 1)
                    VX2.done(e.tensor_scalar(m_t[:], res_tile(t), lnt[:, 0:1], lnt[:, 6:7], ALU.subtract, ALU.mult), "xf")

                def logits(t):
                    PL2.wait(e, "lg", t)
                    VL2.done(e.tensor_copy(LG[:, bass.ds(t, 1), :].rearrange("p a e -> p (a e)"), B6[:, 0:NE]), "lg")
                part(e, t, 0, mean_of)
                part(e, t, 1, x2)
                part(e, t, 3, logits)
            def turn2(i):
                items = body_items(e, i, 2, ITEMS_2, 0)
                one_hots(items, 1)
                for k, t, c, last in items:
                    with e.If(last == 1):
                        finish2(t, k + ITEMS)
            with e.Fori(0, SPLIT_AT) as i:
                turn2(i)
            e.wait_ge(d_fbd, 16)
            for n in range(2):
                a = slice(n * (NE * C // 2), (n + 1) * (NE * C // 2))
                split(step, fbd.rearrange("p e c -> p (e c)")[:, a], fbd_f[:, a], fbd_t)
            e.sem_inc(s_fbd, 1)
            with e.Fori(SPLIT_AT, TILES) as i:
                turn2(i)
            for t in range(TILES, TILES + 3):
                finish2(t, None)
            VL2.wait(e, "lg", TILES - 1)
            VX2.wait(e, "x2", TILES - 1)
            n_rt = [0]

            def rt(ins):
                v_rt.done(ins, f"s{n_rt[0]}")
                v_rt.wait(e, f"s{n_rt[0]}", 0)
                n_rt[0] += 1

            def over_e(a):
                return a.unsqueeze(2).to_broadcast([P, TILES, NE])

            def over_t(a):
                return a.unsqueeze(1).to_broadcast([P, TILES, NE])
            rt(e.tensor_reduce(mx[:], LG[:], AX.X, ALU.max))
            rt(e.tensor_tensor(E1, LG[:], over_e(mx[:]), ALU.is_equal))
            rt(e.tensor_tensor(LG[:], LG[:], over_e(mx[:]), ALU.subtract))
            e.sem_inc(s_lmax, 1)
            rt(e.tensor_scalar(w8[:], iof[:, 0:NE], -1.0, float(NE), ALU.mult, ALU.add))
            rt(e.tensor_tensor(E2, E1, over_t(w8[:]), ALU.mult))
            rt(e.tensor_reduce(mx[:], E2, AX.X, ALU.max))
            rt(e.tensor_tensor(E1, E2, over_e(mx[:]), ALU.is_equal))
            rt(e.tensor_tensor(E1, E1, over_e(vmask[:]), ALU.mult))
            rt(e.tensor_copy(E16[:], E1))
            e.sem_inc(s_onehot, 1)
            e.wait_ge(a_rt, 1)
            rt(e.tensor_reduce(mx[:], LG[:], AX.X, ALU.add))
            rt(e.reciprocal(prob[:], mx[:]))
            e.wait_ge(pe_rt, 1)
            rt(e.tensor_copy(A1, B5[:, 0:TILES * NE].rearrange("p (t e) -> p t e", e=NE)))
            a, b = A1, A2
            s = 1
            while s < TILES:
                rt(e.tensor_copy(b[:, 0:s, :], a[:, 0:s, :]))
                rt(e.tensor_tensor(b[:, s:, :], a[:, s:, :], a[:, :TILES - s, :], ALU.add))
                a, b = b, a
                s *= 2
            rt(e.tensor_scalar(cti[:], a[:, TILES - 1, :], float(P - 1), None, ALU.add))
            rt(e.tensor_scalar(cti[:], cti[:], 7, None, ALU.logical_shift_right))
            rt(e.memset(start[:], 0.0))
            rt(e.tensor_copy(ctf[:], cti[:]))
            for k in range(NE):
                rt(e.tensor_tensor(start[:, k + 1:k + 2], start[:, k:k + 1], ctf[:, k:k + 1], ALU.add))
            rt(e.tensor_scalar(stp[:], start[:, 0:NE], float(P), None, ALU.mult))
            rt(e.tensor_copy(b[:, 0:1, :], B4[:, 0:NE].unsqueeze(1)))
            rt(e.tensor_tensor(b[:, 1:, :], B4[:, NE:TILES * NE].rearrange("p (t e) -> p t e", e=NE),
                               a[:, 0:TILES - 1, :], ALU.add))
            rt(e.tensor_tensor(b[:], b[:], over_t(stp[:]), ALU.add))
            rt(e.tensor_tensor(b[:], b[:], E1, ALU.mult))
            rt(e.tensor_reduce(mx[:], b[:], AX.X, ALU.add))
            rt(e.tensor_scalar(nv[:], vmask[:], -float(NO_ROW), float(NO_ROW), ALU.mult, ALU.add))
            rt(e.tensor_tensor(mx[:], mx[:], nv[:], ALU.add))
            rt(e.tensor_copy(posi[:], mx[:]))
            rt(e.tensor_tensor(ete, ikf[0:1, 0:SLOTS].unsqueeze(2).to_broadcast([1, SLOTS, NE - 1]),
                               start[0:1, 1:NE].unsqueeze(1).to_broadcast([1, SLOTS, NE - 1]), ALU.is_ge))
            rt(e.tensor_reduce(etf[:], ete, AX.X, ALU.add))
            rt(e.tensor_copy(et[:], etf[:]))
            e.sem_inc(s_et, 1)
            rt(e.tensor_scalar(posi[:], posi[:], 7, None, ALU.logical_shift_right))
            rt(e.tensor_copy(nv[:], posi[:]))
            rt(e.scalar_tensor_tensor(mx[:], nv[:], -float(P), mx[:], ALU.mult, ALU.add))
            for first, g in turns(e, TILES // GROUP):
                for h, (a, b) in enumerate(HALVES):
                    n = b - a

                    def of(t, width):
                        return t[:, bass.ds(g * GROUP + a, n)].unsqueeze(2).to_broadcast([P, n, width])

                    def numbers(width):
                        return iof[:, 0:width].unsqueeze(1).to_broadcast([P, n, width])
                    if not first:
                        PP.wait(e, f"sum{h}", g, 1)
                    VP.done(e.tensor_tensor(OL[:, a:b, :], numbers(P), of(mx, P), ALU.is_equal), f"row{h}")
                    VP.done(e.tensor_tensor(RH[:, a:b, 2, :], numbers(SLOTS), of(nv, SLOTS), ALU.is_equal), f"tile{h}")
                    VP.wait(e, f"tile{h}", g)
                    VP.done(e.tensor_tensor(RH[:, a:b, 0, :], RH[:, a:b, 2, :], of(itf, SLOTS), ALU.mult), f"node{h}")
                    VP.done(e.tensor_tensor(RH[:, a:b, 1, :], RH[:, a:b, 2, :], of(prob, SLOTS), ALU.mult), f"prob{h}")
            PP.wait(e, "sum1", TILES // GROUP - 1)
            nodes, probs, there = (FT[:, k * SLOTS:(k + 1) * SLOTS] for k in range(3))
            rt(e.tensor_copy(node_g[:], nodes))
            rt(e.tensor_scalar(place[:], there, -float(NO_ROW), float(NO_ROW), ALU.mult, ALU.add))
            rt(e.tensor_tensor(place[:], place[:], nodes, ALU.add))
            rt(e.tensor_copy(node_s[:], place[:]))
            e.sem_inc(s_perm, 1)
            rt(e.tensor_copy(prob_s[:], probs))
            def normed(i, u, turn):
                e.wait_ge(d_rb[u], turn * 16 + 16)
                layer_norm(e, VT, i, "T", RB[:, u, :])
                PT.wait(e, "tr", i, 1)
                VT.done(e.tensor_scalar(m_t[:], RB[:, u, :], lnt[:, 0:1], lnt[:, 6:7], ALU.subtract, ALU.mult), "xf")

            def result(i, u, turn):
                PY.wait(e, "y", i)
                if turn is not None:
                    e.wait_ge(d_out[u], turn * 16)
                VO.done(e.scalar_tensor_tensor(o_sb[:, u, :], B6[:, 0:C], prob_s[:, bass.ds(i, 1)], RB[:, u, :],
                                               ALU.mult, ALU.add), "o")
            for first, jj in turns(e, SLOTS // RB_SLOTS):
                for u in range(RB_SLOTS):
                    i = jj * RB_SLOTS + u
                    normed(i, u, jj)
                    if u > 0:
                        result(i - 1, u - 1, None if first else jj)
                    elif not first:
                        with e.If(jj > 1):
                            e.wait_ge(d_out[RB_SLOTS - 1], (jj - 1) * 16)
                            hold(e, "DVE")
                        result(i - 1, RB_SLOTS - 1, None)
            result(SLOTS - 1, RB_SLOTS - 1, SLOTS // RB_SLOTS - 1)

        @block.scalar
        def _(e):
            e.wait_ge(s_const, 1)
            e.wait_ge(s_var, 1)
            e.activation(sd[:], mv[:, :, 1], ACT.Sqrt, bias=epsb[:, 0:1]).then_inc(a_setup, 1)
            def transposed(i, u):
                PN.wait(e, "tr", i)
                AXN.done(e.activation(xnT[:, :, bass.ds(i * P, P)],
                                      pb[4 + u % 2][:, 0:C].rearrange("p (h t) -> p h t", h=CH), ACT.Copy), "xnT")
            with e.Fori(0, TILES // GROUP) as g:
                for u in range(GROUP):
                    i = g * GROUP + u
                    VN.wait(e, "xn", i)
                    AN.done(e.activation(xhl[:, u, 0:C], xb[:, u, :], ACT.Copy), "hi")
                    if u > 0:
                        transposed(i - 1, u - 1)
                transposed(g * GROUP + GROUP - 1, GROUP - 1)
            e.wait_ge(s_tab, 1)
            e.wait_ge(d_w, 16 * 20)

            def xT_copy(line, dst_ap, i):
                line.done(e.activation(dst_ap, xnT[:, :, bass.ds(i * P, P)], ACT.Copy), "xT")

            def finish1(t):
                def relu(t):
                    PH1.wait(e, "h", t)
                    VB1.wait(e, "hlo", t, 1)
                    AR1.done(e.activation(hb[:], FO[:, 0:C], ACT.Relu), "relu")

                def store(t):
                    VB1.wait(e, "hlo", t)
                    e.dma_start(hh_d[bass.ds(t * P, P), :], HL[:]).then_inc(d_h, 16)

                def meanT(t):
                    PT1.wait(e, "tr1", t)
                    AM1.done(e.activation(mT[:], FT[:, 0:C].rearrange("p (h t) -> p h t", h=CH), ACT.Copy), "mT")

                def hiddenT(t):
                    PB1.wait(e, "tr2", t)
                    AH1.done(e.activation(hT[:], FH.rearrange("p (h t) -> p h t", h=CH), ACT.Copy), "hT")
                part(e, t, 1, meanT)
                part(e, t, 2, hiddenT)
                part(e, t, 1, relu)
                part(e, t, 0, lambda t: xT_copy(AX1, xTs[:], t))
                part(e, t, 2, store)

            def finishes(items):
                for k, t, c, last in items:
                    with e.If(last == 1):
                        finish1(t)

            AXN.wait(e, "xnT", TILES - 1)
            xT_copy(AXA, xTm, 0)
            with e.Fori(0, TILES) as i:
                PMA.wait(e, "kv", i)
                VMA.wait(e, "k", i, 1)
                AMA.done(e.activation(ek, B4[:, 0:C], ACT.Exp), "ek")
                AMA.done(e.activation(rk, B4[:, 0:C], ACT.Relu), "rk")
                PAC.wait(e, "acc", i, 1)
                AMA.done(e.activation(v1[:, :, 0:P], B4[:, C:2 * C].rearrange("p (h t) -> p h t", h=CH), ACT.Copy), "v")
                PMA.wait(e, "q", i)
                hold(e, "Activation")
                with e.If(i < TILES - 1):
                    AXA.done(e.activation(xTm, xnT[:, :, bass.ds(within(e, i + 1, TILES - 1) * P, P)], ACT.Copy), "xT")
                VMA.wait(e, "q", i, 1)
                AMA.done(e.activation(eq, B5[:, 0:C], ACT.Exp), "eq")
                AMA.done(e.activation(rq, B5[:, 0:C], ACT.Relu), "rq")
                finishes(body_items(e, i, 0, ITEMS_A, 0))
                VMA.wait(e, "q", i)
                e.dma_start(qT_d[bass.ds(i * P, P), :], qb).then_inc(d_q, 16)
            e.wait_ge(d_q, OPENED + 16 * TILES)
            for u in range(len(STORED)):
                e.wait_ge(d_xst[u], OPENED + 32 * (TILES // GROUP))

            def load_b(i):
                e.dma_start(xnS, xn_d[bass.ds(i * P, P), :]).then_inc(d_lx, 16)
                e.dma_start(qS, qT_d[bass.ds(i * P, P), :].rearrange("p (h t) -> p h t", h=CH)).then_inc(d_lq, 16)
            load_b(0)

            def next_loads(i):
                VD.wait(e, "s", i)
                PMt.wait(e, "t", i)
                load_b(i + 1)

            def turn_b(i, stage):
                if stage >= 2:
                    PMB.wait(e, "w2", i - 2)
                    VD.wait(e, "n2", i, 1)
                    AS2.done(e.activation(m_o, B6[:, 0:C], ACT.Copy), "s2")
                if stage >= 1 and stage <= 3:
                    PMB.wait(e, "tr", i - 1)
                    for h in range(CH):
                        AMB.done(e.activation(x1T[:, h, :], B5[:, h * P:(h + 1) * P], ACT.Identity, scale=lnT[:, h:h + 1],
                                              bias=lnT[:, CH + h:CH + h + 1]), f"x1T{h}")
                items = body_items(e, i, 1, ITEMS_B, TILES * ITEMS_A) if stage <= 2 else []
                finishes(items[0:1])
                if stage >= 1 and stage <= 3:
                    PMB.wait(e, "w1", i - 1)
                    for h in range(CH):
                        AMB.done(e.activation(hTm[:, h, :], B5[:, h * P:(h + 1) * P], ACT.Gelu, bias=mb1[:, h:h + 1]), f"gl{h}")
                finishes(items[1:])
                if stage < 2:
                    next_loads(i)
                elif stage == 2:
                    with e.If(i < TILES - 1):
                        next_loads(i)
            turn_b(0, 0)
            turn_b(1, 1)
            with e.Fori(2, TILES) as i:
                turn_b(i, 2)
            for t in range(TILES, TILES + 3):
                finish1(t)
            turn_b(TILES, 3)
            turn_b(TILES + 1, 4)
            PMB.wait(e, "w2", TILES - 1)
            VD.wait(e, "res", TILES + 1)
            PB1.wait(e, "r2", TILES - 1)
            e.dma_start(fbd_f, w["fbd"].rearrange("e c -> (e c)").partition_broadcast(3)).then_inc(d_fbd, 16)

            def gelus(line, pe, i):
                for j in range(HJ):
                    pe.wait(e, f"h{j // 4 * 4 + 3}", i)
                    line.done(e.activation(HT[:, j, :], pb[4 + j // 4][:, (j % 4) * P:(j % 4 + 1) * P], ACT.Gelu,
                                           bias=fb1[:, j:j + 1]), f"g{j}")

            def finish2(t):
                def hid(t):
                    PX2.wait(e, "tr", t)
                    AT2.done(e.activation(x1T[:], B7[:, 0:C].rearrange("p (h t) -> p h t", h=CH), ACT.Copy), "xT")
                    PL2.wait(e, "lg", t, 1)
                    gelus(AG2, PG2, t)

                def store(t):
                    VX2.wait(e, "x2", t)
                    hold(e, "Activation")
                    e.dma_start(x2_d[bass.ds(t * P, P), :], res[:, bass.ds(t, 1), :].rearrange("p a c -> p (a c)")
                                ).then_inc(d_store2, 16)

                def meanT(t):
                    PT2.wait(e, "tr1", t)
                    AM2.done(e.activation(mT[:], FT[:, 0:C].rearrange("p (h t) -> p h t", h=CH), ACT.Copy), "mT")
                part(e, t, 1, meanT)
                part(e, t, 2, hid)
                part(e, t, 1, store)
            with e.Fori(0, TILES) as i:
                for k, t, c, last in body_items(e, i, 2, ITEMS_2, 0):
                    with e.If(last == 1):
                        finish2(t)
            for t in range(TILES, TILES + 2):
                finish2(t)
            e.wait_ge(s_lmax, 1)
            e.activation(LG[:], LG[:], ACT.Exp).then_inc(a_rt, 1)
            with e.Fori(0, SLOTS) as i:
                PT.wait(e, "tr", i)
                AT.done(e.activation(x1T[:], B7[:, 0:C].rearrange("p (h t) -> p h t", h=CH), ACT.Copy), "xT")
                PY.wait(e, "y", i, 1)
                gelus(AT, PT, i)

        @block.tensor
        def _(e):
            e.wait_ge(s_const, 1)
            with e.Fori(0, TILES // GROUP) as g:
                for u in range(GROUP):
                    i = g * GROUP + u
                    VN.wait(e, "xn", i)
                    e.wait_ge(AXN.sem, g * GROUP + (u - 1 if u else 0) + AXN.credit)
                    for h in range(CH):
                        ins = e.transpose(pb[4 + u % 2][:, h * P:(h + 1) * P], xb[:, u, h * P:(h + 1) * P], ident[:])
                    PN.done(ins, "tr")
            e.wait_ge(s_tab, 1)
            e.wait_ge(d_w, 16 * 20)
            AXN.wait(e, "xnT", TILES - 1)
            e.wait_ge(s_gb2, 1)

            def clear(a):
                e.matmul(a, zero16[0:1, 0:P], zero16[0:1, 0:a.shape[1]], start=True, stop=False,
                         skip_group_check=True)
            clear(AGG[:])
            clear(CNT[:, 0:1])
            clear(B6[:])

            def add_item(item, u, layer):
                k, t, c, last = item
                slot = within(e, c & (RING - 1), RING - 1)
                e.wait_ge(s_ready, c + (layer * SUPER + 1))
                VI.wait(e, "S", k + layer * ITEMS)
                for j in range(SC):
                    if layer == 0:
                        e.matmul(CNT[:, 0:1], S[:, u, j, :], ones16[:, 0:1], start=False, stop=False,
                                 skip_group_check=True)
                    ins = e.matmul(AGG[:], S[:, u, j, :], G[:, bass.ds(slot, 1), j, :].rearrange("p a c -> p (a c)"),
                                   start=False, stop=False, skip_group_check=True)
                PI.done(ins, "sum")

            def transposes(bank, off, a):
                for h in range(CH):
                    ins = e.transpose(bank[:, off + h * P:off + (h + 1) * P], a[:, h * P:(h + 1) * P], ident[:])
                return ins

            def finish1(t):
                def tr2(t):
                    AR1.wait(e, "relu", t)
                    AH1.wait(e, "hT", t, 1)
                    PB1.done(transposes(FT, C, hb), "tr2")

                def out1(t):
                    AX1.wait(e, "xT", t)
                    AR1.wait(e, "relu", t, 1)
                    for h in range(CH):
                        e.matmul(FO[:, 0:C], xTs[:, h, :], w1r[:, h, :], start=(h == 0), stop=False)
                    e.matmul(FO[:, 0:C], ones3[:], gb1, start=False, stop=False)
                    AM1.wait(e, "mT", t)
                    for h in range(CH):
                        ins = e.matmul(FO[:, 0:C], mT[:, h, :], w1l[:, h, :], start=False, stop=(h == CH - 1))
                    PH1.done(ins, "h")

                def r2(t):
                    AH1.wait(e, "hT", t)
                    VR1.wait(e, "res", t, 1)
                    PB1.done(matmuls(e, FR[:, 0:C], [(hT[:, 0, :], w2r[:, 0, :]), (hT[:, 1, :], w2r[:, 1, :]),
                                                     (ones3[:], gb2)]), "r2")

                def tr1(t):
                    VM1.wait(e, "mean", t)
                    clear(AGG[:])
                    clear(CNT[:, 0:1])
                    PT1.done(transposes(FT, 0, mean), "tr1")
                part(e, t, 1, out1)
                part(e, t, 2, tr2)
                part(e, t, 2, r2)
                part(e, t, 0, tr1)

            def items_of(items, us, layer, finish):
                for u in us:
                    add_item(items[u], u, layer)
                    with e.If(items[u][3] == 1):
                        finish(items[u][1])

            def accumulate(i):
                VMA.wait(e, "k", i)
                AMA.wait(e, "v", i)
                for h in range(CH):
                    ins = e.matmul(B6[:, h * (P + 1):(h + 1) * (P + 1)], kb[:, h * P:(h + 1) * P], v1[:, h, :],
                                   start=False, stop=False, skip_group_check=True)
                PAC.done(ins, "acc")

            for first, i in turns(e, TILES):
                if not first:
                    accumulate(i - 1)
                AMA.wait(e, "v", i, 1)
                AXA.wait(e, "xT", i)
                PMA.done(matmuls(e, B4[:], [(xTm[:, h, :], wkv[:, h, :]) for h in range(CH)]), "kv")
                AMA.wait(e, "rq", i, 1)
                for d in range(CH):
                    ins = matmuls(e, B5[:, d * P:(d + 1) * P], [(wq[:, h, d * P:(d + 1) * P], xTm[:, h, :]) for h in range(CH)])
                PMA.done(ins, "q")
                items_of(body_items(e, i, 0, ITEMS_A, 0), range(ITEMS_A), 0, finish1)
            accumulate(TILES - 1)
            e.wait_ge(v_kv.sem, 1 + 2 * CH * (P // HD))

            def turn_b(i, stage):
                mlp, items = stage in (1, 2, 3), None
                if stage <= 2:
                    e.wait_ge(d_lq, i * 16 + 16)
                    VD.wait(e, "tz", i, 1)
                    for h in range(CH):
                        ins = e.matmul(B4[:, h * (P + 4):(h + 1) * (P + 4)], qS[:, h, :], KVs[:, h, :], start=True, stop=True)
                    PMt.done(ins, "t")
                if mlp:
                    VD.wait(e, "n1", i - 1)
                    PMB.done(transposes(B5, 0, m_x1), "tr")
                if stage <= 2:
                    items = body_items(e, i, 1, ITEMS_B, TILES * ITEMS_A)
                if mlp:
                    AMB.wait(e, "x1T1", i - 1)
                    for d in range(CH):
                        ins = matmuls(e, B5[:, d * P:(d + 1) * P], [(mw1[:, h, d * P:(d + 1) * P], x1T[:, h, :]) for h in range(CH)])
                    PMB.done(ins, "w1")
                if stage <= 2:
                    items_of(items, range(ITEMS_B), 0, finish1)
                if mlp:
                    AMB.wait(e, "gl1", i - 1)
                    AS2.wait(e, "s2", i - 2) if stage > 1 else None
                    out2 = [(hTm[:, h, :], mw2[:, h, :], B6[:, 0:C]) for h in range(CH)] + [(ones3[:], mb2, B6[:, 0:C])]
                    out2 += [(x1T[:, h, :], ident[:], B6[:, h * P:(h + 1) * P]) for h in range(CH)]
                    for n, (a, b, o) in enumerate(out2):
                        ins = e.matmul(o, a, b, start=(n == 0), stop=(n == len(out2) - 1), skip_group_check=True)
                    PMB.done(ins, "w2")
            turn_b(0, 0)
            turn_b(1, 1)
            with e.Fori(2, TILES) as i:
                turn_b(i, 2)
            for t in range(TILES, TILES + 3):
                finish1(t)
            turn_b(TILES, 3)
            VR1.wait(e, "res", TILES - 1)

            def hidden(pe, xt, act, i):
                xt.wait(e, "xT", i)
                for j in range(HJ):
                    if j % 4 == 0:
                        act.wait(e, f"g{j + 3}", i, 1)
                    pe.done(matmuls(e, pb[4 + j // 4][:, (j % 4) * P:(j % 4 + 1) * P],
                                    [(fw1[:, h, j * P:(j + 1) * P], x1T[:, h, :]) for h in range(CH)]), f"h{j}")

            def finish2(t):
                def out2(t):
                    AM2.wait(e, "mT", t)
                    PO2.done(matmuls(e, FO[:, 0:C], [(mT[:, h, :], w2l[:, h, :]) for h in range(CH)]), "o")

                def trx(t):
                    VX2.wait(e, "xf", t)
                    PX2.done(transposes(B7, 0, m_t), "tr")

                def logits(t):
                    AG2.wait(e, f"g{HJ - 1}", t)
                    VL2.wait(e, "lg", t, 1)
                    PL2.done(matmuls(e, B6[:, 0:NE], [(HT[:, j, :], fwg[:, j, :]) for j in range(HJ)] + [(ones3[:], fbg)]), "lg")

                def tr1(t):
                    VM2.wait(e, "mean", t)
                    clear(AGG[:])
                    PT2.done(transposes(FT, 0, mean), "tr1")
                part(e, t, 2, trx)
                part(e, t, 1, out2)
                part(e, t, 3, logits)
                part(e, t, 2, lambda t: hidden(PG2, AT2, AG2, t))
                part(e, t, 0, tr1)
            with e.Fori(0, TILES) as i:
                items_of(body_items(e, i, 2, ITEMS_2, 0), range(ITEMS_2), 1, finish2)
            for t in range(TILES, TILES + 3):
                finish2(t)
            e.wait_ge(s_onehot, 1)
            e16 = E16.rearrange("p t e -> p (t e)")
            e.matmul(B4[:, 0:TILES * NE], upper[:], e16, start=True, stop=True)
            e.matmul(B5[:, 0:TILES * NE], ones16[:], e16, start=True, stop=True).then_inc(pe_rt, 1)
            clear(FT[:, 0:3 * SLOTS])
            with e.Fori(0, TILES // GROUP) as g:
                for h, (a, b) in enumerate(HALVES):
                    VP.wait(e, f"prob{h}", g)
                    for u in range(a, b):
                        ins = e.matmul(FT[:, 0:3 * SLOTS], OL[:, u, :], RH[:, u, :, :].rearrange("p k s -> p (k s)"),
                                       start=False, stop=False, skip_group_check=True)
                    PP.done(ins, f"sum{h}")
            e.wait_ge(d_wd, 16 * NE)
            e.wait_ge(s_fbd, 1)
            e.wait_ge(s_et, 1)
            def y(i, ex):
                VO.wait(e, "o", i, 1)
                for j in range(HJ):
                    AT.wait(e, f"g{j}", i)
                    e.matmul(B6[:, 0:C], HT[:, j, :], wd[:, j, bass.ds(ex, 1), :].rearrange("p a c -> p (a c)"),
                             start=(j == 0), stop=False)
                PY.done(e.matmul(B6[:, 0:C], ones3[:], fbd[:, bass.ds(ex, 1), :].rearrange("p a c -> p (a c)"),
                                 start=False, stop=True), "y")

            def expert(i):
                return e.value_load(et[0:1, bass.ds(i, 1)], min_val=0, max_val=NE - 1)
            for first, i in turns(e, SLOTS):
                ex = None if first else expert(i - 1)
                VT.wait(e, "xf", i)
                PT.done(transposes(B7, 0, m_t), "tr")
                if not first:
                    y(i - 1, ex)
                hidden(PT, AT, AT, i)
            y(SLOTS - 1, expert(SLOTS - 1))


def kernel(**inputs):
    import numpy as np
    import concourse.bacc as bacc
    from concourse.bass_utils import run_bass_kernel_spmd

    a = {k: np.asarray(v) for k, v in inputs.items()}
    pad = SUPER * SC * P - EDGES
    src = np.concatenate([a["src"], np.zeros(pad, np.int32)])
    dst = np.concatenate([a["dst"], np.full(pad, PAD_NODE, np.int32)])
    laid = {
        "x": a["x"],
        "srcL": src.reshape(SUPER * SC, P).T, "dstL": dst.reshape(SUPER * SC, P).T,
        "dst_tail": dst[SC * P - 1::SC * P],
        "w1lT": a["L0_gnn_W1l"].T, "w1rT": a["L0_gnn_W1r"].T, "w2lT": a["L0_gnn_W2l"].T, "w2rT": a["L0_gnn_W2r"].T,
        "gb1": a["L0_gnn_b1"], "gb2": a["L0_gnn_b2"],
        "wqkvT": a["L0_mix_Wqkv"].T, "mw1T": a["L0_mix_W1"].T, "mw2T": a["L0_mix_W2"].T,
        "ln1_gL": a["L0_mix_ln1_g"].reshape(CH, P).T, "ln1_bL": a["L0_mix_ln1_b"].reshape(CH, P).T, "ln2_g": a["L0_mix_ln2_g"], "ln2_b": a["L0_mix_ln2_b"],
        "mb1L": a["L0_mix_b1"].reshape(CH, P).T, "mb2": a["L0_mix_b2"],
        "fw1": a["L0_ffn_W1"], "fb1L": a["L0_ffn_b1"].reshape(HJ, P).T,
        "fwg": a["L0_ffn_Wg"], "fbg": a["L0_ffn_bg"], "fwd": a["L0_ffn_Wd"], "fbd": a["L0_ffn_bd"],
    }
    nc = bacc.Bacc("TRN2", target_bir_lowering=False, num_devices=1)
    arrays, ap = {}, {}
    for name, v in laid.items():
        v = np.ascontiguousarray(v)
        arrays[f"in_{name}_dram"] = v
        ap[name] = nc.dram_tensor(f"in_{name}_dram", v.shape, mybir.dt.from_np(v.dtype), kind="ExternalInput").ap()
    out = nc.dram_tensor("out_0_dram", (N, C), F32, kind="ExternalOutput").ap()
    build(nc, ap.pop("x"), ap.pop("srcL"), ap.pop("dstL"), ap.pop("dst_tail"), ap, out)
    r = run_bass_kernel_spmd(nc, [arrays], core_ids=[0])
    return r.results[0]["out_0_dram"]
```
